# Optimizing a Trainium2 kernel written in Bass

```python
import numpy as np
import jax
import jax.numpy as jnp

def _softmax(x, axis=-1):
    return jax.nn.softmax(x, axis=axis)

def _gelu(x):
    return jax.nn.gelu(x, approximate=True)

def _silu(x):
    return jax.nn.silu(x)

def _sigmoid(x):
    return jax.nn.sigmoid(x)

def _layernorm(x, axis=-1, eps=1e-05):
    m = jnp.mean(x, axis=axis, keepdims=True)
    v = jnp.var(x, axis=axis, keepdims=True)
    return (x - m) / jnp.sqrt(v + eps)

def _scatter_add(tgt, idx, src, axis=0):
    return tgt.at[idx].add(src)

def _segment_sum(src, seg, n):
    return jax.ops.segment_sum(src, seg, n)
kernel_name = 'mk_adj_resnorm_d2_adj_r2_63aba4'

def setup_inputs(seed: int=0):
    np.random.seed(seed)
    _w = jnp.asarray

    def _rec_inputs():
        import jax
        import jax.numpy as jnp
        _gk = jax.random.key(seed)
        x = -0.0004776 + 1.001 * jax.random.normal(jax.random.fold_in(_gk, 1), (1354, 512), jnp.float32)
        _a = jax.random.bernoulli(jax.random.fold_in(_gk, 2), 0.0014771, (1354, 1354))
        _a = jnp.logical_or(_a, jnp.swapaxes(_a, -1, -2))
        _a = jnp.logical_or(_a, jnp.eye(1354, dtype=bool))
        _af = _a.astype(jnp.float32)
        adj = _af
        return (x, adj)
    x, adj = _rec_inputs()

    def _L0_gnn_setup():
        import jax, jax.numpy as jnp
        import numpy as np
        N, H, E, HEADS = (1500, 512, 10000, 8)
        DK = H // HEADS
        key = jax.random.key(seed)
        k1, k2, k3, k4 = jax.random.split(key, 4)
        inst_feature = jax.random.normal(k1, (N, H), dtype=jnp.float32)
        rel_pair_index = jax.random.randint(k2, (E, 2), 0, N, dtype=jnp.int64)
        agg = jnp.zeros((N, N), dtype=jnp.float32)
        agg = agg.at[rel_pair_index[:, 0], rel_pair_index[:, 1]].set(1.0)
        agg = agg.at[jnp.arange(N), jnp.arange(N)].set(1.0)
        std = float(np.sqrt(2.0 / (H + DK)))
        Wq = jax.random.normal(k3, (H, H), dtype=jnp.float32) * std
        Wk = jax.random.normal(k4, (H, H), dtype=jnp.float32) * std
        bq = jnp.zeros((H,), dtype=jnp.float32)
        bk = jnp.zeros((H,), dtype=jnp.float32)
        return {'inst_feature': inst_feature, 'aggregator_matrix': agg, 'rel_pair_index': rel_pair_index, 'Wq': Wq, 'bq': bq, 'Wk': Wk, 'bk': bk}
    _L0_gnn_all = _L0_gnn_setup()
    _L0_gnn_in = {k: v for k, v in _L0_gnn_all.items() if k in ('rel_pair_index', 'Wq', 'bq', 'Wk', 'bk')}
    del _L0_gnn_all

    def _L1_gnn_setup():
        import jax, jax.numpy as jnp
        import numpy as np
        ALPHA = 0.2
        NEG = -9000000000000000.0
        N, NFEAT, NHID, NHEADS = (2048, 512, 64, 8)
        EMB = NHID * NHEADS
        key = jax.random.key(seed)
        ks = jax.random.split(key, 16)
        x = jax.random.normal(ks[0], (N, NFEAT), dtype=jnp.float32)
        adj = (jax.random.uniform(ks[1], (N, N)) < 0.01).astype(jnp.float32)
        adj = jnp.maximum(adj, jnp.eye(N, dtype=jnp.float32))
        s = 0.05
        W = jax.random.normal(ks[2], (NHEADS, NFEAT, NHID), dtype=jnp.float32) * s
        a1 = jax.random.normal(ks[3], (NHEADS, NHID), dtype=jnp.float32) * s
        a2 = jax.random.normal(ks[4], (NHEADS, NHID), dtype=jnp.float32) * s
        W1 = jax.random.normal(ks[5], (EMB // 2, EMB), dtype=jnp.float32) * s
        b1 = jnp.zeros((EMB // 2,), dtype=jnp.float32)
        W2 = jax.random.normal(ks[6], (NFEAT // 4, EMB // 2), dtype=jnp.float32) * s
        b2 = jnp.zeros((NFEAT // 4,), dtype=jnp.float32)
        W3 = jax.random.normal(ks[7], (NFEAT // 2, NFEAT // 4), dtype=jnp.float32) * s
        b3 = jnp.zeros((NFEAT // 2,), dtype=jnp.float32)
        W4 = jax.random.normal(ks[8], (NFEAT, NFEAT // 2), dtype=jnp.float32) * s
        b4 = jnp.zeros((NFEAT,), dtype=jnp.float32)
        return {'x': x, 'adj': adj, 'W': W, 'a1': a1, 'a2': a2, 'W1': W1, 'b1': b1, 'W2': W2, 'b2': b2, 'W3': W3, 'b3': b3, 'W4': W4, 'b4': b4}
    _L1_gnn_all = _L1_gnn_setup()
    _L1_gnn_in = {k: v for k, v in _L1_gnn_all.items() if k in ('W', 'a1', 'a2', 'W1', 'b1', 'W2', 'b2', 'W3', 'b3', 'W4', 'b4')}
    del _L1_gnn_all
    return {'x': x, 'adj': adj, 'L0_gnn_rel_pair_index': _L0_gnn_in['rel_pair_index'], 'L0_gnn_Wq': _L0_gnn_in['Wq'], 'L0_gnn_bq': _L0_gnn_in['bq'], 'L0_gnn_Wk': _L0_gnn_in['Wk'], 'L0_gnn_bk': _L0_gnn_in['bk'], 'L1_gnn_W': _L1_gnn_in['W'], 'L1_gnn_a1': _L1_gnn_in['a1'], 'L1_gnn_a2': _L1_gnn_in['a2'], 'L1_gnn_W1': _L1_gnn_in['W1'], 'L1_gnn_b1': _L1_gnn_in['b1'], 'L1_gnn_W2': _L1_gnn_in['W2'], 'L1_gnn_b2': _L1_gnn_in['b2'], 'L1_gnn_W3': _L1_gnn_in['W3'], 'L1_gnn_b3': _L1_gnn_in['b3'], 'L1_gnn_W4': _L1_gnn_in['W4'], 'L1_gnn_b4': _L1_gnn_in['b4']}

def reference(x, adj, L0_gnn_rel_pair_index, L0_gnn_Wq, L0_gnn_bq, L0_gnn_Wk, L0_gnn_bk, L1_gnn_W, L1_gnn_a1, L1_gnn_a2, L1_gnn_W1, L1_gnn_b1, L1_gnn_W2, L1_gnn_b2, L1_gnn_W3, L1_gnn_b3, L1_gnn_W4, L1_gnn_b4):
    import jax
    import jax.numpy as jnp

    def _L0_gnn_ref(inst_feature, aggregator_matrix, rel_pair_index, Wq, bq, Wk, bk):
        import jax, jax.numpy as jnp
        import numpy as np
        N, H, E, HEADS = (1500, 512, 10000, 8)
        DK = H // HEADS
        n = inst_feature.shape[0]
        sub = rel_pair_index[:, 0]
        obj = rel_pair_index[:, 1]
        q = (inst_feature[sub] @ Wq.T + bq).reshape(-1, HEADS, DK)
        k = (inst_feature[obj] @ Wk.T + bk).reshape(-1, HEADS, DK)
        att = ((q * k).sum(-1) / np.sqrt(DK)).T.astype(inst_feature.dtype)
        scores = jnp.zeros((HEADS, n, n), dtype=inst_feature.dtype)
        scores = scores.at[:, sub, obj].set(att)
        mask = (1.0 - aggregator_matrix).astype(bool)
        scores = jnp.where(mask[None], -jnp.inf, scores)
        di = jnp.arange(n)
        scores = scores.at[:, di, di].set(1e-07)
        attn = jax.nn.softmax(scores, axis=2)
        aggregator_factor = attn.sum(axis=0) / HEADS
        return aggregator_factor @ inst_feature

    def _L1_gnn_ref(x, adj, W, a1, a2, W1, b1, W2, b2, W3, b3, W4, b4):
        import jax, jax.numpy as jnp
        import numpy as np
        ALPHA = 0.2
        NEG = -9000000000000000.0
        N, NFEAT, NHID, NHEADS = (2048, 512, 64, 8)
        EMB = NHID * NHEADS
        Wh = jnp.einsum('nf,hfd->hnd', x, W)
        e_src = jnp.einsum('hnd,hd->hn', Wh, a1)
        e_dst = jnp.einsum('hnd,hd->hn', Wh, a2)
        e = jax.nn.leaky_relu(e_src[:, :, None] + e_dst[:, None, :], ALPHA)
        e = jnp.where(adj[None] > 0, e, NEG)
        att = jax.nn.softmax(e, axis=-1)
        h = jnp.einsum('hnm,hmd->hnd', att, Wh)
        h = jax.nn.elu(h)
        enc = jnp.transpose(h, (1, 0, 2)).reshape(x.shape[0], -1)
        out = jax.nn.relu(enc @ W1.T + b1)
        out = jax.nn.relu(out @ W2.T + b2)
        out = jax.nn.relu(out @ W3.T + b3)
        out = out @ W4.T + b4
        return out
    x = _layernorm(x + _L0_gnn_ref(x, adj, L0_gnn_rel_pair_index, L0_gnn_Wq, L0_gnn_bq, L0_gnn_Wk, L0_gnn_bk), axis=-1)
    x = _layernorm(x + _L1_gnn_ref(x, adj, L1_gnn_W, L1_gnn_a1, L1_gnn_a2, L1_gnn_W1, L1_gnn_b1, L1_gnn_W2, L1_gnn_b2, L1_gnn_W3, L1_gnn_b3, L1_gnn_W4, L1_gnn_b4), axis=-1)
    return x

_drawn_inputs = setup_inputs


def setup_inputs(seed=0):
    import zlib

    import numpy as np

    out = dict(_drawn_inputs(seed))
    spreads = {'L0_gnn_bq': (0.0, 2.0),
     'L0_gnn_bk': (0.0, 2.0),
     'L1_gnn_b1': (0.0, 0.669),
     'L1_gnn_b2': (0.0, 0.345),
     'L1_gnn_b3': (0.0, 0.1),
     'L1_gnn_b4': (0.0, 0.1)}
    factors = {'L0_gnn_Wq': 14.276, 'L0_gnn_Wk': 13.707, 'L1_gnn_a1': 23.882, 'L1_gnn_a2': 4.098}
    for name, (base, spread) in spreads.items():
        noise = np.random.default_rng([zlib.crc32(name.encode()), seed]).standard_normal(out[name].shape)
        drawn = base * np.exp(spread * noise) if base else spread * noise
        out[name] = jnp.asarray(drawn.astype(out[name].dtype))
    for name, factor in factors.items():
        out[name] = (out[name] * factor).astype(out[name].dtype)
    return out
```

```python
from contextlib import ExitStack

import concourse.bass as bass
from concourse import mybir

ALU = mybir.AluOpType
ACT = mybir.ActivationFunctionType
F32 = mybir.dt.float32
BF16 = mybir.dt.bfloat16
I32 = mybir.dt.int32
U32 = mybir.dt.uint32
AX_X = mybir.AxisListType.X

P = 128
N = 1354
NT = (N + P - 1) // P
NFULL = N // P
LAST = N - NFULL * P
NP = NT * P
D = 512
FT = D // P
HEADS = 8
DK = D // HEADS
EDGES = 10000
EROWS = 125
ECOLS = EDGES // EROWS
CH = [(c, min(512, N - c)) for c in range(0, N, 512)]
TG = [(t, min(4, NT - t)) for t in range(0, NT, 4)]
BIG = 3.0e38
NEG = 9.0e15
EPS = 1.0e-5


def width(t):
    return LAST if t == NT - 1 else P


def program(nc, x, adj, rel, Wq, bq, Wk, bk, W, a1, a2, W1, b1, W2, b2, W3, b3, W4, b4, out, edge_dram, dvec_dram):
    with ExitStack() as ctx:
        def sb(name, shape, dt=F32):
            return ctx.enter_context(nc.sbuf_tensor(name, shape, dt))

        code = sb("code", [P, NT, NP], BF16)
        nodes = sb("nodes", [P, NT, D])
        featT = sb("featT", [P, FT, NP])
        x1 = sb("x1", [P, NT, D])
        qk = sb("qk", [P, 2, FT, NP])
        wcat = sb("wcat", [P, FT, D])
        va = sb("va", [P, FT, 2 * HEADS])
        w1T = sb("w1T", [P, FT, 2 * P])
        w2T = sb("w2T", [P, 2, P])
        w3T = sb("w3T", [P, 2 * P])
        w4T = sb("w4T", [P, 2, D])
        b4bc = sb("b4bc", [P, D])
        bias = sb("bias", [P, 16])
        ident = sb("ident", [P, P])
        stat = sb("stat", [P, 4, NT])
        esd = sb("esd", [P, NT, 2 * HEADS])
        small = sb("small", [P, 64])
        work = sb("work", [P, 8800])
        erow = small[:, 0:1]
        wh = nodes
        hT1 = featT[:, :, :].rearrange("p f n -> p (f n)")[:, 0:NT * D].rearrange("p (t d) -> p t d", t=NT)
        dbc = qk[:, :, :, :].rearrange("p a f n -> p (a f n)")[:, 0:HEADS * N].rearrange("p (h n) -> p h n", h=HEADS)

        def sem(stack, name):
            return stack.enter_context(nc.semaphore(name))

        prep(nc, sem, locals())
        layer0(nc, sem, locals())
        between(nc, sem, locals())
        layer1(nc, sem, locals())
        tail(nc, sem, locals())


def prep(nc, sem, v):
    x, adj, rel, out = v["x"], v["adj"], v["rel"], v["out"]
    code, nodes, featT, x1, qk, wcat, va = (v[k] for k in ("code", "nodes", "featT", "x1", "qk", "wcat", "va"))
    bias, ident, work, b4bc = v["bias"], v["ident"], v["work"], v["b4bc"]
    edge_dram = v["edge_dram"]
    x1f = x1[:, :, :].rearrange("p t d -> p (t d)")
    qnat = work[:, 0:2048].rearrange("p (t f) -> p t f", t=FT)
    knat = work[:, 2048:4096].rearrange("p (t f) -> p t f", t=FT)
    qTw = work[:, 4096:6144].rearrange("p (t o) -> p t o", t=FT)
    kTw = work[:, 6144:8192].rearrange("p (t o) -> p t o", t=FT)
    adjt = [x1f[:, 0:N], x1f[:, 1408:1408 + N]]
    w1n = x1f[:, 2816:3840].rearrange("p (t f) -> p t f", t=2)
    w2n = x1f[:, 3840:4096]
    w3n = x1f[:, 4096:4352].rearrange("p (t f) -> p t f", t=2)
    w4n = x1f[:, 4352:5376].rearrange("p (t f) -> p t f", t=4)
    w1T, w2T, w3T, w4T = v["w1T"], v["w2T"], v["w3T"], v["w4T"]
    with ExitStack() as ctx:
        def S(name):
            return sem(ctx, name)

        qkf = qk[:, :, :, :].rearrange("p a f n -> p (a f n)")
        zeros = qkf[:, 0:N]
        abc = qkf[:, 2048:3072].rearrange("p (k d) -> p k d", k=2)
        prod = qkf[:, 3072:3584]
        brow = ctx.enter_context(nc.sbuf_tensor("brow", [13, P], F32))
        pair = ctx.enter_context(nc.sbuf_tensor("pair", [EROWS, 2 * ECOLS], I32))
        ef = ctx.enter_context(nc.sbuf_tensor("ef", [EROWS, 4, ECOLS], F32))
        eidx = ctx.enter_context(nc.sbuf_tensor("eidx", [EROWS, ECOLS], I32))
        onesc = ctx.enter_context(nc.sbuf_tensor("onesc", [EROWS, 1], F32))
        TP = ctx.enter_context(nc.psum_tensor("TP", [P, 4, 512], F32))
        QP = ctx.enter_context(nc.psum_tensor("QP", [P, 2, 512], F32))

        x_in, wqk_in, wcat_in, a_in, mlp_in, bias_in, rel_in = (S(n) for n in (
            "x_in", "wqk_in", "wcat_in", "a_in", "mlp_in", "bias_in", "rel_in"))
        adj_in = [S("adj_in0"), S("adj_in1")]
        padded, zero_done, ident_set, ident_done = S("padded"), S("zero_done"), S("ident_set"), S("ident_done")
        zeroed, scattered, index_done = S("zeroed"), S("scattered"), S("index_done")
        tp_full, tp_used, qp_full, qp_used = S("tp_full"), S("tp_used"), S("qp_full"), S("qp_used")
        code_done, dve_chain, va_done = S("code_done"), S("dve_chain"), S("va_done")

        jobs = []
        for src, dst in ((qnat, qTw), (knat, kTw)):
            for f in range(FT):
                jobs.append(("wqk", [src[:, t, f * P:(f + 1) * P] for t in range(FT)], dst[:, f, :]))
        for f in range(FT):
            for t0, k in TG:
                jobs.append(("x", [nodes[:, t, f * P:(f + 1) * P] for t in range(t0, t0 + k)],
                             featT[:, f, t0 * P:(t0 + k) * P]))
        for f in range(FT):
            jobs.append(("mlp", [w1n[:, t, f * P:(f + 1) * P] for t in range(2)], w1T[:, f, :]))
        for f in range(2):
            jobs.append(("mlp", [w2n[:, f * P:(f + 1) * P]], w2T[:, f, :]))
        jobs.append(("mlp", [w3n[:, t, :] for t in range(2)], w3T[:, :]))
        for f in range(2):
            jobs.append(("mlp", [w4n[:, t, f * P:(f + 1) * P] for t in range(4)], w4T[:, f, :]))
        jobs.append(("bias", [brow[:, :]], bias[:, 0:13]))
        qkjobs = [(a, o, c, w) for a in range(2) for o in range(FT) for c, w in ((0, 512), (512, 512), (1024, 384))]
        block = ctx.enter_context(nc.Block())

        @block.sync
        def _(sp):
            sp.dma_start(qnat, v["Wq"].rearrange("(t p) f -> p t f", p=P)).then_inc(wqk_in, 16)
            sp.dma_start(knat, v["Wk"].rearrange("(t p) f -> p t f", p=P)).then_inc(wqk_in, 16)
            sp.wait_ge(padded, 1)
            sp.dma_start(nodes[:, 0:NFULL, :], x[0:NFULL * P, :].rearrange("(t p) f -> p t f", p=P)).then_inc(x_in, 16)
            sp.dma_start(nodes[0:LAST, NFULL, :], x[NFULL * P:N, :]).then_inc(x_in, 16)
            for name, c, k in (("bq", 0, 4), ("bk", 4, 4), ("b1", 8, 2), ("b2", 10, 1), ("b3", 11, 2)):
                sp.dma_start(brow[c:c + k, :], v[name].rearrange("(t p) -> t p", p=P)).then_inc(bias_in, 16)
            for t in range(FT):
                sp.dma_start(wcat[:, t, :].rearrange("p (h d) -> p h d", h=HEADS),
                             v["W"][:, t * P:(t + 1) * P, :].rearrange("h p d -> p h d")).then_inc(wcat_in, 16)
            for t in range(NT):
                if t >= 2:
                    sp.wait_ge(code_done, t - 1)
                sp.dma_start(adjt[t % 2][0:width(t), :], adj[t * P:t * P + width(t), :]).then_inc(adj_in[t % 2], 16)

        @block.scalar
        def _(act):
            act.dma_start(pair[:, :], rel.rearrange("(p c) k -> p (c k)", p=EROWS)).then_inc(rel_in, 16)
            act.dma_start(w1n, v["W1"].rearrange("(t p) f -> p t f", p=P)).then_inc(mlp_in, 16)
            act.dma_start(w2n, v["W2"]).then_inc(mlp_in, 16)
            act.dma_start(w3n, v["W3"].rearrange("(t p) f -> p t f", p=P)).then_inc(mlp_in, 16)
            act.dma_start(w4n, v["W4"].rearrange("(t p) f -> p t f", p=P)).then_inc(mlp_in, 16)
            act.dma_start(b4bc[:, :], v["b4"].rearrange("(a d) -> a d", a=1).to_broadcast([P, D])
                          ).then_inc(mlp_in, 16)
            for k, name in enumerate(("a1", "a2")):
                act.dma_start(abc[:, k, :], v[name].rearrange("(a h) d -> a (h d)", a=1).to_broadcast([P, D])
                              ).then_inc(a_in, 16)
            act.wait_ge(zero_done, 1)
            for t in range(NT):
                act.dma_start(edge_dram[t * P:(t + 1) * P, :], zeros).then_inc(zeroed, 16)
            for n, (_, blocks, dst) in enumerate(jobs):
                act.wait_ge(tp_full, n + 1)
                nc.scalar.copy(dst, TP[:, n % 4, 0:dst.shape[-1]]).then_inc(tp_used, 1)
            act.wait_ge(tp_used, len(jobs))
            act.wait_ge(va_done, 1)
            act.wait_ge(zeroed, 16 * NT)
            for n, (a, o, c, w) in enumerate(qkjobs):
                act.wait_ge(qp_full, n + 1)
                nc.scalar.activation(qk[:, a, o, c:c + w], QP[:, n % 2, 0:w], ACT.Identity,
                                     bias=bias[:, 4 * a + o:4 * a + o + 1]).then_inc(qp_used, 1)
            act.wait_ge(mlp_in, 80)

        @block.gpsimd
        def _(pool):
            nc.gpsimd.memset(ident[:, :], 0.0).then_inc(ident_set, 1)
            pool.wait_ge(ident_set, 1)
            nc.gpsimd.affine_select(out=ident[:, :], in_=ident[:, :], compare_op=ALU.not_equal, fill=1.0, base=0,
                                    pattern=[[-1, P]], channel_multiplier=1).then_inc(ident_done, 1)
            pool.wait_ge(zeroed, 16 * NT)
            pool.wait_ge(index_done, 1)
            for c in range(ECOLS):
                pool.wait_ge(scattered, 16 * c)
                nc.gpsimd.indirect_dma_start(
                    out=edge_dram.rearrange("a (b k) -> (a b) k", k=1),
                    out_offset=bass.IndirectOffsetOnAxis(ap=eidx[:, c:c + 1].bitcast(U32), axis=0),
                    in_=onesc[:, 0:1], in_offset=None, bounds_check=N * N - 1, oob_is_err=False).then_inc(scattered, 16)
            pool.wait_ge(scattered, 16 * ECOLS)

        @block.vector
        def _(dve):
            links = [0]

            def link(ins):
                links[0] += 1
                ins.then_inc(dve_chain, 1)
                dve.wait_ge(dve_chain, links[0])

            nc.vector.memset(zeros, 0.0).then_inc(zero_done, 1)
            nc.vector.memset(nodes[64:P, NFULL, :], 0.0).then_inc(padded, 1)
            link(nc.vector.memset(code[:, :, :], 0.0))
            nc.vector.memset(onesc[:, :], 1.0)
            dve.wait_ge(rel_in, 16)
            both = pair[:, :].rearrange("p (c k) -> p k c", k=2)
            for k in range(2):
                link(nc.vector.tensor_copy(ef[:, k, :], both[:, k, :]))
                link(nc.vector.tensor_scalar(ef[:, 2, :], ef[:, k, :], 0.0, float(N), ALU.is_lt, ALU.mult))
                link(nc.vector.tensor_tensor(ef[:, k, :], ef[:, k, :], ef[:, 2, :], ALU.add))
            link(nc.vector.tensor_tensor(ef[:, 2, :], ef[:, 0, :], ef[:, 1, :], ALU.not_equal))
            for k in range(2):
                for lim, op in ((0.0, ALU.is_ge), (float(N), ALU.is_lt)):
                    link(nc.vector.scalar_tensor_tensor(ef[:, 2, :], ef[:, k, :], lim, ef[:, 2, :], op, ALU.mult))
            link(nc.vector.scalar_tensor_tensor(ef[:, 3, :], ef[:, 0, :], float(N), ef[:, 1, :], ALU.mult, ALU.add))
            link(nc.vector.scalar_tensor_tensor(ef[:, 3, :], ef[:, 3, :], float(-N * N), ef[:, 2, :], ALU.add, ALU.mult))
            link(nc.vector.tensor_scalar(ef[:, 3, :], ef[:, 3, :], float(N * N), None, ALU.add))
            nc.vector.tensor_copy(eidx[:, :], ef[:, 3, :]).then_inc(index_done, 1)
            dve.wait_ge(wcat_in, 64)
            dve.wait_ge(a_in, 32)
            for k in range(2):
                for t in range(FT):
                    link(nc.vector.tensor_tensor(prod, wcat[:, t, :], abc[:, k, :], ALU.mult))
                    link(nc.vector.tensor_reduce(va[:, t, k * HEADS:(k + 1) * HEADS],
                                                 prod.rearrange("p (h d) -> p h d", h=HEADS), AX_X, ALU.add))
            dve.sem_inc(va_done, 1)
            for t in range(NT):
                w = width(t)
                dve.wait_ge(adj_in[t % 2], 16 * (t // 2 + 1))
                link(nc.vector.tensor_scalar(code[0:w, t, 0:N], adjt[t % 2][0:w, :], 1.0, None, ALU.is_equal))
                nc.vector.scalar_tensor_tensor(code[0:w, t, 0:N], adjt[t % 2][0:w, :], 0.0, code[0:w, t, 0:N],
                                               ALU.is_gt, ALU.add).then_inc(code_done, 1)

        @block.tensor
        def _(pe):
            pe.wait_ge(ident_done, 1)
            waits = {"wqk": (wqk_in, 32), "x": (x_in, 32), "mlp": (mlp_in, 80), "bias": (bias_in, 80)}
            for n, (kind, blocks, dst) in enumerate(jobs):
                pe.wait_ge(*waits[kind])
                if n >= 4:
                    pe.wait_ge(tp_used, n - 3)
                for k, b in enumerate(blocks):
                    r = b.shape[0]
                    last = nc.tensor.transpose(TP[:, n % 4, k * P:k * P + r], b, ident[0:r, 0:r])
                last.then_inc(tp_full, 1)
            pe.wait_ge(tp_used, len(jobs))
            for n, (a, o, c, w) in enumerate(qkjobs):
                if n >= 2:
                    pe.wait_ge(qp_used, n - 1)
                wT = (qTw, kTw)[a]
                for f in range(FT):
                    last = nc.tensor.matmul(QP[:, n % 2, 0:w], wT[:, f, o * P:(o + 1) * P], featT[:, f, c:c + w],
                                            start=(f == 0), stop=(f == FT - 1))
                last.then_inc(qp_full, 1)


def layer0(nc, sem, v):
    code, nodes, x1, qk, stat, ident, work, small = (v[k] for k in (
        "code", "nodes", "x1", "qk", "stat", "ident", "work", "small"))
    edge_dram = v["edge_dram"]
    o = 0
    def cut(w):
        nonlocal o
        o += w
        return work[:, o - w:o]
    T = [cut(N), cut(N)]
    mask = cut(NP)
    acc = cut(NP)
    edge = cut(N)
    qs = cut(FT * P).rearrange("p (f n) -> p f n", f=FT)
    factT = cut(NP)
    with ExitStack() as ctx:
        def S(name):
            return sem(ctx, "l0_" + name)
        SP_ = [ctx.enter_context(nc.psum_tensor(f"S{k}", [P, 3, 512], F32)) for k in range(2)]
        Y = ctx.enter_context(nc.psum_tensor("Y", [P, D], F32))
        Sf = [s[:, :, :].rearrange("p b n -> p (b n)") for s in SP_]
        edge_in, q_staged, scores, masked, top, prob, accd, transposed, copied, summed, done, mask_ready, chain = (
            S(n) for n in ("edge_in", "q_staged", "scores", "masked", "top", "prob", "accd", "transposed", "copied",
                           "summed", "done", "mask_ready", "chain"))
        nmax, den, rden = small[:, 0:8], small[:, 8:16], small[:, 16:24]
        block = ctx.enter_context(nc.Block())

        @block.sync
        def _(sp):
            with sp.Fori(0, NT) as t:
                sp.wait_ge(done, t + 1)
                sp.dma_start(edge, edge_dram[bass.ts(t, P), :]).then_inc(edge_in, 16)

        @block.scalar
        def _(act):
            act.sem_inc(copied, 1)
            with act.Fori(0, NT) as t:
                act.wait_ge(summed, t + 1)
                nc.scalar.activation(qs, qk[:, 0, :, bass.ts(t, P)], ACT.Copy, scale=DK ** -0.5).then_inc(q_staged, 1)
                for h in range(HEADS):
                    act.wait_ge(top, t * HEADS + (h + 1))
                    nc.scalar.activation(T[h % 2], T[h % 2], ACT.Exp, bias=nmax[:, h:h + 1],
                                         accum_out=den[:, h:h + 1]).then_inc(prob, 1)
                act.wait_ge(transposed, t + 1)
                nc.scalar.copy(factT, Sf[0][:, 0:NP]).then_inc(copied, 1)

        @block.tensor
        def _(pe):
            pe.sem_inc(summed, 1)
            with pe.Fori(0, NT) as t:
                pe.wait_ge(q_staged, t + 1)
                pe.wait_ge(copied, t + 1)
                for h in range(HEADS):
                    if h >= 2:
                        pe.wait_ge(masked, t * HEADS + (h - 1))
                    r = DK * (h % 2)
                    for c, w in CH:
                        last = nc.tensor.matmul(Sf[h % 2][:, c:c + w], qs[r:r + DK, h // 2, :],
                                                qk[r:r + DK, 1, h // 2, c:c + w], start=True, stop=True)
                    last.then_inc(scores, 1)
                pe.wait_ge(accd, t + 1)
                for k in range(NT):
                    last = nc.tensor.transpose(Sf[0][:, k * P:(k + 1) * P], acc[:, k * P:(k + 1) * P], ident[:, :])
                last.then_inc(transposed, 1)
                pe.wait_ge(copied, t + 2)
                pe.wait_ge(done, t + 1)
                for k in range(NT):
                    last = nc.tensor.matmul(Y[:, :], factT[:, k * P:(k + 1) * P], nodes[:, k, :],
                                            start=(k == 0), stop=(k == NT - 1))
                last.then_inc(summed, 1)

        @block.vector
        def _(dve):
            LINKS = 3 + 3 * HEADS - 1
            nc.vector.memset(acc[:, N:NP], 0.0)
            dve.sem_inc(done, 1)
            with dve.Fori(0, NT) as t:
                links = [0]

                def link(ins):
                    links[0] += 1
                    ins.then_inc(chain, 1)
                    dve.wait_ge(chain, t * LINKS + links[0])

                link(nc.vector.tensor_scalar(mask, code[:, t, :], 1.5, -BIG, ALU.is_lt, ALU.mult))
                dg = mask[:, bass.ts(t, P)]
                link(nc.vector.scalar_tensor_tensor(dg, ident[:, :], 1.0, dg, ALU.not_equal, ALU.mult))
                link(nc.vector.scalar_tensor_tensor(dg, ident[:, :], 1.0e-7, dg, ALU.mult, ALU.add))
                dve.wait_ge(edge_in, (t + 1) * 16)
                for h in range(HEADS + 1):
                    if h < HEADS:
                        dve.wait_ge(scores, t * HEADS + (h + 1))
                        nc.vector.tensor_tensor(T[h % 2], Sf[h % 2][:, 0:N], edge, ALU.mult).then_inc(masked, 1)
                        dve.wait_ge(masked, t * HEADS + (h + 1))
                        link(nc.vector.tensor_tensor(T[h % 2], T[h % 2], mask[:, 0:N], ALU.add))
                        nc.vector.tensor_reduce(nmax[:, h:h + 1], T[h % 2], AX_X, ALU.max, negate=True).then_inc(top, 1)
                    if h >= 1:
                        g = h - 1
                        dve.wait_ge(prob, t * HEADS + h)
                        link(nc.vector.reciprocal(rden[:, g:g + 1], den[:, g:g + 1]))
                        if g == 0:
                            link(nc.vector.tensor_scalar(acc[:, 0:N], T[0], rden[:, 0:1], None, ALU.mult))
                        elif g < HEADS - 1:
                            link(nc.vector.scalar_tensor_tensor(acc[:, 0:N], T[g % 2], rden[:, g:g + 1], acc[:, 0:N],
                                                                ALU.mult, ALU.add))
                        else:
                            nc.vector.scalar_tensor_tensor(acc[:, 0:N], T[g % 2], rden[:, g:g + 1], acc[:, 0:N],
                                                           ALU.mult, ALU.add).then_inc(accd, 1)
                dve.wait_ge(summed, t + 2)
                nc.vector.scalar_tensor_tensor(x1[:, t, :], Y[:, :], 1.0 / HEADS, nodes[:, t, :],
                                               ALU.mult, ALU.add).then_inc(done, 1)
                assert links[0] == LINKS


def between(nc, sem, v):
    x1, featT, nodes, wcat, va, stat, esd, ident, work, small = (v[k] for k in (
        "x1", "featT", "nodes", "wcat", "va", "stat", "esd", "ident", "work", "small"))
    dbc, wh, dvec_dram = v["dbc"], v["wh"], v["dvec_dram"]
    with ExitStack() as ctx:
        def S(name):
            return sem(ctx, "b_" + name)
        TP = ctx.enter_context(nc.psum_tensor("TPb", [P, 2, 512], F32))
        WP = ctx.enter_context(nc.psum_tensor("WP", [P, 2, 512], F32))
        EP = ctx.enter_context(nc.psum_tensor("EP", [P, 2, 512], F32))
        dvec = work[0:HEADS, 0:N]
        stats = ctx.enter_context(nc.sbuf_tensor("stats0", [P, NT, 6], F32))
        (var_ready, dev_ready, normed, tp_full, tp_used, wh_full, wh_used, e_full, e_used, vec_out, vec_in, chain) = (
            S(n) for n in ("var_ready", "dev_ready", "normed", "tp_full", "tp_used", "wh_full", "wh_used", "e_full",
                           "e_used", "vec_out", "vec_in", "chain"))
        tjobs = [(t0, k, f) for t0, k in TG for f in range(FT)]
        block = ctx.enter_context(nc.Block())

        @block.scalar
        def _(act):
            act.wait_ge(var_ready, 1)
            nc.scalar.activation(stat[:, 2, :], stat[:, 1, :], ACT.Sqrt).then_inc(dev_ready, 1)
            for n, (t0, k, f) in enumerate(tjobs):
                act.wait_ge(tp_full, n + 1)
                nc.scalar.copy(featT[:, f, t0 * P:(t0 + k) * P], TP[:, n % 2, 0:k * P]).then_inc(tp_used, 1)
            for n, (c, w) in enumerate(CH):
                act.wait_ge(e_full, n + 1)
                nc.scalar.copy(dvec[:, c:c + w], EP[0:HEADS, n % 2, 0:w]).then_inc(e_used, 1)
            act.wait_ge(e_used, len(CH))
            act.dma_start(dvec_dram, dvec).then_inc(vec_out, 16)
            act.wait_ge(vec_out, 16)
            for h in range(HEADS):
                act.dma_start(dbc[:, h, :], dvec_dram[h:h + 1, :].to_broadcast([P, N])).then_inc(vec_in, 16)
            act.wait_ge(vec_in, 16 * HEADS)

        @block.vector
        def _(dve):
            links = [0]

            def link(ins):
                links[0] += 1
                ins.then_inc(chain, 1)
                dve.wait_ge(chain, links[0])

            for t in range(NT):
                link(nc.vector.bn_stats(stats[:, t, :], x1[:, t, :]))
                link(nc.vector.bn_aggr(stat[:, 0:2, t], stats[:, t, :]))
            layer_norm_scale(nc, dve, link, stat, var_ready, dev_ready, small[:, 0:NT])
            for t in range(NT):
                nc.vector.tensor_scalar(x1[:, t, :], x1[:, t, :], stat[:, 0, t:t + 1], stat[:, 3, t:t + 1],
                                        ALU.subtract, ALU.mult).then_inc(normed, 1)
            for t in range(NT):
                dve.wait_ge(wh_full, t + 1)
                nc.vector.tensor_copy(wh[:, t, :], WP[:, t % 2, :])
                nc.vector.tensor_copy(esd[:, t, :], EP[:, t % 2, 0:2 * HEADS]).then_inc(wh_used, 1)

        @block.tensor
        def _(pe):
            for n, (t0, k, f) in enumerate(tjobs):
                pe.wait_ge(normed, t0 + k)
                if n >= 2:
                    pe.wait_ge(tp_used, n - 1)
                for j in range(k):
                    last = nc.tensor.transpose(TP[:, n % 2, j * P:(j + 1) * P], x1[:, t0 + j, f * P:(f + 1) * P],
                                               ident[:, :])
                last.then_inc(tp_full, 1)
            pe.wait_ge(tp_used, len(tjobs))
            for t in range(NT):
                if t >= 2:
                    pe.wait_ge(wh_used, t - 1)
                for f in range(FT):
                    nc.tensor.matmul(WP[:, t % 2, :], featT[:, f, t * P:(t + 1) * P], wcat[:, f, :],
                                     start=(f == 0), stop=(f == FT - 1))
                for f in range(FT):
                    last = nc.tensor.matmul(EP[:, t % 2, 0:2 * HEADS], featT[:, f, t * P:(t + 1) * P], va[:, f, :],
                                            start=(f == 0), stop=(f == FT - 1))
                last.then_inc(wh_full, 1)
            pe.wait_ge(wh_used, NT)
            for n, (c, w) in enumerate(CH):
                if n >= 2:
                    pe.wait_ge(e_used, n - 1)
                for f in range(FT):
                    last = nc.tensor.matmul(EP[0:HEADS, n % 2, 0:w], va[:, f, HEADS:2 * HEADS], featT[:, f, c:c + w],
                                            start=(f == 0), stop=(f == FT - 1))
                last.then_inc(e_full, 1)


def layer_norm_scale(nc, dve, link, stat, var_ready, dev_ready, tmp):
    nc.vector.tensor_scalar(stat[:, 1, :], stat[:, 1, :], EPS, None, ALU.add).then_inc(var_ready, 1)
    dve.wait_ge(dev_ready, 1)
    link(nc.vector.reciprocal(stat[:, 3, :], stat[:, 2, :]))
    link(nc.vector.tensor_tensor(tmp, stat[:, 3, :], stat[:, 3, :], ALU.mult))
    link(nc.vector.tensor_tensor(tmp, tmp, stat[:, 1, :], ALU.mult))
    link(nc.vector.tensor_scalar(tmp, tmp, -0.5, 1.5, ALU.mult, ALU.add))
    link(nc.vector.tensor_tensor(stat[:, 3, :], stat[:, 3, :], tmp, ALU.mult))


def layer1(nc, sem, v):
    code, nodes, work, small, esd, ident = (v[k] for k in ("code", "nodes", "work", "small", "esd", "ident"))
    dbc, wh, hT1 = v["dbc"], v["wh"], v["hT1"]
    o = 0
    def cut(w):
        nonlocal o
        o += w
        return work[:, o - w:o]
    T = [cut(NP), cut(NP)]
    mask = cut(N)
    scaled = cut(N)
    PT = cut(NP)
    with ExitStack() as ctx:
        def S(name):
            return sem(ctx, "l1_" + name)
        SP_ = [ctx.enter_context(nc.psum_tensor(f"PT{k}", [P, 3, 512], F32)) for k in range(2)]
        O = ctx.enter_context(nc.psum_tensor("O", [P, D], F32))
        Sf = [s[:, :, :].rearrange("p b n -> p (b n)") for s in SP_]
        top, prob, transposed, copied, mixed, done, chain = (
            S(n) for n in ("top", "prob", "transposed", "copied", "mixed", "done", "chain"))
        nmax, den, rden = small[:, 0:8], small[:, 8:16], small[:, 16:24]
        block = ctx.enter_context(nc.Block())

        @block.scalar
        def _(act):
            with act.Fori(0, NT) as t:
                for h in range(HEADS + 1):
                    if h < HEADS:
                        act.wait_ge(top, t * HEADS + (h + 1))
                        nc.scalar.activation(T[h % 2][:, 0:N], T[h % 2][:, 0:N], ACT.Exp, bias=nmax[:, h:h + 1],
                                             accum_out=den[:, h:h + 1]).then_inc(prob, 1)
                    if h >= 1:
                        act.wait_ge(transposed, t * HEADS + (h + 1))
                        act.wait_ge(mixed, t * HEADS + h)
                        nc.scalar.copy(PT, Sf[(h - 1) % 2][:, 0:NP]).then_inc(copied, 1)

        @block.tensor
        def _(pe):
            pe.sem_inc(transposed, 1)
            pe.sem_inc(mixed, 1)
            with pe.Fori(0, NT) as t:
                for h in range(HEADS):
                    pe.wait_ge(prob, t * HEADS + (h + 1))
                    for k in range(NT):
                        last = nc.tensor.transpose(Sf[h % 2][:, k * P:(k + 1) * P], T[h % 2][:, k * P:(k + 1) * P],
                                                   ident[:, :])
                    last.then_inc(transposed, 1)
                    pe.wait_ge(copied, t * HEADS + (h + 1))
                    if h == 0:
                        pe.wait_ge(done, t + 1)
                    for k in range(NT):
                        last = nc.tensor.matmul(O[:, h * DK:(h + 1) * DK], PT[:, k * P:(k + 1) * P],
                                                wh[:, k, h * DK:(h + 1) * DK], start=(k == 0), stop=(k == NT - 1))
                    last.then_inc(mixed, 1)

        @block.vector
        def _(dve):
            LINKS = 1 + 3 * HEADS + 1
            nc.vector.memset(T[0][:, N:NP], 0.0)
            nc.vector.memset(T[1][:, N:NP], 0.0)
            dve.sem_inc(done, 1)
            with dve.Fori(0, NT) as t:
                links = [0]

                def link(ins):
                    links[0] += 1
                    ins.then_inc(chain, 1)
                    dve.wait_ge(chain, t * LINKS + links[0])

                link(nc.vector.tensor_scalar(mask, code[:, t, 0:N], 1.0e38, -NEG, ALU.mult, ALU.add))
                for h in range(HEADS):
                    link(nc.vector.tensor_scalar(scaled, dbc[:, h, :], esd[:, t, h:h + 1], 0.2, ALU.add, ALU.mult))
                    if h >= 2:
                        dve.wait_ge(transposed, t * HEADS + h)
                    else:
                        dve.wait_ge(done, t + 1)
                        dve.wait_ge(transposed, t * HEADS + 1)
                    Th = T[h % 2][:, 0:N]
                    link(nc.vector.scalar_tensor_tensor(Th, dbc[:, h, :], esd[:, t, h:h + 1], scaled, ALU.add, ALU.max))
                    link(nc.vector.tensor_tensor(Th, Th, mask, ALU.min))
                    nc.vector.tensor_reduce(nmax[:, h:h + 1], Th, AX_X, ALU.max, negate=True).then_inc(top, 1)
                dve.wait_ge(mixed, t * HEADS + (HEADS + 1))
                link(nc.vector.reciprocal(rden, den))
                nc.vector.tensor_tensor(hT1[:, t, :].rearrange("p (h d) -> p h d", h=HEADS),
                                        O[:, :].rearrange("p (h d) -> p h d", h=HEADS),
                                        rden.rearrange("p (h d) -> p h d", d=1).to_broadcast([P, HEADS, DK]),
                                        ALU.mult).then_inc(done, 1)
                assert links[0] == LINKS


def tail(nc, sem, v):
    x1, hT1, stat, ident, work, small, bias, b4bc = (v[k] for k in (
        "x1", "hT1", "stat", "ident", "work", "small", "bias", "b4bc"))
    w1T, w2T, w3T, w4T, out = (v[k] for k in ("w1T", "w2T", "w3T", "w4T", "out"))
    nodes = v["nodes"]
    qkf = v["qk"][:, :, :, :].rearrange("p a f n -> p (a f n)")
    encT = [qkf[:, k * 2048:(k + 1) * 2048].rearrange("p (f n) -> p f n", f=FT) for k in range(2)]
    o1 = [work[:, k * 1024:(k + 1) * 1024].rearrange("p (f n) -> p f n", f=2) for k in range(2)]
    o2 = [work[:, 2048 + k * 512:2560 + k * 512] for k in range(2)]
    o3 = [work[:, 3072 + k * 1024:4096 + k * 1024].rearrange("p (f n) -> p f n", f=2) for k in range(2)]
    ex = [work[:, 5120 + k * 512:5632 + k * 512] for k in range(2)]
    with ExitStack() as ctx:
        def S(name):
            return sem(ctx, "t_" + name)
        TP = ctx.enter_context(nc.psum_tensor("TPt", [P, 2, 512], F32))
        MP = ctx.enter_context(nc.psum_tensor("MP", [P, 2, 512], F32))
        OP = ctx.enter_context(nc.psum_tensor("OP", [P, 2, 512], F32))
        stats = ctx.enter_context(nc.sbuf_tensor("stats1", [P, NT, 6], F32))
        (neg_ready, exp_ready, elu_done, tp_full, tp_used, mm_full, mm_used, out_full, out_used, var_ready, dev_ready,
         normed, stored, chain) = (S(n) for n in (
            "neg_ready", "exp_ready", "elu_done", "tp_full", "tp_used", "mm_full", "mm_used", "out_full", "out_used",
            "var_ready", "dev_ready", "normed", "stored", "chain"))
        NG = len(TG)
        block = ctx.enter_context(nc.Block())

        @block.sync
        def _(sp):
            for g, (t0, k) in enumerate(TG):
                sp.wait_ge(normed, t0 + k)
                full = min(k, NFULL - t0)
                sp.dma_start(out[t0 * P:(t0 + full) * P, :].rearrange("(t p) f -> p t f", p=P),
                             x1[:, t0:t0 + full, :]).then_inc(stored, 16)
            sp.dma_start(out[NFULL * P:N, :], x1[0:LAST, NFULL, :]).then_inc(stored, 16)
            sp.wait_ge(stored, 16 * (NG + 1))

        @block.scalar
        def _(act):
            for t in range(NT):
                act.wait_ge(neg_ready, t + 1)
                nc.scalar.activation(ex[t % 2], ex[t % 2], ACT.Exp).then_inc(exp_ready, 1)
            m = 0
            for g, (t0, k) in enumerate(TG):
                w = k * P
                for f in range(FT):
                    act.wait_ge(tp_full, g * FT + f + 1)
                    nc.scalar.copy(encT[g % 2][:, f, 0:w], TP[:, f % 2, 0:w]).then_inc(tp_used, 1)
                for dst, b in ((o1[g % 2][:, 0, 0:w], 8), (o1[g % 2][:, 1, 0:w], 9), (o2[g % 2][:, 0:w], 10),
                               (o3[g % 2][:, 0, 0:w], 11), (o3[g % 2][:, 1, 0:w], 12)):
                    act.wait_ge(mm_full, m + 1)
                    nc.scalar.activation(dst, MP[:, m % 2, 0:w], ACT.Relu, bias=bias[:, b:b + 1]).then_inc(mm_used, 1)
                    m += 1
            act.wait_ge(var_ready, 1)
            nc.scalar.activation(stat[:, 2, :], stat[:, 1, :], ACT.Sqrt).then_inc(dev_ready, 1)

        @block.tensor
        def _(pe):
            m = 0
            for g, (t0, k) in enumerate(TG):
                w = k * P
                pe.wait_ge(elu_done, t0 + k)
                for f in range(FT):
                    if g * FT + f >= 2:
                        pe.wait_ge(tp_used, g * FT + f - 1)
                    for j in range(k):
                        last = nc.tensor.transpose(TP[:, f % 2, j * P:(j + 1) * P], hT1[:, t0 + j, f * P:(f + 1) * P],
                                                   ident[:, :])
                    last.then_inc(tp_full, 1)
                pe.wait_ge(tp_used, (g + 1) * FT)
                e, a, b, c = encT[g % 2], o1[g % 2], o2[g % 2], o3[g % 2]
                layers = ([[(w1T[:, f, o * P:(o + 1) * P], e[:, f, 0:w]) for f in range(FT)] for o in range(2)],
                          [[(w2T[:, f, :], a[:, f, 0:w]) for f in range(2)]],
                          [[(w3T[:, o * P:(o + 1) * P], b[:, 0:w])] for o in range(2)])
                for layer in layers:
                    pe.wait_ge(mm_used, m)
                    for terms in layer:
                        for n, (l, r) in enumerate(terms):
                            last = nc.tensor.matmul(MP[:, m % 2, 0:w], l, r, start=(n == 0), stop=(n == len(terms) - 1))
                        last.then_inc(mm_full, 1)
                        m += 1
                pe.wait_ge(mm_used, m)
                for j in range(k):
                    t = t0 + j
                    if t >= 2:
                        pe.wait_ge(out_used, t - 1)
                    for f in range(2):
                        last = nc.tensor.matmul(OP[:, t % 2, :], c[:, f, j * P:(j + 1) * P], w4T[:, f, :],
                                                start=(f == 0), stop=(f == 1))
                    last.then_inc(out_full, 1)

        @block.vector
        def _(dve):
            links = [0]

            def link(ins):
                links[0] += 1
                ins.then_inc(chain, 1)
                dve.wait_ge(chain, links[0])

            for t in range(NT):
                link(nc.vector.tensor_tensor(x1[:, t, :], x1[:, t, :], b4bc[:, :], ALU.add))
            for t in range(NT + 1):
                if t < NT:
                    nc.vector.tensor_scalar(ex[t % 2], hT1[:, t, :], 0.0, None, ALU.min).then_inc(neg_ready, 1)
                if t >= 1:
                    z = hT1[:, t - 1, :]
                    dve.wait_ge(exp_ready, t)
                    link(nc.vector.tensor_scalar(ex[(t - 1) % 2], ex[(t - 1) % 2], -1.0, None, ALU.add))
                    nc.vector.scalar_tensor_tensor(z, z, 0.0, ex[(t - 1) % 2], ALU.max, ALU.add).then_inc(elu_done, 1)
                    dve.wait_ge(elu_done, t)
            for t in range(NT):
                dve.wait_ge(out_full, t + 1)
                nc.vector.tensor_tensor(x1[:, t, :], OP[:, t % 2, :], x1[:, t, :], ALU.add).then_inc(out_used, 1)
                dve.wait_ge(out_used, t + 1)
                link(nc.vector.bn_stats(stats[:, t, :], x1[:, t, :]))
                link(nc.vector.bn_aggr(stat[:, 0:2, t], stats[:, t, :]))
            layer_norm_scale(nc, dve, link, stat, var_ready, dev_ready, small[:, 0:NT])
            for t in range(NT):
                nc.vector.tensor_scalar(x1[:, t, :], x1[:, t, :], stat[:, 0, t:t + 1], stat[:, 3, t:t + 1],
                                        ALU.subtract, ALU.mult).then_inc(normed, 1)


_INS = ['x', 'adj', 'L0_gnn_rel_pair_index', 'L0_gnn_Wq', 'L0_gnn_bq', 'L0_gnn_Wk', 'L0_gnn_bk', 'L1_gnn_W',
        'L1_gnn_a1', 'L1_gnn_a2', 'L1_gnn_W1', 'L1_gnn_b1', 'L1_gnn_W2', 'L1_gnn_b2', 'L1_gnn_W3', 'L1_gnn_b3',
        'L1_gnn_W4', 'L1_gnn_b4']


def kernel(**inputs):
    import numpy as np
    import concourse.bacc as bacc
    from concourse.bass_utils import run_bass_kernel_spmd

    nc = bacc.Bacc("TRN2", target_bir_lowering=False, num_devices=1)
    arrays, args = {}, []
    for name in _INS:
        a = np.ascontiguousarray(inputs[name])
        arrays[f"in_{name}"] = a
        args.append(nc.dram_tensor(f"in_{name}", a.shape, mybir.dt.from_np(a.dtype), kind="ExternalInput").ap())
    args.append(nc.dram_tensor("out_0", (N, D), F32, kind="ExternalOutput").ap())
    args.append(nc.dram_tensor("edge_matrix", (NP, N), F32, kind="Internal").ap())
    args.append(nc.dram_tensor("dst_scores", (HEADS, N), F32, kind="Internal").ap())
    program(nc, *args)
    r = run_bass_kernel_spmd(nc, [arrays], core_ids=[0])
    return r.results[0]["out_0"]
```

```python
from contextlib import ExitStack

import concourse.bass as bass
from concourse import mybir

ALU = mybir.AluOpType
ACT = mybir.ActivationFunctionType
F32 = mybir.dt.float32
BF16 = mybir.dt.bfloat16
I32 = mybir.dt.int32
U32 = mybir.dt.uint32
AX_X = mybir.AxisListType.X

P = 128
N = 1354
NT = (N + P - 1) // P
NFULL = N // P
LAST = N - NFULL * P
NP = NT * P
D = 512
FT = D // P
HEADS = 8
DK = D // HEADS
EDGES = 10000
EROWS = 125
ECOLS = EDGES // EROWS
CH = [(c, min(512, N - c)) for c in range(0, N, 512)]
TG = [(t, min(4, NT - t)) for t in range(0, NT, 4)]
BIG = 3.0e38
SLOTS = P
SPREAD = 80.0
NEG = 9.0e15
EPS = 1.0e-5


def width(t):
    return LAST if t == NT - 1 else P


def program(nc, x, adj, rel, Wq, bq, Wk, bk, W, a1, a2, W1, b1, W2, b2, W3, b3, W4, b4, out, edge_dram, adj_dram,
            sd_dram):
    with ExitStack() as ctx:
        def sb(name, shape, dt=F32):
            return ctx.enter_context(nc.sbuf_tensor(name, shape, dt))

        near1T = sb("near1T", [P, NT, NP], BF16)
        nodes = sb("nodes", [P, NT, D])
        featT = sb("featT", [P, FT, NP])
        x1 = sb("x1", [P, NT, D])
        qk = sb("qk", [P, 2 * FT * NP])
        work = sb("work", [P, 9400])
        wcat = sb("wcat", [P, FT, D])
        va = sb("va", [P, FT, 40])
        w1T = sb("w1T", [P, FT, 2 * P])
        w2T = sb("w2T", [P, 2, P])
        w3T = sb("w3T", [P, 2 * P])
        w4T = sb("w4T", [P, 2, D])
        b4bc = sb("b4bc", [P, D])
        bias = sb("bias", [P, 16])
        ident = sb("ident", [P, P])
        before = sb("before", [P, P])
        ones = sb("ones", [P, P])
        stat = sb("stat", [P, 4, NT])
        esd = sb("esd", [P, NT, 2 * HEADS])
        deg0 = sb("deg0", [P, NT])
        codesum = sb("codesum", [P, NT])
        edges = sb("edges", [EROWS, ECOLS, 3])
        met = sb("met", [EROWS, ECOLS])
        colsum = sb("colsum", [ECOLS, 1])
        eidx = sb("eidx", [EROWS, ECOLS], I32)
        small = sb("small", [P, 64])
        flags = sb("flags", [1, 2], I32)
        wh = nodes
        hT1 = featT[:, :, :].rearrange("p f n -> p (f n)")[:, 0:NT * D].rearrange("p (t d) -> p t d", t=NT)
        qk4 = qk[:, :].rearrange("p (a f n) -> p a f n", a=2, f=FT)
        sbc = qk[:, 0:HEADS * N].rearrange("p (h n) -> p h n", h=HEADS)
        qTw = work[:, 4116:6164].rearrange("p (t o) -> p t o", t=FT)
        kTw = work[:, 6164:8212].rearrange("p (t o) -> p t o", t=FT)

        def sem(stack, name):
            return stack.enter_context(nc.semaphore(name))

        v = locals()
        prep(nc, sem, v)
        (flag,) = load_flag(nc, flags[0:1, 0:1])
        with nc.If(flag == 1):
            layer0_sparse(nc, sem, v)
        with nc.Else():
            dense_prep(nc, sem, v, 0)
            layer0_dense(nc, sem, v)
        nc.end_all_ifs()
        between(nc, sem, v)
        (flag,) = load_flag(nc, flags[0:1, 1:2])
        with nc.If(flag == 1):
            layer1_factored(nc, sem, v)
        with nc.Else():
            dense_prep(nc, sem, v, 1)
            layer1_dense(nc, sem, v)
        nc.end_all_ifs()
        tail(nc, sem, v)


def load_flag(nc, ap):
    r = nc.values_load(ap, min_val=0, max_val=1)
    return (r,)


def prep(nc, sem, v):
    x, adj, rel = v["x"], v["adj"], v["rel"]
    near1T, nodes, featT, x1, qk, wcat, va = (v[k] for k in ("near1T", "nodes", "featT", "x1", "qk", "wcat", "va"))
    bias, ident, work, b4bc, before, ones = (v[k] for k in ("bias", "ident", "work", "b4bc", "before", "ones"))
    deg0, codesum, edges, met, colsum, eidx, flags = (v[k] for k in (
        "deg0", "codesum", "edges", "met", "colsum", "eidx", "flags"))
    x1f = x1[:, :, :].rearrange("p t d -> p (t d)")
    ff = featT[:, :, :].rearrange("p f n -> p (f n)")
    qnat = x1f[:, 0:2048].rearrange("p (t f) -> p t f", t=FT)
    knat = x1f[:, 2048:4096].rearrange("p (t f) -> p t f", t=FT)
    qTw, kTw = v["qTw"], v["kTw"]
    abc = ff[:, 0:1024].rearrange("p (k d) -> p k d", k=2)
    prod = ff[:, 1024:1536]
    w1n = ff[:, 1536:2560].rearrange("p (t f) -> p t f", t=2)
    w2n = ff[:, 2560:2816]
    w3n = ff[:, 2816:3072].rearrange("p (t f) -> p t f", t=2)
    w4n = ff[:, 3072:4096].rearrange("p (t f) -> p t f", t=4)
    w1T, w2T, w3T, w4T = v["w1T"], v["w2T"], v["w3T"], v["w4T"]
    ffb = ff.bitcast(BF16)
    xpart = [ffb[:, 0:NT * D].rearrange("p (t d) -> p t d", t=NT),
             ffb[:, NT * D:2 * NT * D].rearrange("p (t d) -> p t d", t=NT),
             qk[:, 7744:7744 + NT * D // 2].bitcast(BF16).rearrange("p (t d) -> p t d", t=NT)]
    near0T = qk[:, 0:7744].bitcast(BF16).rearrange("p (t n) -> p t n", t=NT)
    adjt = [work[:, 0:N], work[:, N:2 * N]]
    codet = [work[:, 2708 + k * 704:3412 + k * 704].bitcast(BF16) for k in range(2)]
    rest = [work[:, 8212 + k * D:8724 + k * D] for k in range(2)]
    with ExitStack() as ctx:
        def S(name):
            return sem(ctx, name)

        brow = ctx.enter_context(nc.sbuf_tensor("brow", [13, P], F32))
        pair = ctx.enter_context(nc.sbuf_tensor("pair", [EROWS, 2 * ECOLS], I32))
        ef = ctx.enter_context(nc.sbuf_tensor("ef", [EROWS, 2, ECOLS], F32))
        got = ctx.enter_context(nc.sbuf_tensor("got", [EROWS, ECOLS], F32))
        identb = ctx.enter_context(nc.sbuf_tensor("identb", [P, P], BF16))
        offdiag = ctx.enter_context(nc.sbuf_tensor("offdiag", [P, P], BF16))
        onesb = ctx.enter_context(nc.sbuf_tensor("onesb", [P, 1], BF16))
        minus1 = ctx.enter_context(nc.sbuf_tensor("minus1", [P, 1], F32))
        MT = [ctx.enter_context(nc.psum_tensor(f"MT{k}", [P, 2048], BF16)) for k in range(2)]
        TP = ctx.enter_context(nc.psum_tensor("TP", [P, 3, 512], F32))
        DG = ctx.enter_context(nc.psum_tensor("DG", [P, 512], F32))

        x_in, wq_in, wcat_in, a_in, mlp_in, bias_in, rel_in = (S(n) for n in (
            "x_in", "wq_in", "wcat_in", "a_in", "mlp_in", "bias_in", "rel_in"))
        adj_in = [S("adj_in0"), S("adj_in1")]
        padded, ident_set, ident_done, index_done, gathered = (S(n) for n in (
            "padded", "ident_set", "ident_done", "index_done", "gathered"))
        tp_full, tp_used, dve_chain, va_done = (S(n) for n in ("tp_full", "tp_used", "dve_chain", "va_done"))
        hi_ready, rest_ready, mid_ready, rest2_ready, lo_ready = (S(n) for n in (
            "hi_ready", "rest_ready", "mid_ready", "rest2_ready", "lo_ready"))
        code_ready, flipped, near1_ready, near0_ready, diag_off, y_full, y_used = (S(n) for n in (
            "code_ready", "flipped", "near1_ready", "near0_ready", "diag_off", "y_full", "y_used"))
        deg_ready = S("deg_ready")
        met_ready, col_full, col_ready, total_full = (S(n) for n in ("met_ready", "col_full", "col_ready", "total_full"))

        jobs = []
        for f in range(FT):
            jobs.append(("mlp", [w1n[:, t, f * P:(f + 1) * P] for t in range(2)], w1T[:, f, :]))
        for f in range(2):
            jobs.append(("mlp", [w2n[:, f * P:(f + 1) * P]], w2T[:, f, :]))
        jobs.append(("mlp", [w3n[:, t, :] for t in range(2)], w3T[:, :]))
        for f in range(2):
            jobs.append(("mlp", [w4n[:, t, f * P:(f + 1) * P] for t in range(4)], w4T[:, f, :]))
        jobs.append(("bias", [brow[:, :]], bias[:, 0:13]))
        n_mlp = len(jobs)
        for src, dst in ((qnat, qTw), (knat, kTw)):
            for f in range(FT):
                jobs.append(("wqk", [src[:, t, f * P:(f + 1) * P] for t in range(FT)], dst[:, f, :]))
        block = ctx.enter_context(nc.Block())

        @block.sync
        def _(sp):
            def load_adj(t, k, rows):
                sp.wait_ge(code_ready, t + 1)
                sp.dma_start(adjt[k][0:rows, :], adj[bass.ds(t * P, rows), :]).then_inc(adj_in[k], 16)

            sp.dma_start(qnat, v["Wq"].rearrange("(t p) f -> p t f", p=P)).then_inc(wq_in, 16)
            sp.dma_start(knat, v["Wk"].rearrange("(t p) f -> p t f", p=P)).then_inc(wq_in, 16)
            sp.wait_ge(padded, 1)
            sp.dma_start(nodes[:, 0:NFULL, :], x[0:NFULL * P, :].rearrange("(t p) f -> p t f", p=P)).then_inc(x_in, 16)
            sp.dma_start(nodes[0:LAST, NFULL, :], x[NFULL * P:N, :]).then_inc(x_in, 16)
            with sp.Fori(0, NFULL // 2) as u:
                for k in range(2):
                    load_adj(u * 2 + k, k, P)
            load_adj(NFULL, 0, LAST)

        @block.scalar
        def _(act):
            act.dma_start(pair[:, :], rel.rearrange("(p c) k -> p (c k)", p=EROWS)).then_inc(rel_in, 16)
            for k, name in enumerate(("a1", "a2")):
                act.dma_start(abc[:, k, :], v[name].rearrange("(a h) d -> a (h d)", a=1).to_broadcast([P, D])
                              ).then_inc(a_in, 16)
            act.dma_start(w1n, v["W1"].rearrange("(t p) f -> p t f", p=P)).then_inc(mlp_in, 16)
            act.dma_start(w2n, v["W2"]).then_inc(mlp_in, 16)
            act.dma_start(w3n, v["W3"].rearrange("(t p) f -> p t f", p=P)).then_inc(mlp_in, 16)
            act.dma_start(w4n, v["W4"].rearrange("(t p) f -> p t f", p=P)).then_inc(mlp_in, 16)
            act.dma_start(b4bc[:, :], v["b4"].rearrange("(a d) -> a d", a=1).to_broadcast([P, D])
                          ).then_inc(mlp_in, 16)
            for t in range(FT):
                act.dma_start(wcat[:, t, :].rearrange("p (h d) -> p h d", h=HEADS),
                              v["W"][:, t * P:(t + 1) * P, :].rearrange("h p d -> p h d")).then_inc(wcat_in, 16)
            for name, c, k in (("bq", 0, 4), ("bk", 4, 4), ("b1", 8, 2), ("b2", 10, 1), ("b3", 11, 2)):
                act.dma_start(brow[c:c + k, :], v[name].rearrange("(t p) -> t p", p=P)).then_inc(bias_in, 16)
            for n, (_, blocks, dst) in enumerate(jobs):
                act.wait_ge(tp_full, n + 1)
                nc.scalar.copy(dst, TP[:, n % 3, 0:dst.shape[-1]]).then_inc(tp_used, 1)
            act.wait_ge(x_in, 32)
            act.wait_ge(va_done, 1)
            for t in range(NT):
                nc.scalar.copy(xpart[0][:, t, :], nodes[:, t, :]).then_inc(hi_ready, 1)
                if t >= 1:
                    act.wait_ge(rest_ready, t)
                    nc.scalar.copy(xpart[1][:, t - 1, :], rest[(t - 1) % 2]).then_inc(mid_ready, 1)
            act.wait_ge(rest_ready, NT)
            nc.scalar.copy(xpart[1][:, NT - 1, :], rest[(NT - 1) % 2]).then_inc(mid_ready, 1)

            def near0(t, k):
                act.wait_ge(flipped, t + 3)
                nc.scalar.activation(near0T[:, :, bass.ds(t * P, P)],
                                     MT[k][:, 0:NP].rearrange("p (t n) -> p t n", t=NT), ACT.Relu,
                                     bias=minus1[:, :]).then_inc(near0_ready, 1)

            def keep_y(t, k):
                act.wait_ge(y_full, t + 1)
                nc.scalar.copy(x1[:, t, :], TP[:, k, :]).then_inc(y_used, 1)

            act.sem_inc(near0_ready, 2)
            act.sem_inc(y_used, 2)
            near0(0, 0)
            with act.Fori(0, NFULL // 2) as u:
                for k in range(2):
                    near0(u * 2 + (k + 1), (k + 1) % 2)
                    keep_y(u * 2 + k, k)
            keep_y(NFULL, 0)
            act.wait_ge(y_full, NT)
            nc.scalar.copy(deg0[:, :], DG[:, 0:NT]).then_inc(deg_ready, 1)

        @block.gpsimd
        def _(pool):
            nc.gpsimd.memset(ident[:, :], 0.0).then_inc(ident_set, 1)
            nc.gpsimd.memset(before[:, :], 1.0).then_inc(ident_set, 1)
            pool.wait_ge(ident_set, 2)
            nc.gpsimd.affine_select(out=ident[:, :], in_=ident[:, :], compare_op=ALU.not_equal, fill=1.0, base=0,
                                    pattern=[[-1, P]], channel_multiplier=1).then_inc(ident_done, 1)
            nc.gpsimd.affine_select(out=before[:, :], in_=before[:, :], compare_op=ALU.is_gt, fill=0.0, base=0,
                                    pattern=[[1, P]], channel_multiplier=-1).then_inc(ident_done, 1)
            pool.wait_ge(index_done, 1)
            for c in range(ECOLS):
                nc.gpsimd.indirect_dma_start(
                    out=got[:, c:c + 1], out_offset=None, in_=adj.rearrange("a (b k) -> (a b) k", k=1),
                    in_offset=bass.IndirectOffsetOnAxis(ap=eidx[:, c:c + 1].bitcast(U32), axis=0),
                    bounds_check=N * N - 1, oob_is_err=False).then_inc(gathered, 16)

        @block.vector
        def _(dve):
            links = [0]

            def link(ins):
                links[0] += 1
                ins.then_inc(dve_chain, 1)
                dve.wait_ge(dve_chain, links[0])

            nc.vector.memset(nodes[64:P, NFULL, :], 0.0).then_inc(padded, 1)
            nc.vector.memset(got[:, :], 0.0)
            nc.vector.memset(edges[:, :, 2], 1.0)
            dve.wait_ge(rel_in, 16)
            both = pair[:, :].rearrange("p (c k) -> p k c", k=2)
            for k in range(2):
                link(nc.vector.tensor_copy(edges[:, :, k], both[:, k, :]))
                link(nc.vector.tensor_scalar(ef[:, 0, :], edges[:, :, k], 0.0, float(N), ALU.is_lt, ALU.mult))
                link(nc.vector.tensor_tensor(edges[:, :, k], edges[:, :, k], ef[:, 0, :], ALU.add))
            link(nc.vector.tensor_tensor(ef[:, 0, :], edges[:, :, 0], edges[:, :, 1], ALU.not_equal))
            for k in range(2):
                for lim, op in ((0.0, ALU.is_ge), (float(N), ALU.is_lt)):
                    link(nc.vector.scalar_tensor_tensor(ef[:, 0, :], edges[:, :, k], lim, ef[:, 0, :], op, ALU.mult))
            link(nc.vector.scalar_tensor_tensor(ef[:, 1, :], edges[:, :, 0], float(N), edges[:, :, 1], ALU.mult, ALU.add))
            link(nc.vector.scalar_tensor_tensor(ef[:, 1, :], ef[:, 1, :], float(-N * N), ef[:, 0, :], ALU.add, ALU.mult))
            link(nc.vector.tensor_scalar(ef[:, 1, :], ef[:, 1, :], float(N * N), None, ALU.add))
            nc.vector.tensor_copy(eidx[:, :], ef[:, 1, :]).then_inc(index_done, 1)
            nc.vector.memset(ones[:, :], 1.0)
            nc.vector.memset(onesb[:, :], 1.0)
            nc.vector.memset(minus1[:, :], -1.0)
            link(nc.vector.memset(va[:, :, :], 0.0))
            link(nc.vector.memset(codesum[:, :], 1.0))
            for k in range(2):
                link(nc.vector.memset(codet[k], 0.0))
            dve.wait_ge(ident_done, 2)
            link(nc.vector.tensor_copy(identb[:, :], ident[:, :]))
            link(nc.vector.tensor_scalar(offdiag[:, :], ident[:, :], -1.0, 1.0, ALU.mult, ALU.add))
            dve.wait_ge(wcat_in, 64)
            dve.wait_ge(a_in, 32)
            for k in range(2):
                for t in range(FT):
                    link(nc.vector.tensor_tensor(prod, wcat[:, t, :], abc[:, k, :], ALU.mult))
                    link(nc.vector.tensor_reduce(va[:, t, k * 32:k * 32 + HEADS],
                                                 prod.rearrange("p (h d) -> p h d", h=HEADS), AX_X, ALU.add))
            dve.wait_ge(tp_used, n_mlp)
            dve.sem_inc(va_done, 1)
            for t in range(NT + 1):
                if t < NT:
                    dve.wait_ge(hi_ready, t + 1)
                    if t >= 2:
                        dve.wait_ge(lo_ready, t - 1)
                    nc.vector.tensor_tensor(rest[t % 2], nodes[:, t, :], xpart[0][:, t, :], ALU.subtract
                                            ).then_inc(rest_ready, 1)
                if t >= 1:
                    dve.wait_ge(mid_ready, t)
                    nc.vector.tensor_tensor(xpart[2][:, t - 1, :], rest[(t - 1) % 2], xpart[1][:, t - 1, :],
                                            ALU.subtract).then_inc(lo_ready, 1)

            base = links[0]

            def mask_code(t, k, rows, n):
                dve.wait_ge(adj_in[k], n)
                dve.wait_ge(flipped, t + 1)
                c = codet[k][0:rows, 0:N]
                nc.vector.tensor_scalar(c, adjt[k][0:rows, :], 1.0, None, ALU.is_equal).then_inc(dve_chain, 1)
                dve.wait_ge(dve_chain, t + (base + 1))
                nc.vector.scalar_tensor_tensor(c, adjt[k][0:rows, :], 0.0, c, ALU.is_gt, ALU.add,
                                               accum_out=codesum[0:rows, bass.ds(t, 1)]).then_inc(code_ready, 1)

            def near1(t, k):
                dve.wait_ge(near0_ready, t + 3)
                nc.vector.tensor_scalar(near1T[:, :, bass.ds(t * P, P)],
                                        MT[k][:, 0:NP].rearrange("p (t n) -> p t n", t=NT), 1.0, None, ALU.min
                                        ).then_inc(near1_ready, 1)
                d = near0T[:, bass.ds(t, 1), bass.ds(t * P, P)].rearrange("p a n -> p (a n)")
                nc.vector.tensor_tensor(d, d, offdiag[:, :], ALU.mult).then_inc(diag_off, 1)

            dve.sem_inc(code_ready, 2)
            dve.sem_inc(near1_ready, 2)
            mask_code(0, 0, P, 16)
            with dve.Fori(0, NFULL // 2 - 1) as u:
                for k in range(2):
                    mask_code(u * 2 + (k + 1), (k + 1) % 2, P, u * 16 + 16 * (k + 1))
                    near1(u * 2 + k, k)
            t = NFULL - 1
            mask_code(t, t % 2, P, 16 * (t // 2 + 1))
            near1(t - 1, (t - 1) % 2)
            dve.wait_ge(flipped, NFULL + 1)
            nc.vector.memset(codet[0][64:P, :], 0.0).then_inc(padded, 1)
            dve.wait_ge(padded, 2)
            mask_code(NFULL, 0, LAST, 16 * (NFULL // 2 + 1))
            near1(NFULL - 1, 1)
            near1(NFULL, 0)
            dve.wait_ge(near1_ready, NT + 2)
            nc.vector.memset(near1T[:, 0, N:NP], 1.0)
            dve.wait_ge(gathered, 16 * ECOLS)
            nc.vector.tensor_scalar(met[:, :], got[:, :], 1.0, None, ALU.is_equal).then_inc(met_ready, 1)
            dve.wait_ge(col_full, 1)
            nc.vector.tensor_copy(colsum[:, :], DG[0:ECOLS, 16:17]).then_inc(col_ready, 1)
            dve.wait_ge(total_full, 1)
            nc.vector.tensor_scalar(flags[0:1, 0:1], DG[0:1, 17:18], float(SLOTS), None, ALU.is_le)

        @block.tensor
        def _(pe):
            pe.wait_ge(ident_done, 1)
            waits = {"wqk": (wq_in, 32), "mlp": (mlp_in, 80), "bias": (bias_in, 80)}
            for n, (kind, blocks, dst) in enumerate(jobs):
                pe.wait_ge(*waits[kind])
                if n >= 3:
                    pe.wait_ge(tp_used, n - 2)
                for k, b in enumerate(blocks):
                    r = b.shape[0]
                    last = nc.tensor.transpose(TP[:, n % 3, k * P:k * P + r], b, ident[0:r, 0:r])
                last.then_inc(tp_full, 1)
            pe.wait_ge(tp_used, len(jobs))
            pe.wait_ge(lo_ready, NT)

            def flip(t, k):
                pe.wait_ge(code_ready, t + 3)
                pe.wait_ge(near1_ready, t + 1)
                pe.wait_ge(near0_ready, t + 1)
                for j in range(NT):
                    last = nc.tensor.transpose(MT[k][:, j * P:(j + 1) * P], codet[k][:, j * P:(j + 1) * P], identb[:, :])
                last.then_inc(flipped, 1)

            def mix(t, k):
                pe.wait_ge(diag_off, t + 1)
                pe.wait_ge(y_used, t + 1)
                for j in range(NT):
                    rows = near0T[:, j, bass.ds(t * P, P)]
                    nc.tensor.matmul(DG[:, bass.ds(t, 1)], rows, onesb[:, :], start=(j == 0), stop=(j == NT - 1),
                                     skip_group_check=True)
                    for n in range(3):
                        last = nc.tensor.matmul(TP[:, k, :], rows, xpart[n][:, j, :],
                                                start=(j == 0 and n == 0), stop=(j == NT - 1 and n == 2))
                last.then_inc(y_full, 1)

            pe.sem_inc(flipped, 2)
            flip(0, 0)
            with pe.Fori(0, NFULL // 2) as u:
                for k in range(2):
                    flip(u * 2 + (k + 1), (k + 1) % 2)
                    mix(u * 2 + k, k)
            mix(NFULL, 0)
            pe.wait_ge(met_ready, 1)
            pe.wait_ge(deg_ready, 1)
            nc.tensor.matmul(DG[0:ECOLS, 16:17], met[:, :], ones[0:EROWS, 0:1], start=True, stop=True
                             ).then_inc(col_full, 1)
            pe.wait_ge(col_ready, 1)
            nc.tensor.matmul(DG[0:1, 17:18], colsum[:, :], ones[0:ECOLS, 0:1], start=True, stop=True
                             ).then_inc(total_full, 1)


def dense_prep(nc, sem, v, layer):
    x, adj, adj_dram, edge_dram = v["x"], v["adj"], v["adj_dram"], v["edge_dram"]
    nodes, featT, x1, qk4, ident, bias, qTw, kTw = (v[k] for k in (
        "nodes", "featT", "x1", "qk4", "ident", "bias", "qTw", "kTw"))
    zeros = v["x1"][:, 0:3, :].rearrange("p t d -> p (t d)")[:, 0:N] if layer == 0 else v["work"][:, 0:N]
    with ExitStack() as ctx:
        def S(name):
            return sem(ctx, f"dp{layer}_" + name)
        TP = ctx.enter_context(nc.psum_tensor(f"TPd{layer}", [P, 3, 512], F32))
        QP = ctx.enter_context(nc.psum_tensor(f"QPd{layer}", [P, 2, 512], F32))
        copied, zero_done, padded, zeroed, scattered, tp_full, tp_used, qp_full, qp_used = (S(n) for n in (
            "copied", "zero_done", "padded", "zeroed", "scattered", "tp_full", "tp_used", "qp_full", "qp_used"))
        jobs = [(f, t0, k) for f in range(FT) for t0, k in TG] if layer == 0 else []
        qkjobs = [(a, o, c, w) for a in range(2) for o in range(FT) for c, w in ((0, 512), (512, 512), (1024, 384))
                  ] if layer == 0 else []
        block = ctx.enter_context(nc.Block())

        @block.sync
        def _(sp):
            sp.dma_start(adj_dram[0:N, :], adj).then_inc(copied, 16)
            sp.wait_ge(zero_done, 1)
            sp.dma_start(adj_dram[N:NP, :], zeros[0:NP - N, :]).then_inc(padded, 16)
            if layer == 0:
                for t in range(NT):
                    sp.dma_start(edge_dram[t * P:(t + 1) * P, :], zeros).then_inc(zeroed, 16)
            sp.wait_ge(copied, 16)
            sp.wait_ge(padded, 16)

        @block.vector
        def _(dve):
            nc.vector.memset(zeros, 0.0).then_inc(zero_done, 1)

        @block.gpsimd
        def _(pool):
            if layer == 0:
                pool.wait_ge(zeroed, 16 * NT)
                for c in range(ECOLS):
                    if c:
                        pool.wait_ge(scattered, 16 * c)
                    nc.gpsimd.indirect_dma_start(
                        out=edge_dram.rearrange("a (b k) -> (a b) k", k=1),
                        out_offset=bass.IndirectOffsetOnAxis(ap=v["eidx"][:, c:c + 1].bitcast(U32), axis=0),
                        in_=v["ones"][0:EROWS, 0:1], in_offset=None, bounds_check=N * N - 1, oob_is_err=False
                    ).then_inc(scattered, 16)
                pool.wait_ge(scattered, 16 * ECOLS)

        @block.scalar
        def _(act):
            for n, (f, t0, k) in enumerate(jobs):
                act.wait_ge(tp_full, n + 1)
                nc.scalar.copy(featT[:, f, t0 * P:(t0 + k) * P], TP[:, n % 3, 0:k * P]).then_inc(tp_used, 1)
            for n, (a, o, c, w) in enumerate(qkjobs):
                act.wait_ge(qp_full, n + 1)
                nc.scalar.activation(qk4[:, a, o, c:c + w], QP[:, n % 2, 0:w], ACT.Identity,
                                     bias=bias[:, 4 * a + o:4 * a + o + 1]).then_inc(qp_used, 1)

        @block.tensor
        def _(pe):
            for n, (f, t0, k) in enumerate(jobs):
                if n >= 3:
                    pe.wait_ge(tp_used, n - 2)
                for j in range(k):
                    last = nc.tensor.transpose(TP[:, n % 3, j * P:(j + 1) * P], nodes[:, t0 + j, f * P:(f + 1) * P],
                                               ident[:, :])
                last.then_inc(tp_full, 1)
            if jobs:
                pe.wait_ge(tp_used, len(jobs))
            for n, (a, o, c, w) in enumerate(qkjobs):
                if n >= 2:
                    pe.wait_ge(qp_used, n - 1)
                for f in range(FT):
                    last = nc.tensor.matmul(QP[:, n % 2, 0:w], (qTw, kTw)[a][:, f, o * P:(o + 1) * P],
                                            featT[:, f, c:c + w], start=(f == 0), stop=(f == FT - 1))
                last.then_inc(qp_full, 1)


def layer0_sparse(nc, sem, v):
    nodes, featT, x1, qk, work, ident, before, ones, deg0, edges, met, colsum = (v[k] for k in (
        "nodes", "featT", "x1", "qk", "work", "ident", "before", "ones", "deg0", "edges", "met", "colsum"))
    qTw, kTw = v["qTw"], v["kTw"]
    o = 0

    def cut(w):
        nonlocal o
        o += w
        assert o <= 2 * FT * NP
        return qk[:, o - w:o]

    CC = 16
    onehot = [cut(CC * P)[0:EROWS, :].rearrange("p (c s) -> p c s", c=CC) for _ in range(2)]
    hot, iota = cut(NP), cut(NP)
    adjrow = cut(N)
    xs, xo = cut(D), cut(D)
    xsT, xoT = (featT[:, k, 0:D].rearrange("p (f s) -> p f s", f=FT) for k in range(2))
    bqbc, bkbc = featT[:, 2, 0:D], featT[:, 3, 0:D]
    prod = featT[:, 0, D:2 * D]
    gains = featT[:, 1, D:2 * D]
    t8 = work[:, 0:1024].rearrange("p (h s) -> p h s", h=HEADS)
    d8 = work[:, 1024:2048].rearrange("p (h s) -> p h s", h=HEADS)
    same, penal, keq, ub = (work[:, 2048 + k * P:2048 + (k + 1) * P] for k in range(4))
    c = work[:, 2560:2960]
    sub, obj, used, key, dup, uniq, rep, cnt, deg = (c[:, k:k + 1] for k in range(9))
    w3 = c[:, 16:19]
    att, top, zsum, den, wgt = (c[:, 24 + 8 * k:32 + 8 * k] for k in range(5))
    ex3 = c[:, 64:88].rearrange("p (k h) -> p k h", k=3)
    fsum = c[:, 88:112].rearrange("p (k h) -> p k h", k=3)
    f3 = c[:, 112:115]
    gain = c[:, 115:116]
    rowv = c[:, 120:120 + 3 * NT].rearrange("p (t k) -> p t k", k=3)
    fdef, ddef, plain = (c[:, 160 + NT * k:160 + NT * (k + 1)] for k in range(3))
    with ExitStack() as ctx:
        def S(name):
            return sem(ctx, "s_" + name)
        place = ctx.enter_context(nc.sbuf_tensor("place", [EROWS, ECOLS], F32))
        slotidx = ctx.enter_context(nc.sbuf_tensor("slotidx", [P, 2], I32))
        PA = ctx.enter_context(nc.psum_tensor("PA", [P, 512], F32))
        PB = ctx.enter_context(nc.psum_tensor("PB", [P, 512], F32))
        PT = ctx.enter_context(nc.psum_tensor("PTs", [P, 2, 512], F32))
        PQ = ctx.enter_context(nc.psum_tensor("PQ", [P, 2, 512], F32))
        PC = ctx.enter_context(nc.psum_tensor("PCs", [P, 2, 512], F32))
        (colb_ready, place_full, hot_ready, hot_used, slot_full, idx_ready, rows_in, adj_in, bias_in, iota_ready,
         diag_ready, bc_full, uniq_ready, ub_full, xt_full, xt_ready, proj_full, d8_ready, att_full, args_ready,
         exp_ready, gain_ready, corr_full, corr_used, chain) = (S(n) for n in (
            "colb_ready", "place_full", "hot_ready", "hot_used", "slot_full", "idx_ready", "rows_in", "adj_in",
            "bias_in", "iota_ready", "diag_ready", "bc_full", "uniq_ready", "ub_full", "xt_full", "xt_ready",
            "proj_full", "d8_ready", "att_full", "args_ready", "exp_ready", "gain_ready", "corr_full", "corr_used",
            "chain"))
        colb = work[0:ECOLS, 2960:2960 + EROWS]
        block = ctx.enter_context(nc.Block())

        @block.sync
        def _(sp):
            for name, dst in (("bq", bqbc), ("bk", bkbc)):
                sp.dma_start(dst, v[name].rearrange("(a d) -> a d", a=1).to_broadcast([P, D])).then_inc(bias_in, 16)

        @block.gpsimd
        def _(pool):
            nc.gpsimd.iota(iota, pattern=[[1, NP]], base=0, channel_multiplier=0,
                           allow_small_or_imprecise_dtypes=True).then_inc(iota_ready, 1)
            pool.wait_ge(idx_ready, 1)
            for k, dst in enumerate((xs, xo)):
                nc.gpsimd.indirect_dma_start(
                    out=dst, out_offset=None, in_=v["x"], in_offset=bass.IndirectOffsetOnAxis(
                        ap=slotidx[:, k:k + 1].bitcast(U32), axis=0),
                    bounds_check=N - 1, oob_is_err=False).then_inc(rows_in, 16)
            nc.gpsimd.indirect_dma_start(
                out=adjrow, out_offset=None, in_=v["adj"], in_offset=bass.IndirectOffsetOnAxis(
                    ap=slotidx[:, 0:1].bitcast(U32), axis=0),
                bounds_check=N - 1, oob_is_err=False).then_inc(adj_in, 16)

        @block.scalar
        def _(act):
            act.wait_ge(xt_full, 1)
            nc.scalar.copy(xsT.rearrange("p f s -> p (f s)"), PT[:, 0, :])
            act.wait_ge(xt_full, 2)
            nc.scalar.copy(xoT.rearrange("p f s -> p (f s)"), PT[:, 1, :]).then_inc(xt_ready, 1)
            act.wait_ge(args_ready, 1)
            nc.scalar.activation(t8, t8, ACT.Exp)
            nc.scalar.activation(ex3, ex3, ACT.Exp).then_inc(exp_ready, 1)

        @block.tensor
        def _(pe):
            pe.wait_ge(colb_ready, 1)
            nc.tensor.matmul(PA[0:EROWS, 0:ECOLS], before[0:EROWS, 0:EROWS], met[:, :], start=True, stop=False)
            nc.tensor.matmul(PA[0:EROWS, 0:ECOLS], colb, before[0:ECOLS, 0:ECOLS], start=False, stop=True
                             ).then_inc(place_full, 1)
            for n in range(ECOLS // CC):
                pe.wait_ge(hot_ready, n + 1)
                for k in range(CC):
                    e = n * CC + k
                    last = nc.tensor.matmul(PB[:, 0:3], onehot[n % 2][:, k, :], edges[:, e, :], start=(e == 0),
                                            stop=(e == ECOLS - 1))
                last.then_inc(hot_used, 1)
            pe.wait_ge(diag_ready, 1)
            nc.tensor.matmul(PA[:, 0:2 * P], ones[:, :], d8[:, 0:2, :].rearrange("p h s -> p (h s)"), start=True,
                             stop=True).then_inc(bc_full, 1)
            pe.wait_ge(uniq_ready, 1)
            nc.tensor.matmul(PB[:, 0:P], ones[:, :], d8[:, 2, :], start=True, stop=True).then_inc(ub_full, 1)
            pe.wait_ge(rows_in, 32)
            for k, src in enumerate((xs, xo)):
                for f in range(FT):
                    last = nc.tensor.transpose(PT[:, k, f * P:(f + 1) * P], src[:, f * P:(f + 1) * P], ident[:, :])
                last.then_inc(xt_full, 1)
            pe.wait_ge(xt_ready, 1)
            for k, (l, w) in enumerate(((xsT, qTw), (xoT, kTw))):
                for f in range(FT):
                    last = nc.tensor.matmul(PQ[:, k, :], l[:, f, :], w[:, f, :], start=(f == 0), stop=(f == FT - 1))
                last.then_inc(proj_full, 1)
            pe.wait_ge(d8_ready, 1)
            d8f = d8.rearrange("p h s -> p (h s)")
            for k in range(2):
                last = nc.tensor.matmul(PC[:, k, :], ones[:, :], d8f[:, k * 512:(k + 1) * 512], start=True, stop=True)
            last.then_inc(att_full, 1)
            pe.wait_ge(gain_ready, 1)
            for t in range(NT):
                last = nc.tensor.matmul(PA[:, 3 * t:3 * t + 3], hot[:, t * P:(t + 1) * P], w3, start=True, stop=True)
            last.then_inc(corr_full, 1)
            for t in range(NT):
                if t >= 2:
                    pe.wait_ge(corr_used, t - 1)
                nc.tensor.matmul(PT[:, t % 2, :], hot[:, t * P:(t + 1) * P], gains, start=True, stop=True
                                 ).then_inc(corr_full, 1)

        @block.vector
        def _(dve):
            links = [0]

            def link(ins):
                links[0] += 1
                ins.then_inc(chain, 1)
                dve.wait_ge(chain, links[0])

            TT, TS, STT = nc.vector.tensor_tensor, nc.vector.tensor_scalar, nc.vector.scalar_tensor_tensor
            TS(colb, ones[0:ECOLS, 0:EROWS], colsum[:, 0:1], None, ALU.mult).then_inc(colb_ready, 1)
            dve.wait_ge(place_full, 1)
            link(STT(place[:, :], PA[0:EROWS, 0:ECOLS], 1.0, met[:, :], ALU.add, ALU.mult))
            link(TS(place[:, :], place[:, :], -1.0, None, ALU.add))
            dve.wait_ge(iota_ready, 1)
            nums = iota[0:EROWS, 0:P].rearrange("p (c s) -> p c s", c=1).to_broadcast([EROWS, CC, P])
            for n in range(ECOLS // CC):
                if n >= 2:
                    dve.wait_ge(hot_used, n - 1)
                at = place[:, n * CC:(n + 1) * CC].rearrange("p (c s) -> p c s", s=1).to_broadcast([EROWS, CC, P])
                TT(onehot[n % 2], nums, at, ALU.is_equal).then_inc(hot_ready, 1)
            dve.wait_ge(hot_used, ECOLS // CC)
            nc.vector.tensor_copy(slotidx[:, :], PB[:, 0:2]).then_inc(idx_ready, 1)
            link(nc.vector.tensor_copy(c[:, 0:3], PB[:, 0:3]))
            link(STT(key, sub, float(N), obj, ALU.mult, ALU.add))
            link(TS(d8[:, 0, :], ident[:, :], key, None, ALU.mult))
            TS(d8[:, 1, :], ident[:, :], sub, None, ALU.mult).then_inc(diag_ready, 1)
            link(TS(hot, iota, sub, None, ALU.is_equal))
            dve.wait_ge(bc_full, 1)
            link(TT(ub, before[:, :], ident[:, :], ALU.add))
            link(TS(ub, ub, -1.0, 1.0, ALU.mult, ALU.add))
            link(STT(keq, PA[:, 0:P], key, ub, ALU.is_equal, ALU.mult))
            link(nc.vector.tensor_reduce(dup, keq, AX_X, ALU.max))
            link(TS(uniq, dup, 0.5, used, ALU.is_lt, ALU.mult))
            TS(d8[:, 2, :], ident[:, :], uniq, None, ALU.mult).then_inc(uniq_ready, 1)
            dve.wait_ge(ub_full, 1)
            link(nc.vector.tensor_copy(penal, PB[:, 0:P]))
            link(STT(same, PA[:, P:2 * P], sub, penal, ALU.is_equal, ALU.mult))
            link(TT(keq, same, ub, ALU.mult))
            link(nc.vector.tensor_reduce(dup, keq, AX_X, ALU.max))
            link(TS(rep, dup, 0.5, uniq, ALU.is_lt, ALU.mult))
            link(nc.vector.tensor_reduce(cnt, same, AX_X, ALU.add))
            link(TS(penal, same, -1.0, BIG, ALU.add, ALU.mult))
            dve.wait_ge(adj_in, 16)
            link(TS(adjrow, adjrow, 1.0, None, ALU.is_equal))
            link(STT(adjrow, hot[:, 0:N], 0.5, adjrow, ALU.is_lt, ALU.mult, accum_out=deg))
            dve.wait_ge(bias_in, 32)
            dve.wait_ge(proj_full, 2)
            link(TT(bqbc, PQ[:, 0, :], bqbc, ALU.add))
            link(TT(bkbc, PQ[:, 1, :], bkbc, ALU.add))
            link(TT(prod, bqbc, bkbc, ALU.mult))
            link(nc.vector.tensor_reduce(att, prod.rearrange("p (h d) -> p h d", h=HEADS), AX_X, ALU.add))
            link(TS(att, att, DK ** -0.5, uniq, ALU.mult, ALU.mult))
            wide = lambda a: a.rearrange("p (h s) -> p h s", h=1).to_broadcast([P, HEADS, P])
            deep = lambda a: a.rearrange("p (h s) -> p h s", s=1).to_broadcast([P, HEADS, P])
            TT(d8, wide(ident[:, :]), deep(att), ALU.mult).then_inc(d8_ready, 1)
            dve.wait_ge(att_full, 1)
            pc = PC[:, :, :].rearrange("p b (h s) -> p (b h) s", h=HEADS // 2)
            link(TT(t8, pc, wide(same), ALU.mult))
            link(TT(t8, t8, wide(penal), ALU.add))
            link(nc.vector.tensor_reduce(top, t8, AX_X, ALU.max))
            link(TS(top, top, 1.0e-7, None, ALU.max))
            link(TT(t8, t8, deep(top), ALU.subtract))
            link(TT(ex3[:, 0, :], att, top, ALU.subtract))
            link(TS(ex3[:, 1, :], top, -1.0, None, ALU.mult))
            TS(ex3[:, 2, :], top, -1.0, 1.0e-7, ALU.mult, ALU.add).then_inc(args_ready, 1)
            dve.wait_ge(exp_ready, 1)
            link(nc.vector.tensor_reduce(zsum, t8, AX_X, ALU.add))
            link(TT(deg, deg, cnt, ALU.subtract))
            link(TT(zsum, zsum, ex3[:, 2, :], ALU.add))
            link(STT(den, ex3[:, 1, :], deg, zsum, ALU.mult, ALU.add))
            link(nc.vector.reciprocal(den, den))
            link(TS(den, den, 1.0 / HEADS, None, ALU.mult))
            link(TT(fsum, ex3, den.rearrange("p (k h) -> p k h", k=1).to_broadcast([P, 3, HEADS]), ALU.mult))
            link(nc.vector.tensor_reduce(f3, fsum, AX_X, ALU.add))
            link(TS(w3[:, 1:3], f3[:, 1:3], rep, None, ALU.mult))
            link(nc.vector.tensor_copy(w3[:, 0:1], rep))
            link(TT(gain, f3[:, 0:1], f3[:, 1:2], ALU.subtract))
            link(TT(gain, gain, uniq, ALU.mult))
            TS(gains, xo, gain, None, ALU.mult).then_inc(gain_ready, 1)
            W0 = 1.0 - 2.0 ** -23
            link(TS(ddef, deg0[:, :], W0, 1.0, ALU.mult, ALU.add))
            link(nc.vector.reciprocal(ddef, ddef))
            link(TS(fdef, ddef, W0, None, ALU.mult))
            dve.wait_ge(corr_full, 1)
            link(nc.vector.tensor_copy(rowv, PA[:, 0:3 * NT].rearrange("p (t k) -> p t k", k=3)))
            link(TS(plain, rowv[:, :, 0], -1.0, 1.0, ALU.mult, ALU.add))
            link(TT(fdef, fdef, plain, ALU.mult))
            link(TT(fdef, fdef, rowv[:, :, 1], ALU.add))
            link(TT(ddef, ddef, plain, ALU.mult))
            link(TT(ddef, ddef, rowv[:, :, 2], ALU.add))
            link(TS(ddef, ddef, 1.0, None, ALU.add))
            for t in range(NT):
                dve.wait_ge(corr_full, t + 2)
                STT(x1[:, t, :], x1[:, t, :], fdef[:, t:t + 1], PT[:, t % 2, :], ALU.mult, ALU.add
                    ).then_inc(corr_used, 1)
                dve.wait_ge(corr_used, t + 1)
                STT(x1[:, t, :], nodes[:, t, :], ddef[:, t:t + 1], x1[:, t, :], ALU.mult, ALU.add)


def layer0_dense(nc, sem, v):
    nodes, x1, qk, ident, work, small, featT = (v[k] for k in (
        "nodes", "x1", "qk4", "ident", "work", "small", "featT"))
    spare = featT[:, :, :].rearrange("p f n -> p (f n)")
    edge_dram = v["edge_dram"]
    o = 0
    def cut(w):
        nonlocal o
        o += w
        return work[:, o - w:o]
    T = [cut(N), cut(N)]
    mask, acc, adjt = spare[:, 0:NP], spare[:, NP:2 * NP], spare[:, 2 * NP:2 * NP + N]
    edge = cut(N)
    qs = cut(FT * P).rearrange("p (f n) -> p f n", f=FT)
    factT = cut(NP)
    with ExitStack() as ctx:
        def S(name):
            return sem(ctx, "l0_" + name)
        SP_ = [ctx.enter_context(nc.psum_tensor(f"S{k}", [P, 3, 512], F32)) for k in range(2)]
        Y = ctx.enter_context(nc.psum_tensor("Y", [P, D], F32))
        Sf = [s[:, :, :].rearrange("p b n -> p (b n)") for s in SP_]
        edge_in, q_staged, scores, masked, top, prob, accd, transposed, copied, summed, done, mask_ready, chain = (
            S(n) for n in ("edge_in", "q_staged", "scores", "masked", "top", "prob", "accd", "transposed", "copied",
                           "summed", "done", "mask_ready", "chain"))
        nmax, den, rden = small[:, 0:8], small[:, 8:16], small[:, 16:24]
        block = ctx.enter_context(nc.Block())

        @block.sync
        def _(sp):
            with sp.Fori(0, NT) as t:
                sp.wait_ge(done, t + 1)
                sp.dma_start(edge, edge_dram[bass.ts(t, P), :]).then_inc(edge_in, 16)
                sp.dma_start(adjt, v["adj_dram"][bass.ts(t, P), :]).then_inc(edge_in, 16)

        @block.scalar
        def _(act):
            act.sem_inc(copied, 1)
            with act.Fori(0, NT) as t:
                act.wait_ge(summed, t + 1)
                nc.scalar.activation(qs, qk[:, 0, :, bass.ts(t, P)], ACT.Copy, scale=DK ** -0.5).then_inc(q_staged, 1)
                for h in range(HEADS):
                    act.wait_ge(top, t * HEADS + (h + 1))
                    nc.scalar.activation(T[h % 2], T[h % 2], ACT.Exp, bias=nmax[:, h:h + 1],
                                         accum_out=den[:, h:h + 1]).then_inc(prob, 1)
                act.wait_ge(transposed, t + 1)
                nc.scalar.copy(factT, Sf[0][:, 0:NP]).then_inc(copied, 1)

        @block.tensor
        def _(pe):
            pe.sem_inc(summed, 1)
            with pe.Fori(0, NT) as t:
                pe.wait_ge(q_staged, t + 1)
                pe.wait_ge(copied, t + 1)
                for h in range(HEADS):
                    if h >= 2:
                        pe.wait_ge(masked, t * HEADS + (h - 1))
                    r = DK * (h % 2)
                    for c, w in CH:
                        last = nc.tensor.matmul(Sf[h % 2][:, c:c + w], qs[r:r + DK, h // 2, :],
                                                qk[r:r + DK, 1, h // 2, c:c + w], start=True, stop=True)
                    last.then_inc(scores, 1)
                pe.wait_ge(accd, t + 1)
                for k in range(NT):
                    last = nc.tensor.transpose(Sf[0][:, k * P:(k + 1) * P], acc[:, k * P:(k + 1) * P], ident[:, :])
                last.then_inc(transposed, 1)
                pe.wait_ge(copied, t + 2)
                pe.wait_ge(done, t + 1)
                for k in range(NT):
                    last = nc.tensor.matmul(Y[:, :], factT[:, k * P:(k + 1) * P], nodes[:, k, :],
                                            start=(k == 0), stop=(k == NT - 1))
                last.then_inc(summed, 1)

        @block.vector
        def _(dve):
            LINKS = 3 + 3 * HEADS - 1
            nc.vector.memset(acc[:, N:NP], 0.0)
            nc.vector.memset(mask[:, N:NP], 0.0)
            dve.sem_inc(done, 1)
            with dve.Fori(0, NT) as t:
                links = [0]

                def link(ins):
                    links[0] += 1
                    ins.then_inc(chain, 1)
                    dve.wait_ge(chain, t * LINKS + links[0])

                dve.wait_ge(edge_in, (t + 1) * 32)
                link(nc.vector.tensor_scalar(mask[:, 0:N], adjt, 1.0, -BIG, ALU.not_equal, ALU.mult))
                dg = mask[:, bass.ts(t, P)]
                link(nc.vector.scalar_tensor_tensor(dg, ident[:, :], 1.0, dg, ALU.not_equal, ALU.mult))
                link(nc.vector.scalar_tensor_tensor(dg, ident[:, :], 1.0e-7, dg, ALU.mult, ALU.add))
                for h in range(HEADS + 1):
                    if h < HEADS:
                        dve.wait_ge(scores, t * HEADS + (h + 1))
                        nc.vector.tensor_tensor(T[h % 2], Sf[h % 2][:, 0:N], edge, ALU.mult).then_inc(masked, 1)
                        dve.wait_ge(masked, t * HEADS + (h + 1))
                        link(nc.vector.tensor_tensor(T[h % 2], T[h % 2], mask[:, 0:N], ALU.add))
                        nc.vector.tensor_reduce(nmax[:, h:h + 1], T[h % 2], AX_X, ALU.max, negate=True).then_inc(top, 1)
                    if h >= 1:
                        g = h - 1
                        dve.wait_ge(prob, t * HEADS + h)
                        link(nc.vector.reciprocal(rden[:, g:g + 1], den[:, g:g + 1]))
                        if g == 0:
                            link(nc.vector.tensor_scalar(acc[:, 0:N], T[0], rden[:, 0:1], None, ALU.mult))
                        elif g < HEADS - 1:
                            link(nc.vector.scalar_tensor_tensor(acc[:, 0:N], T[g % 2], rden[:, g:g + 1], acc[:, 0:N],
                                                                ALU.mult, ALU.add))
                        else:
                            nc.vector.scalar_tensor_tensor(acc[:, 0:N], T[g % 2], rden[:, g:g + 1], acc[:, 0:N],
                                                           ALU.mult, ALU.add).then_inc(accd, 1)
                dve.wait_ge(summed, t + 2)
                nc.vector.scalar_tensor_tensor(x1[:, t, :], Y[:, :], 1.0 / HEADS, nodes[:, t, :],
                                               ALU.mult, ALU.add).then_inc(done, 1)
                assert links[0] == LINKS


def between(nc, sem, v):
    x1, featT, wcat, va, stat, esd, ident, work, small, ones, codesum, flags = (v[k] for k in (
        "x1", "featT", "wcat", "va", "stat", "esd", "ident", "work", "small", "ones", "codesum", "flags"))
    wh, sd_dram = v["wh"], v["sd_dram"]
    with ExitStack() as ctx:
        def S(name):
            return sem(ctx, "b_" + name)
        TP = ctx.enter_context(nc.psum_tensor("TPb", [P, 2, 512], F32))
        WP = ctx.enter_context(nc.psum_tensor("WP", [P, 2, 512], F32))
        EP = ctx.enter_context(nc.psum_tensor("EP", [P, 2, 512], F32))
        RP = ctx.enter_context(nc.psum_tensor("RP", [P, 512], F32))
        sd = work[0:40, 0:N]
        dst = work[32:40, 0:N]
        ext = work[32:40, 1408:1424]
        mid = work[32:40, 1424:1432]
        lone = work[:, 1440:1440 + NT]
        lones = work[:, 1460:1461]
        cnt = work[0:1, 1464:1466]
        stats = work[:, 1500:1500 + 6 * NT].rearrange("p (t k) -> p t k", k=6)
        (var_ready, dev_ready, normed, tp_full, tp_used, wh_full, wh_used, e_full, e_used, vec_out, chain, mid_ready,
         ref_full) = (S(n) for n in ("var_ready", "dev_ready", "normed", "tp_full", "tp_used", "wh_full", "wh_used",
                                     "e_full", "e_used", "vec_out", "chain", "mid_ready", "ref_full"))
        tjobs = [(t0, k, f) for t0, k in TG for f in range(FT)]
        block = ctx.enter_context(nc.Block())

        @block.scalar
        def _(act):
            act.wait_ge(var_ready, 1)
            nc.scalar.activation(stat[:, 2, :], stat[:, 1, :], ACT.Sqrt).then_inc(dev_ready, 1)
            for n, (t0, k, f) in enumerate(tjobs):
                act.wait_ge(tp_full, n + 1)
                nc.scalar.copy(featT[:, f, t0 * P:(t0 + k) * P], TP[:, n % 2, 0:k * P]).then_inc(tp_used, 1)
            for n, (c, w) in enumerate(CH):
                act.wait_ge(e_full, n + 1)
                nc.scalar.copy(sd[:, c:c + w], EP[0:40, n % 2, 0:w]).then_inc(e_used, 1)
            act.wait_ge(e_used, len(CH))
            act.dma_start(sd_dram[0:HEADS, :], sd[0:HEADS, :]).then_inc(vec_out, 16)
            act.dma_start(sd_dram[HEADS:2 * HEADS, :], dst).then_inc(vec_out, 16)
            for t in range(NT):
                act.wait_ge(wh_full, t + 1)
                nc.scalar.copy(wh[:, t, :], WP[:, t % 2, :])
                nc.scalar.copy(esd[:, t, :].rearrange("p (a h) -> p a h", a=2),
                               EP[:, t % 2, 0:64].rearrange("p (a h) -> p a h", a=2)[:, :, 0:HEADS]
                               ).then_inc(wh_used, 1)
            act.wait_ge(vec_out, 32)

        @block.vector
        def _(dve):
            links = [0]

            def link(ins):
                links[0] += 1
                ins.then_inc(chain, 1)
                dve.wait_ge(chain, links[0])

            for t in range(NT):
                link(nc.vector.bn_stats(stats[:, t, :], x1[:, t, :]))
                link(nc.vector.bn_aggr(stat[:, 0:2, t], stats[:, t, :]))
            layer_norm_scale(nc, dve, link, stat, var_ready, dev_ready, small[:, 0:NT])
            for t in range(NT):
                nc.vector.tensor_scalar(x1[:, t, :], x1[:, t, :], stat[:, 0, t:t + 1], stat[:, 3, t:t + 1],
                                        ALU.subtract, ALU.mult).then_inc(normed, 1)
            dve.wait_ge(e_used, len(CH))
            link(nc.vector.tensor_reduce(ext[:, 0:1], dst, AX_X, ALU.max))
            link(nc.vector.tensor_reduce(ext[:, 1:2], dst, AX_X, ALU.min))
            link(nc.vector.tensor_tensor(ext[:, 3:4], ext[:, 0:1], ext[:, 1:2], ALU.subtract))
            link(nc.vector.tensor_scalar(ext[:, 2:3], ext[:, 3:4], -0.5, ext[:, 0:1], ALU.mult, ALU.add))
            link(nc.vector.tensor_scalar(ext[:, 4:5], ext[:, 3:4], SPREAD, None, ALU.is_le))
            link(nc.vector.tensor_scalar(lone, codesum[:, :], 0.0, None, ALU.is_le))
            link(nc.vector.tensor_reduce(lones, lone, AX_X, ALU.add))
            nc.vector.tensor_scalar(mid, ident[32:40, 32:40], ext[:, 2:3], None, ALU.mult).then_inc(mid_ready, 1)
            dve.wait_ge(ref_full, 1)
            nc.vector.tensor_copy(small[:, 24:32], RP[:, 0:8])
            link(nc.vector.tensor_copy(cnt, RP[0:1, 8:10]))
            link(nc.vector.tensor_scalar(cnt[:, 0:1], cnt[:, 0:1], float(HEADS), None, ALU.is_ge))
            link(nc.vector.tensor_scalar(cnt[:, 1:2], cnt[:, 1:2], 0.0, None, ALU.is_le))
            nc.vector.tensor_tensor(flags[0:1, 1:2], cnt[:, 0:1], cnt[:, 1:2], ALU.mult)

        @block.tensor
        def _(pe):
            for n, (t0, k, f) in enumerate(tjobs):
                pe.wait_ge(normed, t0 + k)
                if n >= 2:
                    pe.wait_ge(tp_used, n - 1)
                for j in range(k):
                    last = nc.tensor.transpose(TP[:, n % 2, j * P:(j + 1) * P], x1[:, t0 + j, f * P:(f + 1) * P],
                                               ident[:, :])
                last.then_inc(tp_full, 1)
            pe.wait_ge(tp_used, len(tjobs))
            for n, (c, w) in enumerate(CH):
                if n >= 2:
                    pe.wait_ge(e_used, n - 1)
                for f in range(FT):
                    last = nc.tensor.matmul(EP[0:40, n % 2, 0:w], va[:, f, :], featT[:, f, c:c + w],
                                            start=(f == 0), stop=(f == FT - 1))
                last.then_inc(e_full, 1)
            pe.wait_ge(e_used, len(CH))
            for t in range(NT):
                if t >= 2:
                    pe.wait_ge(wh_used, t - 1)
                for f in range(FT):
                    nc.tensor.matmul(WP[:, t % 2, :], featT[:, f, t * P:(t + 1) * P], wcat[:, f, :],
                                     start=(f == 0), stop=(f == FT - 1))
                for f in range(FT):
                    last = nc.tensor.matmul(EP[:, t % 2, 0:40], featT[:, f, t * P:(t + 1) * P], va[:, f, :],
                                            start=(f == 0), stop=(f == FT - 1))
                last.then_inc(wh_full, 1)
            pe.wait_ge(mid_ready, 1)
            nc.tensor.matmul(RP[:, 0:8], ones[32:40, :], mid, start=True, stop=True)
            nc.tensor.matmul(RP[0:1, 8:9], ext[:, 4:5], ones[32:40, 0:1], start=True, stop=True)
            nc.tensor.matmul(RP[0:1, 9:10], lones, ones[:, 0:1], start=True, stop=True).then_inc(ref_full, 1)


def layer_norm_scale(nc, dve, link, stat, var_ready, dev_ready, tmp):
    nc.vector.tensor_scalar(stat[:, 1, :], stat[:, 1, :], EPS, None, ALU.add).then_inc(var_ready, 1)
    dve.wait_ge(dev_ready, 1)
    link(nc.vector.reciprocal(stat[:, 3, :], stat[:, 2, :]))
    link(nc.vector.tensor_tensor(tmp, stat[:, 3, :], stat[:, 3, :], ALU.mult))
    link(nc.vector.tensor_tensor(tmp, tmp, stat[:, 1, :], ALU.mult))
    link(nc.vector.tensor_scalar(tmp, tmp, -0.5, 1.5, ALU.mult, ALU.add))
    link(nc.vector.tensor_tensor(stat[:, 3, :], stat[:, 3, :], tmp, ALU.mult))


def layer1_dense(nc, sem, v):
    work, small, esd, ident = (v[k] for k in ("work", "small", "esd", "ident"))
    dbc, wh, hT1 = v["sbc"], v["wh"], v["hT1"]
    o = 0
    def cut(w):
        nonlocal o
        o += w
        return work[:, o - w:o]
    T = [cut(NP), cut(NP)]
    mask = cut(N)
    scaled = cut(N)
    PT = cut(NP)
    adjt = cut(N)
    with ExitStack() as ctx:
        def S(name):
            return sem(ctx, "l1_" + name)
        SP_ = [ctx.enter_context(nc.psum_tensor(f"PT{k}", [P, 3, 512], F32)) for k in range(2)]
        O = ctx.enter_context(nc.psum_tensor("O", [P, D], F32))
        Sf = [s[:, :, :].rearrange("p b n -> p (b n)") for s in SP_]
        adj_in, dst_in, top, prob, transposed, copied, mixed, done, chain = (
            S(n) for n in ("adj_in", "dst_in", "top", "prob", "transposed", "copied", "mixed", "done", "chain"))
        nmax, den, rden = small[:, 0:8], small[:, 8:16], small[:, 16:24]
        block = ctx.enter_context(nc.Block())

        @block.sync
        def _(sp):
            for h in range(HEADS):
                sp.dma_start(dbc[:, h, :], v["sd_dram"][HEADS + h:HEADS + h + 1, :].to_broadcast([P, N])
                             ).then_inc(dst_in, 16)
            with sp.Fori(0, NT) as t:
                sp.wait_ge(done, t + 1)
                sp.dma_start(adjt, v["adj_dram"][bass.ts(t, P), :]).then_inc(adj_in, 16)

        @block.scalar
        def _(act):
            with act.Fori(0, NT) as t:
                for h in range(HEADS + 1):
                    if h < HEADS:
                        act.wait_ge(top, t * HEADS + (h + 1))
                        nc.scalar.activation(T[h % 2][:, 0:N], T[h % 2][:, 0:N], ACT.Exp, bias=nmax[:, h:h + 1],
                                             accum_out=den[:, h:h + 1]).then_inc(prob, 1)
                    if h >= 1:
                        act.wait_ge(transposed, t * HEADS + (h + 1))
                        act.wait_ge(mixed, t * HEADS + h)
                        nc.scalar.copy(PT, Sf[(h - 1) % 2][:, 0:NP]).then_inc(copied, 1)

        @block.tensor
        def _(pe):
            pe.sem_inc(transposed, 1)
            pe.sem_inc(mixed, 1)
            with pe.Fori(0, NT) as t:
                for h in range(HEADS):
                    pe.wait_ge(prob, t * HEADS + (h + 1))
                    for k in range(NT):
                        last = nc.tensor.transpose(Sf[h % 2][:, k * P:(k + 1) * P], T[h % 2][:, k * P:(k + 1) * P],
                                                   ident[:, :])
                    last.then_inc(transposed, 1)
                    pe.wait_ge(copied, t * HEADS + (h + 1))
                    if h == 0:
                        pe.wait_ge(done, t + 1)
                    for k in range(NT):
                        last = nc.tensor.matmul(O[:, h * DK:(h + 1) * DK], PT[:, k * P:(k + 1) * P],
                                                wh[:, k, h * DK:(h + 1) * DK], start=(k == 0), stop=(k == NT - 1))
                    last.then_inc(mixed, 1)

        @block.vector
        def _(dve):
            LINKS = 2 + 3 * HEADS + 1
            dve.wait_ge(dst_in, 16 * HEADS)
            nc.vector.memset(T[0][:, N:NP], 0.0)
            nc.vector.memset(T[1][:, N:NP], 0.0)
            dve.sem_inc(done, 1)
            with dve.Fori(0, NT) as t:
                links = [0]

                def link(ins):
                    links[0] += 1
                    ins.then_inc(chain, 1)
                    dve.wait_ge(chain, t * LINKS + links[0])

                dve.wait_ge(adj_in, (t + 1) * 16)
                link(nc.vector.tensor_scalar(mask, adjt, 0.0, 1.0e38, ALU.is_gt, ALU.mult))
                link(nc.vector.tensor_scalar(mask, mask, -NEG, None, ALU.add))
                for h in range(HEADS):
                    link(nc.vector.tensor_scalar(scaled, dbc[:, h, :], esd[:, t, h:h + 1], 0.2, ALU.add, ALU.mult))
                    if h >= 2:
                        dve.wait_ge(transposed, t * HEADS + h)
                    else:
                        dve.wait_ge(done, t + 1)
                        dve.wait_ge(transposed, t * HEADS + 1)
                    Th = T[h % 2][:, 0:N]
                    link(nc.vector.scalar_tensor_tensor(Th, dbc[:, h, :], esd[:, t, h:h + 1], scaled, ALU.add, ALU.max))
                    link(nc.vector.tensor_tensor(Th, Th, mask, ALU.min))
                    nc.vector.tensor_reduce(nmax[:, h:h + 1], Th, AX_X, ALU.max, negate=True).then_inc(top, 1)
                dve.wait_ge(mixed, t * HEADS + (HEADS + 1))
                link(nc.vector.reciprocal(rden, den))
                nc.vector.tensor_tensor(hT1[:, t, :].rearrange("p (h d) -> p h d", h=HEADS),
                                        O[:, :].rearrange("p (h d) -> p h d", h=HEADS),
                                        rden.rearrange("p (h d) -> p h d", d=1).to_broadcast([P, HEADS, DK]),
                                        ALU.mult).then_inc(done, 1)
                assert links[0] == LINKS


def layer1_factored(nc, sem, v):
    near1T, wh, sbc, hT1, esd, work, small = (v[k] for k in ("near1T", "wh", "sbc", "hT1", "esd", "work", "small"))
    C = DK + 1
    RING = 6
    V = [work[:, k * 2145:(k + 1) * 2145].bitcast(BF16).rearrange("p (t a s c) -> p t a s c", t=NT, a=2, s=3)
         for k in range(2)]
    o = 4290
    full = work[:, o:o + NT * 2 * C].rearrange("p (t a c) -> p t a c", t=NT, a=2)
    o += NT * 2 * C
    sums = work[:, o:o + 4 * 6 * C].rearrange("p (t s c) -> p t s c", t=4, s=6)
    o += 4 * 6 * C
    assert o + RING * 256 <= 9400
    with ExitStack() as ctx:
        def S(name):
            return sem(ctx, "f_" + name)
        def sb(name, shape, dt=F32):
            return ctx.enter_context(nc.sbuf_tensor(name, shape, dt))
        ring = v["wcat"][:, :, :].rearrange("p t d -> p (t d)")[:, 0:RING * 256].bitcast(BF16).rearrange(
            "p (r n) -> p r n", r=RING)
        ring2 = work[:, o:o + RING * 256].bitcast(BF16).rearrange("p (r n) -> p r n", r=RING)
        be = sb("be", [P, 2, NT, HEADS])
        ac = sb("ac", [P, 2, NT, HEADS])
        nd = sb("nd", [P, NT, HEADS])
        tm = v["wcat"][:, 3, 0:NT * HEADS].rearrange("p (t h) -> p t h", t=NT)
        red = sb("red", [P, 4, C])
        rden = sb("rden", [P, 4])
        O = [ctx.enter_context(nc.psum_tensor(f"O{k}", [P, 4, 512], F32)) for k in range(2)]
        src_in = [S(f"src_in{h}") for h in range(HEADS)]
        (args_ready, exps_ready, full_ready, hi_ready, rest_ready, mid_ready, v_ready, pos_ready, neg_ready, pn_used,
         moved, summed, chain) = (S(n) for n in (
            "args_ready", "exps_ready", "full_ready", "hi_ready", "rest_ready", "mid_ready", "v_ready", "pos_ready",
            "neg_ready", "pn_used", "moved", "summed", "chain"))
        STEPS = len(TG) * NT
        block = ctx.enter_context(nc.Block())

        @block.sync
        def _(sp):
            for h in range(HEADS):
                sp.dma_start(sbc[:, h, :], v["sd_dram"][h:h + 1, :].to_broadcast([P, N])).then_inc(src_in[h], 16)

        @block.scalar
        def _(act):
            def weigh(h, n, first=False):
                if not first:
                    act.wait_ge(v_ready, n)
                    act.wait_ge(pn_used, (n - 1) * STEPS + RING)
                for t in range(NT):
                    for a in range(2):
                        nc.scalar.activation(full[:, t, a, 0:DK], wh[:, t, bass.ds(h * DK, DK)], ACT.Copy,
                                             scale=be[:, a, t, bass.ds(h, 1)])
                nc.scalar.copy(full[:, :, :, DK:C], be[:, :, :, bass.ds(h, 1)].rearrange("p a t h -> p t a h")
                               ).then_inc(full_ready, 1)
                act.wait_ge(full_ready, n + 1)

            def cut(k, s, sem_):
                nc.scalar.copy(V[k][:, :, :, s, :], full).then_inc(sem_, 1)

            act.wait_ge(args_ready, 1)
            nc.scalar.activation(be[:, :, :, :], be[:, :, :, :], ACT.Exp)
            nc.scalar.activation(ac[:, :, :, :], ac[:, :, :, :], ACT.Exp).then_inc(exps_ready, 1)
            act.wait_ge(exps_ready, 1)
            weigh(0, 0, first=True)
            cut(0, 0, hi_ready)
            act.wait_ge(rest_ready, 1)
            cut(0, 1, mid_ready)
            act.sem_inc(moved, 2)

            def head(u, k, last):
                h = u * 2 + k
                for g, (t0, n) in enumerate(TG):
                    if not last:
                        if g == 0:
                            weigh(h + 1, h + 1)
                            cut((k + 1) % 2, 0, hi_ready)
                        if g == 1:
                            act.wait_ge(rest_ready, h + 2)
                            cut((k + 1) % 2, 1, mid_ready)
                    act.wait_ge(pn_used, h * STEPS + (RING + (g + 1) * NT))
                    act.wait_ge(summed, h * len(TG) + (g + 1))
                    bank = O[(k * len(TG) + g) % 2]
                    for i in range(n):
                        for a in range(2):
                            ins = nc.scalar.activation(
                                sums[:, i, 3 * a:3 * a + 3, :].rearrange("p s c -> p (s c)"),
                                bank[:, i, a * 3 * C:(a + 1) * 3 * C], ACT.Copy,
                                scale=ac[:, a, t0 + i, bass.ds(h, 1)])
                    ins.then_inc(moved, 1)

            with act.Fori(0, HEADS // 2 - 1) as u:
                head(u, 0, False)
                head(u, 1, False)
            head(HEADS // 2 - 1, 0, False)
            head(HEADS // 2 - 1, 1, True)

        @block.vector
        def _(dve):
            links = [0]

            def link(ins):
                links[0] += 1
                ins.then_inc(chain, 1)
                dve.wait_ge(chain, links[0])

            ref = small[:, 24:32].rearrange("p (a h) -> p a h", a=1).to_broadcast([P, NT, HEADS])
            link(nc.vector.tensor_tensor(be[:, 0, :, :], esd[:, :, HEADS:], ref, ALU.subtract))
            link(nc.vector.tensor_scalar(be[:, 1, :, :], be[:, 0, :, :], 0.2, None, ALU.mult))
            link(nc.vector.tensor_scalar(nd[:, :, :], esd[:, :, HEADS:], -1.0, None, ALU.mult))
            link(nc.vector.tensor_tensor(ac[:, 0, :, :], esd[:, :, 0:HEADS], ref, ALU.add))
            link(nc.vector.tensor_scalar(ac[:, 1, :, :], ac[:, 0, :, :], 0.2, None, ALU.mult))
            link(nc.vector.tensor_tensor(tm, ac[:, 0, :, :], ac[:, 1, :, :], ALU.max))
            link(nc.vector.tensor_tensor(ac[:, 0, :, :], ac[:, 0, :, :], tm, ALU.subtract))
            link(nc.vector.tensor_tensor(ac[:, 1, :, :], ac[:, 1, :, :], tm, ALU.subtract))
            dve.sem_inc(args_ready, 1)
            dve.sem_inc(summed, 1)
            base = links[0]

            def rest(n, k):
                dve.wait_ge(hi_ready, n)
                nc.vector.tensor_tensor(full, full, V[k][:, :, :, 0, :], ALU.subtract).then_inc(rest_ready, 1)

            def low(n, k):
                dve.wait_ge(mid_ready, n)
                nc.vector.tensor_tensor(V[k][:, :, :, 2, :], full, V[k][:, :, :, 1, :], ALU.subtract
                                        ).then_inc(v_ready, 1)

            def columns(g):
                t0, n = TG[g]
                return t0 * P, min(n * P, N - t0 * P), n

            def positive(u, k, q, sbh):
                h, (c0, w, _), j, slot = u * 2 + k, columns(q // NT), q % NT, (k * STEPS + q) % RING
                dve.wait_ge(pn_used, h * STEPS + (q + 1))
                nc.vector.scalar_tensor_tensor(ring[:, slot, 0:w], sbh[:, c0:c0 + w], nd[:, j, bass.ds(h, 1)],
                                               near1T[:, j, c0:c0 + w], ALU.is_gt, ALU.mult).then_inc(pos_ready, 1)

            def negative(u, k, q):
                h, (c0, w, _), j, slot = u * 2 + k, columns(q // NT), q % NT, (k * STEPS + q) % RING
                dve.wait_ge(pos_ready, h * STEPS + (q + 1))
                nc.vector.tensor_tensor(ring2[:, slot, 0:w], near1T[:, j, c0:c0 + w], ring[:, slot, 0:w],
                                        ALU.subtract).then_inc(neg_ready, 1)

            def reduce(u, k, g):
                h, (t0, n) = u * 2 + k, TG[g]
                dve.wait_ge(moved, h * len(TG) + (g + 3))
                nc.vector.tensor_reduce(red[:, 0:n, :], sums[:, 0:n, :, :].rearrange("p t s c -> p t c s"), AX_X,
                                        ALU.add).then_inc(summed, 1)
                dve.wait_ge(summed, h * len(TG) + (g + 2))
                nc.vector.reciprocal(rden[:, 0:n], red[:, 0:n, DK]).then_inc(chain, 1)
                dve.wait_ge(chain, h * len(TG) + (base + g + 1))
                nc.vector.tensor_tensor(
                    hT1[:, t0:t0 + n, bass.ds(h * DK, DK)], red[:, 0:n, 0:DK],
                    rden[:, 0:n].rearrange("p (t d) -> p t d", d=1).to_broadcast([P, n, DK]), ALU.mult)

            def head(u, k, first=False, last=False):
                h = u * 2 + k
                sbh = sbc[:, bass.ds(h, 1), :].rearrange("p a n -> p (a n)")
                for q in range(STEPS + 1):
                    if q < STEPS:
                        positive(u, k, q, sbh)
                    if q >= 1:
                        negative(u, k, q - 1)
                    if not last and q == NT - 3:
                        rest(h + 2, (k + 1) % 2)
                    if not last and q == 2 * NT:
                        low(h + 2, (k + 1) % 2)
                    if q in (NT + 6, 2 * NT + 6):
                        reduce(u, k, (q - 6) // NT - 1)
                    if q == 6 and not first:
                        reduce(*((u, 0) if k else (u - 1, 1)), len(TG) - 1)

            rest(1, 0)
            low(1, 0)
            dve.wait_ge(src_in[0], 16)
            head(0, 0, first=True)
            dve.wait_ge(src_in[1], 16)
            head(0, 1)
            for h in range(2, HEADS):
                dve.wait_ge(src_in[h], 16)
            with dve.Fori(1, HEADS // 2 - 1) as u:
                head(u, 0)
                head(u, 1)
            u = HEADS // 2 - 1
            head(u, 0)
            head(u, 1, last=True)
            reduce(u, 1, len(TG) - 1)

        @block.tensor
        def _(pe):
            pe.sem_inc(pn_used, RING)

            def head(u, k):
                h = u * 2 + k
                pe.wait_ge(v_ready, h + 1)
                for g, (t0, n) in enumerate(TG):
                    pe.wait_ge(moved, h * len(TG) + (g + 1))
                    bank = O[(k * len(TG) + g) % 2]
                    for j in range(NT):
                        q = g * NT + j
                        slot = (k * STEPS + q) % RING
                        pe.wait_ge(neg_ready, h * STEPS + (q + 1))
                        for i in range(n):
                            for a, m in enumerate((ring, ring2)):
                                last = nc.tensor.matmul(
                                    bank[:, i, a * 3 * C:(a + 1) * 3 * C], m[:, slot, i * P:(i + 1) * P],
                                    V[k][:, j, a, :, :].rearrange("p s c -> p (s c)"),
                                    start=(j == 0 and a == 0), stop=(j == NT - 1), skip_group_check=True)
                        last.then_inc(pn_used, 1)

            with pe.Fori(0, HEADS // 2) as u:
                head(u, 0)
                head(u, 1)


def tail(nc, sem, v):
    x1, hT1, stat, ident, work, small, bias, b4bc = (v[k] for k in (
        "x1", "hT1", "stat", "ident", "work", "small", "bias", "b4bc"))
    w1T, w2T, w3T, w4T, out = (v[k] for k in ("w1T", "w2T", "w3T", "w4T", "out"))
    nodes = v["nodes"]
    qkf = v["qk"][:, :]
    encT = [qkf[:, k * 2048:(k + 1) * 2048].rearrange("p (f n) -> p f n", f=FT) for k in range(2)]
    o1 = [work[:, k * 1024:(k + 1) * 1024].rearrange("p (f n) -> p f n", f=2) for k in range(2)]
    o2 = [work[:, 2048 + k * 512:2560 + k * 512] for k in range(2)]
    o3 = [work[:, 3072 + k * 1024:4096 + k * 1024].rearrange("p (f n) -> p f n", f=2) for k in range(2)]
    ex = [work[:, 5120 + k * 512:5632 + k * 512] for k in range(2)]
    with ExitStack() as ctx:
        def S(name):
            return sem(ctx, "t_" + name)
        TP = ctx.enter_context(nc.psum_tensor("TPt", [P, 2, 512], F32))
        MP = ctx.enter_context(nc.psum_tensor("MP", [P, 2, 512], F32))
        OP = ctx.enter_context(nc.psum_tensor("OP", [P, 2, 512], F32))
        stats = ctx.enter_context(nc.sbuf_tensor("stats1", [P, NT, 6], F32))
        (neg_ready, exp_ready, elu_done, tp_full, tp_used, mm_full, mm_used, out_full, out_used, var_ready, dev_ready,
         normed, stored, chain) = (S(n) for n in (
            "neg_ready", "exp_ready", "elu_done", "tp_full", "tp_used", "mm_full", "mm_used", "out_full", "out_used",
            "var_ready", "dev_ready", "normed", "stored", "chain"))
        NG = len(TG)
        block = ctx.enter_context(nc.Block())

        @block.sync
        def _(sp):
            for g, (t0, k) in enumerate(TG):
                sp.wait_ge(normed, t0 + k)
                full = min(k, NFULL - t0)
                sp.dma_start(out[t0 * P:(t0 + full) * P, :].rearrange("(t p) f -> p t f", p=P),
                             x1[:, t0:t0 + full, :]).then_inc(stored, 16)
            sp.dma_start(out[NFULL * P:N, :], x1[0:LAST, NFULL, :]).then_inc(stored, 16)
            sp.wait_ge(stored, 16 * (NG + 1))

        @block.scalar
        def _(act):
            for t in range(NT):
                act.wait_ge(neg_ready, t + 1)
                nc.scalar.activation(ex[t % 2], ex[t % 2], ACT.Exp).then_inc(exp_ready, 1)
            m = 0
            for g, (t0, k) in enumerate(TG):
                w = k * P
                for f in range(FT):
                    act.wait_ge(tp_full, g * FT + f + 1)
                    nc.scalar.copy(encT[g % 2][:, f, 0:w], TP[:, f % 2, 0:w]).then_inc(tp_used, 1)
                for dst, b in ((o1[g % 2][:, 0, 0:w], 8), (o1[g % 2][:, 1, 0:w], 9), (o2[g % 2][:, 0:w], 10),
                               (o3[g % 2][:, 0, 0:w], 11), (o3[g % 2][:, 1, 0:w], 12)):
                    act.wait_ge(mm_full, m + 1)
                    nc.scalar.activation(dst, MP[:, m % 2, 0:w], ACT.Relu, bias=bias[:, b:b + 1]).then_inc(mm_used, 1)
                    m += 1
            act.wait_ge(var_ready, 1)
            nc.scalar.activation(stat[:, 2, :], stat[:, 1, :], ACT.Sqrt).then_inc(dev_ready, 1)

        @block.tensor
        def _(pe):
            m = 0
            for g, (t0, k) in enumerate(TG):
                w = k * P
                pe.wait_ge(elu_done, t0 + k)
                for f in range(FT):
                    if g * FT + f >= 2:
                        pe.wait_ge(tp_used, g * FT + f - 1)
                    for j in range(k):
                        last = nc.tensor.transpose(TP[:, f % 2, j * P:(j + 1) * P], hT1[:, t0 + j, f * P:(f + 1) * P],
                                                   ident[:, :])
                    last.then_inc(tp_full, 1)
                pe.wait_ge(tp_used, (g + 1) * FT)
                e, a, b, c = encT[g % 2], o1[g % 2], o2[g % 2], o3[g % 2]
                layers = ([[(w1T[:, f, o * P:(o + 1) * P], e[:, f, 0:w]) for f in range(FT)] for o in range(2)],
                          [[(w2T[:, f, :], a[:, f, 0:w]) for f in range(2)]],
                          [[(w3T[:, o * P:(o + 1) * P], b[:, 0:w])] for o in range(2)])
                for layer in layers:
                    pe.wait_ge(mm_used, m)
                    for terms in layer:
                        for n, (l, r) in enumerate(terms):
                            last = nc.tensor.matmul(MP[:, m % 2, 0:w], l, r, start=(n == 0), stop=(n == len(terms) - 1))
                        last.then_inc(mm_full, 1)
                        m += 1
                pe.wait_ge(mm_used, m)
                for j in range(k):
                    t = t0 + j
                    if t >= 2:
                        pe.wait_ge(out_used, t - 1)
                    for f in range(2):
                        last = nc.tensor.matmul(OP[:, t % 2, :], c[:, f, j * P:(j + 1) * P], w4T[:, f, :],
                                                start=(f == 0), stop=(f == 1))
                    last.then_inc(out_full, 1)

        @block.vector
        def _(dve):
            links = [0]

            def link(ins):
                links[0] += 1
                ins.then_inc(chain, 1)
                dve.wait_ge(chain, links[0])

            for t in range(NT):
                link(nc.vector.tensor_tensor(x1[:, t, :], x1[:, t, :], b4bc[:, :], ALU.add))
            for t in range(NT + 1):
                if t < NT:
                    nc.vector.tensor_scalar(ex[t % 2], hT1[:, t, :], 0.0, None, ALU.min).then_inc(neg_ready, 1)
                if t >= 1:
                    z = hT1[:, t - 1, :]
                    dve.wait_ge(exp_ready, t)
                    link(nc.vector.tensor_scalar(ex[(t - 1) % 2], ex[(t - 1) % 2], -1.0, None, ALU.add))
                    nc.vector.scalar_tensor_tensor(z, z, 0.0, ex[(t - 1) % 2], ALU.max, ALU.add).then_inc(elu_done, 1)
                    dve.wait_ge(elu_done, t)
            for t in range(NT):
                dve.wait_ge(out_full, t + 1)
                nc.vector.tensor_tensor(x1[:, t, :], OP[:, t % 2, :], x1[:, t, :], ALU.add).then_inc(out_used, 1)
                dve.wait_ge(out_used, t + 1)
                link(nc.vector.bn_stats(stats[:, t, :], x1[:, t, :]))
                link(nc.vector.bn_aggr(stat[:, 0:2, t], stats[:, t, :]))
            layer_norm_scale(nc, dve, link, stat, var_ready, dev_ready, small[:, 0:NT])
            for t in range(NT):
                nc.vector.tensor_scalar(x1[:, t, :], x1[:, t, :], stat[:, 0, t:t + 1], stat[:, 3, t:t + 1],
                                        ALU.subtract, ALU.mult).then_inc(normed, 1)


_INS = ['x', 'adj', 'L0_gnn_rel_pair_index', 'L0_gnn_Wq', 'L0_gnn_bq', 'L0_gnn_Wk', 'L0_gnn_bk', 'L1_gnn_W',
        'L1_gnn_a1', 'L1_gnn_a2', 'L1_gnn_W1', 'L1_gnn_b1', 'L1_gnn_W2', 'L1_gnn_b2', 'L1_gnn_W3', 'L1_gnn_b3',
        'L1_gnn_W4', 'L1_gnn_b4']


def kernel(**inputs):
    import numpy as np
    import concourse.bacc as bacc
    from concourse.bass_utils import run_bass_kernel_spmd

    nc = bacc.Bacc("TRN2", target_bir_lowering=False, num_devices=1)
    arrays, args = {}, []
    for name in _INS:
        a = np.ascontiguousarray(inputs[name])
        arrays[f"in_{name}"] = a
        args.append(nc.dram_tensor(f"in_{name}", a.shape, mybir.dt.from_np(a.dtype), kind="ExternalInput").ap())
    args.append(nc.dram_tensor("out_0", (N, D), F32, kind="ExternalOutput").ap())
    args.append(nc.dram_tensor("edge_matrix", (NP, N), F32, kind="Internal").ap())
    args.append(nc.dram_tensor("adj_padded", (NP, N), F32, kind="Internal").ap())
    args.append(nc.dram_tensor("scores_src_dst", (2 * HEADS, N), F32, kind="Internal").ap())
    program(nc, *args)
    r = run_bass_kernel_spmd(nc, [arrays], core_ids=[0])
    return r.results[0]["out_0"]
```

```python
from contextlib import ExitStack

import concourse.bass as bass
from concourse import mybir

ALU = mybir.AluOpType
ACT = mybir.ActivationFunctionType
F32 = mybir.dt.float32
BF16 = mybir.dt.bfloat16
I32 = mybir.dt.int32
U32 = mybir.dt.uint32
AX_X = mybir.AxisListType.X

P = 128
N = 1354
NT = (N + P - 1) // P
NFULL = N // P
LAST = N - NFULL * P
NP = NT * P
D = 512
FT = D // P
HEADS = 8
DK = D // HEADS
EDGES = 10000
EROWS = 125
ECOLS = EDGES // EROWS
CH = [(c, min(512, N - c)) for c in range(0, N, 512)]
TG = [(t, min(4, NT - t)) for t in range(0, NT, 4)]
BIG = 3.0e38
SLOTS = P
SPREAD = 80.0
KMAX = 16
CT = 6
CLAST = -(-(LAST * CT + P - LAST) // P)
GONE = 2048
NAT = 4116
REC = D + 2 * HEADS
NEG = 9.0e15
EPS = 1.0e-5


def width(t):
    return LAST if t == NT - 1 else P


def program(nc, x, adj, rel, Wq, bq, Wk, bk, W, a1, a2, W1, b1, W2, b2, W3, b3, W4, b4, out, edge_dram, adj_dram,
            sd_dram, rec_dram, x1_dram, y_dram):
    with ExitStack() as ctx:
        def sb(name, shape, dt=F32):
            return ctx.enter_context(nc.sbuf_tensor(name, shape, dt))

        slotT = sb("slotT", [P, NT, CT * P], BF16)
        wqk = sb("wqk", [P, 2 * FT * D])
        nodes = sb("nodes", [P, NT, D])
        featT = sb("featT", [P, FT, NP])
        x1 = sb("x1", [P, NT, D])
        qk = sb("qk", [P, 2 * FT * NP])
        work = sb("work", [P, 3 * CT * REC])
        wcat = sb("wcat", [P, FT, REC])
        w1T = sb("w1T", [P, FT, 2 * P])
        w2T = sb("w2T", [P, 2, P])
        w3T = sb("w3T", [P, 2 * P])
        w4T = sb("w4T", [P, 2, D])
        b4bc = sb("b4bc", [P, D])
        bias = sb("bias", [P, 16])
        ident = sb("ident", [P, P])
        before = sb("before", [P, P])
        ones = sb("ones", [P, P])
        stat = sb("stat", [P, 4, NT])
        esd = sb("esd", [P, NT + 1, 2 * HEADS])
        deg0 = sb("deg0", [P, NT])
        ell = sb("ell", [P, NT, KMAX + 2])
        ends = sb("ends", [P, NT])
        span = sb("span", [P, 2, NT])
        allsum = sb("allsum", [P, NT])
        edges = sb("edges", [EROWS, ECOLS, 3])
        met = sb("met", [EROWS, ECOLS])
        colsum = sb("colsum", [ECOLS, 1])
        nbr = sb("nbr", [P, NT, CT], I32)
        owner = sb("owner", [P, NT, CT])
        eidx = sb("eidx", [EROWS, ECOLS], I32)
        small = sb("small", [P, 64])
        flags = sb("flags", [1, 2], I32)
        wh = nodes
        hT1 = featT[:, :, :].rearrange("p f n -> p (f n)")[:, 0:NT * D].rearrange("p (t d) -> p t d", t=NT)
        qk4 = qk[:, :].rearrange("p (a f n) -> p a f n", a=2, f=FT)
        sbc = qk[:, 0:HEADS * N].rearrange("p (h n) -> p h n", h=HEADS)
        qTw, kTw = (wqk[:, k * FT * D:(k + 1) * FT * D].rearrange("p (t o) -> p t o", t=FT) for k in range(2))
        qnat, knat = (work[:, NAT + k * FT * D:NAT + (k + 1) * FT * D].rearrange("p (t f) -> p t f", t=FT)
                      for k in range(2))
        qk_jobs = []
        for src, dst in ((qnat, qTw), (knat, kTw)):
            for f in range(FT):
                qk_jobs.append(([src[:, t, f * P:(f + 1) * P] for t in range(FT)], dst[:, f, :]))
        w1n = work[:, NAT:NAT + 2 * D].rearrange("p (t f) -> p t f", t=2)
        w2n = work[:, NAT + 2 * D:NAT + 2 * D + 2 * P]
        w3n = work[:, NAT + 2 * D + 2 * P:NAT + 2 * D + 4 * P].rearrange("p (t f) -> p t f", t=2)
        w4n = work[:, NAT + 3 * D:NAT + 5 * D].rearrange("p (t f) -> p t f", t=4)
        mlp_jobs = [([w1n[:, t, f * P:(f + 1) * P] for t in range(2)], w1T[:, f, :]) for f in range(FT)]
        mlp_jobs += [([w2n[:, f * P:(f + 1) * P]], w2T[:, f, :]) for f in range(2)]
        mlp_jobs += [([w3n[:, t, :] for t in range(2)], w3T[:, :])]
        mlp_jobs += [([w4n[:, t, f * P:(f + 1) * P] for t in range(4)], w4T[:, f, :]) for f in range(2)]

        def sem(stack, name):
            return stack.enter_context(nc.semaphore(name))

        sparse_nums = []

        def sparse_sem(stack, name):
            handle = sem(stack, name)
            sparse_nums.append(handle.num)
            return handle

        def dense_sem(stack, name):
            if not sparse_nums:
                return sem(stack, name)
            return stack.enter_context(nc.semaphore(name, num=sparse_nums.pop(0)))

        v = locals()
        prep(nc, sem, v)
        (flag,) = load_flag(nc, flags[0:1, 0:1])
        with nc.If(flag == 1):
            records(nc, sparse_sem, v, True)
        with nc.Else():
            dense_prep(nc, dense_sem, v, 0)
            layer0_dense(nc, dense_sem, v)
            records(nc, dense_sem, v, False)
        nc.end_all_ifs()
        sparse_nums.clear()
        (flag,) = load_flag(nc, flags[0:1, 1:2])
        with nc.If(flag == 1):
            layer1_sparse(nc, sparse_sem, v)
        with nc.Else():
            dense_prep(nc, dense_sem, v, 1)
            layer1_dense(nc, dense_sem, v)
            dense_weights(nc, dense_sem, v)
            tail(nc, dense_sem, v)
        nc.end_all_ifs()


def load_flag(nc, ap):
    r = nc.values_load(ap, min_val=0, max_val=1)
    return (r,)


def prep(nc, sem, v):
    x, adj, rel = v["x"], v["adj"], v["rel"]
    slotT, nodes, featT, x1, qk, wcat = (v[k] for k in ("slotT", "nodes", "featT", "x1", "qk", "wcat"))
    bias, ident, work, b4bc, before, ones = (v[k] for k in ("bias", "ident", "work", "b4bc", "before", "ones"))
    deg0, ell, ends, span, allsum, edges, met, colsum, eidx, flags = (v[k] for k in (
        "deg0", "ell", "ends", "span", "allsum", "edges", "met", "colsum", "eidx", "flags"))
    gbuf = v["wqk"][:, :]
    ff = featT[:, :, :].rearrange("p f n -> p (f n)")
    prods = work[:, NAT:NAT + 2 * FT * D].rearrange("p (k t d) -> p k t d", k=2, t=FT)
    number, dist = gbuf[:, 3200:3200 + CT * P], work[:, 8212:8212 + CT * P]
    abc = v["w4T"][:, :, :]
    ffb = ff.bitcast(BF16)
    xpart = [ffb[:, 0:NT * D].rearrange("p (t d) -> p t d", t=NT),
             ffb[:, NT * D:2 * NT * D].rearrange("p (t d) -> p t d", t=NT),
             qk[:, 7744:7744 + NT * D // 2].bitcast(BF16).rearrange("p (t d) -> p t d", t=NT)]
    near0T = qk[:, 0:7744].bitcast(BF16).rearrange("p (t n) -> p t n", t=NT)
    adjt = [work[:, 0:N], work[:, N:2 * N]]
    codet = [work[:, 2708 + k * 704:3412 + k * 704].bitcast(BF16) for k in range(2)]
    revn, keys = gbuf[:, 0:N], gbuf[:, N:2 * N]
    rest = [work[:, 8212 + k * D:8724 + k * D] for k in range(2)]
    with ExitStack() as ctx:
        def S(name):
            return sem(ctx, name)

        brow = ctx.enter_context(nc.sbuf_tensor("brow", [13, P], F32))
        pair = gbuf[0:EROWS, 2 * N:2 * N + 2 * ECOLS].bitcast(I32)
        ef = gbuf[0:EROWS, 2900:2900 + 2 * ECOLS].rearrange("p (a c) -> p a c", a=2)
        got = gbuf[0:EROWS, 3100:3100 + ECOLS]
        identb = ctx.enter_context(nc.sbuf_tensor("identb", [P, P], BF16))
        offdiag = ctx.enter_context(nc.sbuf_tensor("offdiag", [P, P], BF16))
        onesb = ctx.enter_context(nc.sbuf_tensor("onesb", [P, 1], BF16))
        rownum = ctx.enter_context(nc.sbuf_tensor("rownum", [P, 1], F32))
        count = ctx.enter_context(nc.sbuf_tensor("count", [P, NT], F32))
        there = ctx.enter_context(nc.sbuf_tensor("there", [P, KMAX], F32))
        best = ctx.enter_context(nc.sbuf_tensor("best", [P, KMAX], F32))
        MT = [ctx.enter_context(nc.psum_tensor(f"MT{k}", [P, 2048], BF16)) for k in range(2)]
        TP = ctx.enter_context(nc.psum_tensor("TP", [P, 3, 512], F32))
        DG = ctx.enter_context(nc.psum_tensor("DG", [P, 512], F32))

        x_in = [S(f"x_in{k}") for k in range(len(TG))]
        wcat_in, a_in, b4_in, bias_in, rel_in, y_out, prods_ready = (S(n) for n in (
            "wcat_in", "a_in", "b4_in", "bias_in", "rel_in", "y_out", "prods_ready"))
        adj_in = [S("adj_in0"), S("adj_in1")]
        padded, ident_set, ident_done, index_done, gathered = (S(n) for n in (
            "padded", "ident_set", "ident_done", "index_done", "gathered"))
        tp_full, tp_used, dve_chain = (S(n) for n in ("tp_full", "tp_used", "dve_chain"))
        hi_ready, rest_ready, mid_ready, rest2_ready, lo_ready = (S(n) for n in (
            "hi_ready", "rest_ready", "mid_ready", "rest2_ready", "lo_ready"))
        code_ready, flipped, key_ready, near0_ready, diag_off, y_full, y_used = (S(n) for n in (
            "code_ready", "flipped", "key_ready", "near0_ready", "diag_off", "y_full", "y_used"))
        deg_ready, revn_ready, keys_used, kept = (S(n) for n in ("deg_ready", "revn_ready", "keys_used", "kept"))
        rownum_ready, count_ready, first_full, first_used, spanned, masks_made, numbered = (S(n) for n in (
            "rownum_ready", "count_ready", "first_full", "first_used", "spanned", "masks_made", "numbered"))
        firsts = [S("firsts0"), S("firsts1")]
        met_ready, col_full, col_ready, total_full = (S(n) for n in ("met_ready", "col_full", "col_ready", "total_full"))

        block = ctx.enter_context(nc.Block())

        @block.sync
        def _(sp):
            def load_adj(t, k, rows):
                sp.wait_ge(key_ready, t + 1)
                sp.dma_start(adjt[k][0:rows, :], adj[bass.ds(t * P, rows), :]).then_inc(adj_in[k], 16)

            for g, (t0, k) in enumerate(TG):
                full = min(k, NFULL - t0)
                sp.dma_start(nodes[:, t0:t0 + full, :], x[t0 * P:(t0 + full) * P, :].rearrange("(t p) f -> p t f", p=P)
                             ).then_inc(x_in[g], 16)
            sp.wait_ge(padded, 1)
            sp.dma_start(nodes[0:LAST, NFULL, :], x[NFULL * P:N, :]).then_inc(x_in[-1], 16)
            for t in range(2):
                load_adj(t, t, P)
            for t in range(FT):
                sp.dma_start(wcat[:, t, 0:D].rearrange("p (h d) -> p h d", h=HEADS),
                             v["W"][:, t * P:(t + 1) * P, :].rearrange("h p d -> p h d")).then_inc(wcat_in, 16)
            for k, name in enumerate(("a1", "a2")):
                sp.dma_start(abc[:, k, :], v[name].rearrange("(a h) d -> a (h d)", a=1).to_broadcast([P, D])
                             ).then_inc(a_in, 16)
            for name, c, k in (("bq", 0, 4), ("bk", 4, 4), ("b1", 8, 2), ("b2", 10, 1), ("b3", 11, 2)):
                sp.dma_start(brow[c:c + k, :], v[name].rearrange("(t p) -> t p", p=P)).then_inc(bias_in, 16)
            with sp.Fori(1, NFULL // 2) as u:
                for k in range(2):
                    load_adj(u * 2 + k, k, P)
            load_adj(NFULL, 0, LAST)
            sp.dma_start(b4bc[:, :], v["b4"].rearrange("(a d) -> a d", a=1).to_broadcast([P, D])).then_inc(b4_in, 16)
            sp.wait_ge(b4_in, 16)

        @block.scalar
        def _(act):
            act.dma_start(pair[:, :], rel.rearrange("(p c) k -> p (c k)", p=EROWS)).then_inc(rel_in, 16)
            def near0(t, k):
                act.wait_ge(flipped, t + 3)
                nc.scalar.copy(near0T[:, :, t * P:(t + 1) * P],
                               MT[k][:, 0:NP].rearrange("p (t n) -> p t n", t=NT)).then_inc(near0_ready, 1)

            act.sem_inc(near0_ready, 2)
            act.sem_inc(y_used, 2)
            for g, (t0, k) in enumerate(TG):
                act.wait_ge(x_in[g], 32 if g == len(TG) - 1 else 16)
                for t in range(t0, t0 + k):
                    if t == 6:
                        near0(0, 0)
                    nc.scalar.copy(xpart[0][:, t, :], nodes[:, t, :]).then_inc(hi_ready, 1)
                    if t >= 1:
                        act.wait_ge(rest_ready, t)
                        nc.scalar.copy(xpart[1][:, t - 1, :], rest[(t - 1) % 2]).then_inc(mid_ready, 1)
            act.wait_ge(rest_ready, NT)
            nc.scalar.copy(xpart[1][:, NT - 1, :], rest[(NT - 1) % 2]).then_inc(mid_ready, 1)

            def keep_y(t, k):
                act.wait_ge(y_full, t + 1)
                nc.scalar.copy(x1[:, t, :], TP[:, k, :]).then_inc(y_used, 1)
                act.wait_ge(y_used, t + 3)
                rows = width(t)
                act.dma_start(v["y_dram"][t * P:t * P + rows, :], x1[0:rows, t, :]).then_inc(y_out, 16)

            act.wait_ge(tp_full, 1)
            nc.scalar.copy(bias[:, 0:13], TP[:, 2, 0:13]).then_inc(tp_used, 1)

            def slots_of(t):
                act.wait_ge(first_full, t + 1)
                at, n = TP[:, 2, 16 + t:17 + t], count[:, t:t + 1]
                nc.scalar.copy(ell[:, t, KMAX:KMAX + 1], at).then_inc(first_used, 1)
                nc.scalar.activation(span[:, 1, t:t + 1], n, ACT.Copy, scale=0.5).then_inc(spanned, 1)
                nc.scalar.activation(span[:, 0, t:t + 1], n, ACT.Copy, scale=-0.5, bias=0.5).then_inc(spanned, 1)
                act.wait_ge(spanned, 3 * t + 2)
                nc.scalar.activation(span[:, 0, t:t + 1], at, ACT.Identity, scale=-1.0, bias=span[:, 0, t:t + 1]
                                     ).then_inc(spanned, 1)
                act.wait_ge(spanned, 3 * t + 3)
                slot_mask(nc, act, v, number, dist, masks_made, t)

            act.wait_ge(numbered, 1)
            act.wait_ge(lo_ready, NT)
            for t in range(NT):
                if t + 1 < NT:
                    near0(t + 1, (t + 1) % 2)
                if 1 <= t < NT - 1:
                    slots_of(t - 1)
                if t == NT - 1:
                    slots_of(t - 1)
                    slots_of(t)
                keep_y(t, t % 2)
            act.wait_ge(y_full, NT)
            nc.scalar.copy(deg0[:, :], DG[:, 0:NT]).then_inc(deg_ready, 1)
            act.wait_ge(y_out, 16 * NT)

        @block.gpsimd
        def _(pool):
            nc.gpsimd.memset(ident[:, :], 0.0).then_inc(ident_set, 1)
            nc.gpsimd.memset(before[:, :], 1.0).then_inc(ident_set, 1)
            pool.wait_ge(ident_set, 2)
            nc.gpsimd.affine_select(out=ident[:, :], in_=ident[:, :], compare_op=ALU.not_equal, fill=1.0, base=0,
                                    pattern=[[-1, P]], channel_multiplier=1).then_inc(ident_done, 1)
            nc.gpsimd.affine_select(out=before[:, :], in_=before[:, :], compare_op=ALU.is_gt, fill=0.0, base=0,
                                    pattern=[[1, P]], channel_multiplier=-1).then_inc(ident_done, 1)
            nc.gpsimd.iota(revn, pattern=[[-1, N]], base=GONE, channel_multiplier=0,
                           allow_small_or_imprecise_dtypes=True).then_inc(revn_ready, 1)
            nc.gpsimd.iota(rownum[:, :], pattern=[[0, 1]], base=1, channel_multiplier=1,
                           allow_small_or_imprecise_dtypes=True).then_inc(rownum_ready, 1)
            nc.gpsimd.iota(number, pattern=[[1, CT * P]], base=0, channel_multiplier=0,
                           allow_small_or_imprecise_dtypes=True).then_inc(numbered, 1)
            pool.wait_ge(index_done, 1)
            for c in range(ECOLS):
                nc.gpsimd.indirect_dma_start(
                    out=got[:, c:c + 1], out_offset=None, in_=adj.rearrange("a (b k) -> (a b) k", k=1),
                    in_offset=bass.IndirectOffsetOnAxis(ap=eidx[:, c:c + 1].bitcast(U32), axis=0),
                    bounds_check=N * N - 1, oob_is_err=False).then_inc(gathered, 16)
            pool.wait_ge(wcat_in, 16 * FT)
            pool.wait_ge(a_in, 32)
            for k in range(2):
                for t in range(FT):
                    nc.gpsimd.tensor_tensor(prods[:, k, t, :], wcat[:, t, 0:D], abc[:, k, :], ALU.mult
                                            ).then_inc(prods_ready, 1)

        @block.vector
        def _(dve):
            links = [0]

            def link(ins):
                links[0] += 1
                ins.then_inc(dve_chain, 1)
                dve.wait_ge(dve_chain, links[0])

            dve.sem_inc(code_ready, 2)
            dve.sem_inc(key_ready, 2)
            nc.vector.memset(nodes[64:P, NFULL, :], 0.0).then_inc(padded, 1)
            nc.vector.memset(got[:, :], 0.0)
            nc.vector.memset(edges[:, :, 2], 1.0)
            nc.vector.memset(ones[:, :], 1.0)
            nc.vector.memset(onesb[:, :], 1.0)
            link(nc.vector.memset(ell[:, :, :], 0.0))
            link(nc.vector.memset(ell[64:P, NFULL, 0:1], float(GONE)))
            link(nc.vector.memset(allsum[64:P, NFULL:NT], float(GONE)))
            for k in range(2):
                link(nc.vector.memset(codet[k], 0.0))
            dve.wait_ge(rel_in, 16)
            both = pair[:, :].rearrange("p (c k) -> p k c", k=2)
            for k in range(2):
                link(nc.vector.tensor_copy(edges[:, :, k], both[:, k, :]))
                link(nc.vector.tensor_scalar(ef[:, 0, :], edges[:, :, k], 0.0, float(N), ALU.is_lt, ALU.mult))
                link(nc.vector.tensor_tensor(edges[:, :, k], edges[:, :, k], ef[:, 0, :], ALU.add))
            link(nc.vector.tensor_tensor(ef[:, 0, :], edges[:, :, 0], edges[:, :, 1], ALU.not_equal))
            for k in range(2):
                for lim, op in ((0.0, ALU.is_ge), (float(N), ALU.is_lt)):
                    link(nc.vector.scalar_tensor_tensor(ef[:, 0, :], edges[:, :, k], lim, ef[:, 0, :], op, ALU.mult))
            link(nc.vector.scalar_tensor_tensor(ef[:, 1, :], edges[:, :, 0], float(N), edges[:, :, 1], ALU.mult, ALU.add))
            link(nc.vector.scalar_tensor_tensor(ef[:, 1, :], ef[:, 1, :], float(-N * N), ef[:, 0, :], ALU.add, ALU.mult))
            link(nc.vector.tensor_scalar(ef[:, 1, :], ef[:, 1, :], float(N * N), None, ALU.add))
            nc.vector.tensor_copy(eidx[:, :], ef[:, 1, :]).then_inc(index_done, 1)
            dve.wait_ge(ident_done, 2)
            link(nc.vector.tensor_copy(identb[:, :], ident[:, :]))
            link(nc.vector.tensor_scalar(offdiag[:, :], ident[:, :], -1.0, 1.0, ALU.mult, ALU.add))

            def mask_code(t):
                rows = width(t)
                if t == NFULL:
                    dve.wait_ge(flipped, NFULL + 1)
                    nc.vector.memset(codet[0][64:P, :], 0.0).then_inc(padded, 1)
                    dve.wait_ge(padded, 2)
                dve.wait_ge(adj_in[t % 2], 16 * (t // 2 + 1))
                dve.wait_ge(flipped, t + 1)
                nc.vector.tensor_scalar(codet[t % 2][0:rows, 0:N], adjt[t % 2][0:rows, :], 1.0, None, ALU.is_equal
                                        ).then_inc(code_ready, 1)

            def key_tile(t):
                rows = width(t)
                dve.wait_ge(kept, t + 1)
                nc.vector.scalar_tensor_tensor(keys[0:rows, :], adjt[t % 2][0:rows, :], 0.0, revn[0:rows, :], ALU.is_gt,
                                               ALU.mult, accum_out=allsum[0:rows, t:t + 1]
                                               ).then_inc(key_ready, 1)

            def neighbours(t):
                rows = width(t)
                dve.wait_ge(key_ready, t + 3)
                nc.vector.max(best[0:rows, 0:8], keys[0:rows, :]).then_inc(firsts[0], 1)
                dve.wait_ge(firsts[0], t + 1)
                nc.vector.match_replace(keys[0:rows, :], best[0:rows, 0:8], keys[0:rows, :], 0.0).then_inc(keys_used, 1)
                dve.wait_ge(keys_used, t + 1)
                nc.vector.max(best[0:rows, 8:16], keys[0:rows, :]).then_inc(firsts[1], 1)
                dve.wait_ge(firsts[1], t + 1)
                nc.vector.tensor_copy(ell[0:rows, t, 0:KMAX], best[0:rows, :]
                                      ).then_inc(kept, 1)
                dve.wait_ge(kept, t + 2)
                nc.vector.scalar_tensor_tensor(there[:, :], ell[:, t, 0:KMAX], 0.0, ones[:, 0:KMAX], ALU.is_gt,
                                               ALU.mult, accum_out=count[:, t:t + 1]).then_inc(count_ready, 1)

            def cut_diagonal(t):
                dve.wait_ge(near0_ready, t + 3)
                d = near0T[:, t, t * P:(t + 1) * P]
                nc.vector.tensor_tensor(d, d, offdiag[:, :], ALU.mult).then_inc(diag_off, 1)

            dve.sem_inc(kept, 1)
            dve.wait_ge(revn_ready, 1)
            mask_code(0)
            mask_code(1)
            for t in range(NT + 1):
                if t == 8:
                    cut_diagonal(0)
                if t < NT:
                    dve.wait_ge(hi_ready, t + 1)
                    if t >= 2:
                        dve.wait_ge(lo_ready, t - 1)
                    nc.vector.tensor_tensor(rest[t % 2], nodes[:, t, :], xpart[0][:, t, :], ALU.subtract
                                            ).then_inc(rest_ready, 1)
                if t >= 1:
                    dve.wait_ge(mid_ready, t)
                    nc.vector.tensor_tensor(xpart[2][:, t - 1, :], rest[(t - 1) % 2], xpart[1][:, t - 1, :],
                                            ALU.subtract).then_inc(lo_ready, 1)

            for t in range(NT):
                if 2 <= t + 1 < NT:
                    mask_code(t + 1)
                if t >= 1:
                    cut_diagonal(t)
                key_tile(t)
                neighbours(t)
            dve.wait_ge(rownum_ready, 1)
            nc.vector.tensor_copy(ell[:, :, KMAX + 1], rownum[:, :].to_broadcast([P, NT]))
            for k in range(2):
                dve.wait_ge(prods_ready, FT * (k + 1))
                nc.vector.tensor_reduce(wcat[:, :, D + k * HEADS:D + (k + 1) * HEADS],
                                        prods[:, k, :, :].rearrange("p t (h d) -> p t h d", h=HEADS), AX_X, ALU.add)
            dve.wait_ge(first_used, NT)
            nc.vector.tensor_tensor(ends[:, :], count[:, :], ell[:, :, KMAX], ALU.add)
            dve.wait_ge(gathered, 16 * ECOLS)
            nc.vector.tensor_scalar(met[:, :], got[:, :], 1.0, None, ALU.is_equal).then_inc(met_ready, 1)
            dve.wait_ge(col_full, 1)
            nc.vector.tensor_copy(colsum[:, :], DG[0:ECOLS, 16:17]).then_inc(col_ready, 1)
            dve.wait_ge(total_full, 1)
            nc.vector.tensor_scalar(flags[0:1, 0:1], DG[0:1, 17:18], float(SLOTS), None, ALU.is_le)

        @block.tensor
        def _(pe):
            pe.wait_ge(ident_done, 1)

            def flip(t, k):
                pe.wait_ge(code_ready, t + 3)
                pe.wait_ge(near0_ready, t + 1)
                for j in range(NT):
                    last = nc.tensor.transpose(MT[k][:, j * P:(j + 1) * P], codet[k][:, j * P:(j + 1) * P], identb[:, :])
                last.then_inc(flipped, 1)

            def mix(t, k):
                pe.wait_ge(diag_off, t + 1)
                pe.wait_ge(y_used, t + 1)
                for j in range(NT):
                    nc.tensor.matmul(DG[:, t:t + 1], near0T[:, j, t * P:(t + 1) * P], onesb[:, :], start=(j == 0),
                                     stop=(j == NT - 1), skip_group_check=True)
                for n, ready in enumerate((hi_ready, mid_ready, lo_ready)):
                    pe.wait_ge(ready, NT)
                    for j in range(NT):
                        last = nc.tensor.matmul(TP[:, k, :], near0T[:, j, t * P:(t + 1) * P], xpart[n][:, j, :],
                                                start=(j == 0 and n == 0), stop=(j == NT - 1 and n == 2))
                last.then_inc(y_full, 1)

            def first_slots(t):
                pe.wait_ge(count_ready, t + 1)
                if t >= 1:
                    pe.wait_ge(spanned, 3 * t)
                nc.tensor.matmul(TP[:, 2, 16 + t:17 + t], before[:, :], count[:, t:t + 1], start=True, stop=True
                                 ).then_inc(first_full, 1)

            pe.sem_inc(flipped, 2)
            flip(0, 0)
            pe.wait_ge(bias_in, 80)
            nc.tensor.transpose(TP[:, 2, 0:13], brow[:, :], ident[0:13, 0:13]).then_inc(tp_full, 1)
            pe.wait_ge(tp_used, 1)
            for t in range(NT):
                if t + 1 < NT:
                    flip(t + 1, (t + 1) % 2)
                if t >= 1:
                    first_slots(t - 1)
                if t == NT - 1:
                    first_slots(t)
                mix(t, t % 2)
            pe.wait_ge(deg_ready, 1)
            pe.wait_ge(met_ready, 1)
            nc.tensor.matmul(DG[0:ECOLS, 16:17], met[:, :], ones[0:EROWS, 0:1], start=True, stop=True
                             ).then_inc(col_full, 1)
            pe.wait_ge(col_ready, 1)
            nc.tensor.matmul(DG[0:1, 17:18], colsum[:, :], ones[0:ECOLS, 0:1], start=True, stop=True
                             ).then_inc(total_full, 1)


def slot_mask(nc, act, v, number, dist, made, t):
    slotT, span = v["slotT"], v["span"]
    if t:
        act.wait_ge(made, 3 * t)
    nc.scalar.activation(dist, number, ACT.Abs, bias=span[:, 0, t:t + 1]).then_inc(made, 1)
    act.wait_ge(made, 3 * t + 1)
    nc.scalar.activation(dist, dist, ACT.Relu, scale=-1.0, bias=span[:, 1, t:t + 1]).then_inc(made, 1)
    act.wait_ge(made, 3 * t + 2)
    nc.scalar.activation(slotT[:, t, :], dist, ACT.Sign).then_inc(made, 1)


def flip_blocks(nc, pe, jobs, banks, ident, full, used):
    for n, (blocks, dst) in enumerate(jobs):
        if n >= len(banks):
            pe.wait_ge(used, n - len(banks) + 1)
        for k, b in enumerate(blocks):
            last = nc.tensor.transpose(banks[n % len(banks)][:, k * P:(k + 1) * P], b, ident[:, :])
        last.then_inc(full, 1)


def keep_blocks(nc, act, jobs, banks, full, used):
    for n, (blocks, dst) in enumerate(jobs):
        act.wait_ge(full, n + 1)
        nc.scalar.copy(dst, banks[n % len(banks)][:, 0:dst.shape[-1]]).then_inc(used, 1)


def load_qk(v, queue, wq_in):
    queue.dma_start(v["qnat"], v["Wq"].rearrange("(t p) f -> p t f", p=P)).then_inc(wq_in, 16)
    queue.dma_start(v["knat"], v["Wk"].rearrange("(t p) f -> p t f", p=P)).then_inc(wq_in, 16)


def load_dense_weights(v, queue, w_in):
    queue.dma_start(v["w1n"], v["W1"].rearrange("(t p) f -> p t f", p=P)).then_inc(w_in, 16)
    queue.dma_start(v["w2n"], v["W2"]).then_inc(w_in, 16)
    queue.dma_start(v["w3n"], v["W3"].rearrange("(t p) f -> p t f", p=P)).then_inc(w_in, 16)
    queue.dma_start(v["w4n"], v["W4"].rearrange("(t p) f -> p t f", p=P)).then_inc(w_in, 16)


def dense_weights(nc, sem, v):
    with ExitStack() as ctx:
        w_in, full, used = (sem(ctx, n) for n in ("dw_w_in", "dw_full", "dw_used"))
        B = [ctx.enter_context(nc.psum_tensor(f"DW{k}", [P, 512], F32)) for k in range(2)]
        block = ctx.enter_context(nc.Block())

        @block.sync
        def _(sp):
            load_dense_weights(v, sp, w_in)

        @block.tensor
        def _(pe):
            pe.wait_ge(w_in, 64)
            flip_blocks(nc, pe, v["mlp_jobs"], B, v["ident"], full, used)

        @block.scalar
        def _(act):
            keep_blocks(nc, act, v["mlp_jobs"], B, full, used)


def dense_prep(nc, sem, v, layer):
    x, adj, adj_dram, edge_dram = v["x"], v["adj"], v["adj_dram"], v["edge_dram"]
    nodes, featT, x1, qk4, ident, bias, qTw, kTw, esd = (v[k] for k in (
        "nodes", "featT", "x1", "qk4", "ident", "bias", "qTw", "kTw", "esd"))
    src = nodes if layer == 0 else x1
    zeros = v["work"][:, 0:N]
    with ExitStack() as ctx:
        def S(name):
            return sem(ctx, f"dp{layer}_" + name)
        TP = ctx.enter_context(nc.psum_tensor(f"TPd{layer}", [P, 3, 512], F32))
        QP = ctx.enter_context(nc.psum_tensor(f"QPd{layer}", [P, 2, 512], F32))
        EP = ctx.enter_context(nc.psum_tensor(f"EPd{layer}", [P, 512], F32))
        WB = [ctx.enter_context(nc.psum_tensor(f"WBd{layer}{k}", [P, 512], F32)) for k in range(2)]
        (copied, zero_done, padded, zeroed, scattered, tp_full, tp_used, qp_full, qp_used, e_full, e_used, sd_out,
         x1_in, wq_in, w_full, w_used) = (S(n) for n in (
            "copied", "zero_done", "padded", "zeroed", "scattered", "tp_full", "tp_used", "qp_full", "qp_used",
            "e_full", "e_used", "sd_out", "x1_in", "wq_in", "w_full", "w_used"))
        jobs = [(f, t0, k) for f in range(FT) for t0, k in TG]
        qkjobs = [(a, o, c, w) for a in range(2) for o in range(FT) for c, w in ((0, 512), (512, 512), (1024, 384))]
        sd = v["work"][0:2 * HEADS, 2 * N:3 * N]
        block = ctx.enter_context(nc.Block())

        @block.sync
        def _(sp):
            if layer == 1:
                load_x1(v, sp, [x1_in] * NT)
            else:
                load_qk(v, sp, wq_in)
            sp.dma_start(adj_dram[0:N, :], adj).then_inc(copied, 16)
            sp.wait_ge(zero_done, 1)
            sp.dma_start(adj_dram[N:NP, :], zeros[0:NP - N, :]).then_inc(padded, 16)
            if layer == 0:
                for t in range(NT):
                    sp.dma_start(edge_dram[t * P:(t + 1) * P, :], zeros).then_inc(zeroed, 16)
            else:
                sp.wait_ge(e_used, len(CH))
                sp.dma_start(v["sd_dram"], sd).then_inc(sd_out, 16)
                sp.wait_ge(sd_out, 16)
            sp.wait_ge(copied, 16)
            sp.wait_ge(padded, 16)

        @block.vector
        def _(dve):
            nc.vector.memset(zeros, 0.0).then_inc(zero_done, 1)

        @block.gpsimd
        def _(pool):
            if layer == 0:
                pool.wait_ge(zeroed, 16 * NT)
                for c in range(ECOLS):
                    if c:
                        pool.wait_ge(scattered, 16 * c)
                    nc.gpsimd.indirect_dma_start(
                        out=edge_dram.rearrange("a (b k) -> (a b) k", k=1),
                        out_offset=bass.IndirectOffsetOnAxis(ap=v["eidx"][:, c:c + 1].bitcast(U32), axis=0),
                        in_=v["ones"][0:EROWS, 0:1], in_offset=None, bounds_check=N * N - 1, oob_is_err=False
                    ).then_inc(scattered, 16)
                pool.wait_ge(scattered, 16 * ECOLS)

        @block.scalar
        def _(act):
            if layer == 0:
                keep_blocks(nc, act, v["qk_jobs"], WB, w_full, w_used)
            for n, (f, t0, k) in enumerate(jobs):
                act.wait_ge(tp_full, n + 1)
                nc.scalar.copy(featT[:, f, t0 * P:(t0 + k) * P], TP[:, n % 3, 0:k * P]).then_inc(tp_used, 1)
            if layer == 0:
                for n, (a, o, c, w) in enumerate(qkjobs):
                    act.wait_ge(qp_full, n + 1)
                    nc.scalar.activation(qk4[:, a, o, c:c + w], QP[:, n % 2, 0:w], ACT.Identity,
                                         bias=bias[:, 4 * a + o:4 * a + o + 1]).then_inc(qp_used, 1)
            else:
                for n, (c, w) in enumerate(CH):
                    act.wait_ge(e_full, n + 1)
                    nc.scalar.copy(sd[:, c:c + w], TP[0:2 * HEADS, n, 0:w]).then_inc(e_used, 1)
                for t in range(NT):
                    act.wait_ge(qp_full, t + 1)
                    nc.scalar.copy(nodes[:, t, :], QP[:, t % 2, :]).then_inc(qp_used, 1)
                act.wait_ge(qp_full, NT + 1)
                nc.scalar.copy(esd[:, 0:NT, :],
                               EP[:, 0:NT * 2 * HEADS].rearrange("p (t a) -> p t a", t=NT))

        @block.tensor
        def _(pe):
            if layer == 0:
                pe.wait_ge(wq_in, 32)
                flip_blocks(nc, pe, v["qk_jobs"], WB, ident, w_full, w_used)
            else:
                pe.wait_ge(x1_in, 16 * NT)
            for n, (f, t0, k) in enumerate(jobs):
                if n >= 3:
                    pe.wait_ge(tp_used, n - 2)
                for j in range(k):
                    last = nc.tensor.transpose(TP[:, n % 3, j * P:(j + 1) * P], src[:, t0 + j, f * P:(f + 1) * P],
                                               ident[:, :])
                last.then_inc(tp_full, 1)
            pe.wait_ge(tp_used, len(jobs))
            if layer == 0:
                pe.wait_ge(w_used, len(v["qk_jobs"]))
                for n, (a, o, c, w) in enumerate(qkjobs):
                    if n >= 2:
                        pe.wait_ge(qp_used, n - 1)
                    for f in range(FT):
                        last = nc.tensor.matmul(QP[:, n % 2, 0:w], (qTw, kTw)[a][:, f, o * P:(o + 1) * P],
                                                featT[:, f, c:c + w], start=(f == 0), stop=(f == FT - 1))
                    last.then_inc(qp_full, 1)
            else:
                for n, (c, w) in enumerate(CH):
                    for f in range(FT):
                        last = nc.tensor.matmul(TP[0:2 * HEADS, n, 0:w], v["wcat"][:, f, D:], featT[:, f, c:c + w],
                                                start=(f == 0), stop=(f == FT - 1))
                    last.then_inc(e_full, 1)
                for t in range(NT):
                    if t >= 2:
                        pe.wait_ge(qp_used, t - 1)
                    rows = featT[:, :, t * P:(t + 1) * P]
                    for f in range(FT):
                        last = nc.tensor.matmul(QP[:, t % 2, :], rows[:, f, :], v["wcat"][:, f, 0:D],
                                                start=(f == 0), stop=(f == FT - 1))
                    last.then_inc(qp_full, 1)
                    for f in range(FT):
                        last = nc.tensor.matmul(EP[:, t * 2 * HEADS:(t + 1) * 2 * HEADS], rows[:, f, :],
                                                v["wcat"][:, f, D:],
                                                start=(f == 0), stop=(f == FT - 1))
                last.then_inc(qp_full, 1)


def load_x1(v, queue, x1_in, after=None):
    for t in range(NT):
        if after is not None:
            queue.wait_ge(after, t + 1)
        queue.dma_start(v["x1"][0:width(t), t, :], v["x1_dram"][t * P:t * P + width(t), :]).then_inc(x1_in[t], 16)


def records(nc, sem, v, sparse):
    nodes, featT, x1, qk, work, ident, before, ones, deg0, edges, met, colsum = (v[k] for k in (
        "nodes", "featT", "x1", "qk", "work", "ident", "before", "ones", "deg0", "edges", "met", "colsum"))
    wcat, stat, esd, small, ell, ends, allsum, flags, slotT, nbr, owner = (v[k] for k in (
        "wcat", "stat", "esd", "small", "ell", "ends", "allsum", "flags", "slotT", "nbr", "owner"))
    qTw, kTw, rec_dram, x1_dram = (v[k] for k in ("qTw", "kTw", "rec_dram", "x1_dram"))
    ff = featT[:, :, :].rearrange("p f n -> p (f n)")
    W = KMAX + 2
    HR = REC // 2
    CC = 16
    GW = 2 * CT * REC
    spare = {"qk": (qk, GW, 2 * FT * NP), "low": (work, 0, 4116), "high": (work, 8212, 3 * CT * REC)}
    taken = {k: a for k, (_, a, _) in spare.items()}

    def cut(where, w):
        buf, _, end = spare[where]
        taken[where] += w
        assert taken[where] <= end
        return buf[:, taken[where] - w:taken[where]]

    xT = [ff[:, k * D:(k + 1) * D].rearrange("p (f n) -> p f n", f=FT) for k in range(2)]
    xs, xo, ys, xsT, xoT, bqbc, bkbc, prod, gains = (ff[:, (2 + k) * D:(3 + k) * D] for k in range(9))
    parts = lambda a: a.rearrange("p (f s) -> p f s", f=FT)
    onehots = cut("qk", CC * P)
    t8d8 = cut("low", 2048)
    onehot = [b[0:EROWS, k * CC * P // 2:(k + 1) * CC * P // 2].bitcast(BF16).rearrange("p (c s) -> p c s", c=CC)
              for b in (onehots, t8d8) for k in range(2)]
    iota, adjrow = cut("qk", N), cut("qk", N)
    recs = onehots[:, 0:REC]
    table = onehots[:, REC:REC + NT * CT * W].rearrange("p (s w) -> p s w", w=W)
    t8 = t8d8[:, 0:1024].rearrange("p (h s) -> p h s", h=HEADS)
    d8 = t8d8[:, 1024:2048].rearrange("p (h s) -> p h s", h=HEADS)
    column = t8d8[:, 0:NT * CT * KMAX].rearrange("p (s k) -> p s k", k=KMAX)
    same, penal, keq, ub, eqm = (cut("low", P) for _ in range(5))
    c = cut("low", 112)
    sub, obj, used, key, dup, uniq, rep, cnt, deg, gain, far = (c[:, k:k + 1] for k in range(11))
    mv = c[:, 12:16]
    att, top, zsum, den = (c[:, 16 + 8 * k:24 + 8 * k] for k in range(4))
    ex3 = c[:, 48:72].rearrange("p (k h) -> p k h", k=3)
    fsum = c[:, 72:96].rearrange("p (k h) -> p k h", k=3)
    f3 = c[:, 96:99]
    sstats = c[:, 100:106]
    newton = c[:, 106:107]
    fd = cut("low", 2 * NT).rearrange("p (k t) -> p k t", k=2)
    slotnum, rank, rankno = cut("low", NT * CT), cut("low", NT * CT), cut("low", KMAX)
    colb = cut("high", EROWS)[0:ECOLS, :]
    ellb = cut("high", NT * W).bitcast(BF16).rearrange("p (t a w) -> p t a w", t=NT, a=2)
    stats = cut("high", 6 * NT).rearrange("p (t k) -> p t k", k=6)
    summed, lone, lones = cut("high", NT), cut("high", NT), cut("high", 1)
    ext8, ext, cnt2 = cut("high", 2 * HEADS), cut("high", 4)[0:HEADS, :], cut("high", 4)[0:1, :]
    mid8 = cut("high", HEADS)[0:HEADS, :]
    half = cut("high", 4)
    SG = [(s, min(512 // W, NT * CT - s)) for s in range(0, NT * CT, 512 // W)]
    name = "s_" if sparse else "b_"
    with ExitStack() as ctx:
        def S(n):
            return sem(ctx, name + n)
        sb = lambda n, shape, dt=F32: ctx.enter_context(nc.sbuf_tensor(name + n, shape, dt))
        place = sb("place", [EROWS, ECOLS])
        halves = sb("halves", [EROWS, ECOLS, 6], BF16)
        slotidx = sb("slotidx", [P, 3], I32)
        TP = ctx.enter_context(nc.psum_tensor(name + "TP", [P, 512], F32))
        WP = ctx.enter_context(nc.psum_tensor(name + "WP", [P, 2, 2, 512], F32))
        PA, PB, PC = (ctx.enter_context(nc.psum_tensor(name + n, [P, 512], F32)) for n in ("PA", "PB", "PC"))
        (fd_ready, scaled, normed, tp_full, tp_used, wh_full, wh_used, x1_out,
         rec_out, ell_ready, iota_ready, tab_full, tab_used, ext_ready, ext_full, lone_ready, lone_full,
         chain) = (S(n) for n in (
            "fd_ready", "scaled", "normed", "tp_full", "tp_used", "wh_full", "wh_used",
            "x1_out", "rec_out", "ell_ready", "iota_ready", "tab_full", "tab_used",
            "ext_ready", "ext_full", "lone_ready", "lone_full", "chain"))
        if sparse:
            wq_in = S("wq_in")
            (colb_ready, place_full, wqk_full, wqk_used, hot_ready, hot_used, idx_ready, rows_in, adj_in, bias_in,
             diag_ready, bc_full, uniq_ready, ub_full, xt_full, xt_ready, proj_full, d8_ready, att_full, args_ready,
             exp_ready, gain_ready, own_full, x1s_ready, st_full, st_ready, swh_full, swh_kept,
             srec_ready, halves_ready, scattered) = (S(n) for n in (
                "colb_ready", "place_full", "wqk_full", "wqk_used", "hot_ready", "hot_used", "idx_ready", "rows_in",
                "adj_in", "bias_in", "diag_ready", "bc_full", "uniq_ready", "ub_full", "xt_full", "xt_ready",
                "proj_full", "d8_ready", "att_full", "args_ready", "exp_ready", "gain_ready", "own_full",
                "x1s_ready", "st_full", "st_ready", "swh_full", "swh_kept", "srec_ready",
                "halves_ready", "scattered"))
            eqm_ready, ub_used = S("eqm_ready"), S("ub_used")
        w_in = S("w_in")
        aggr_done, var_ready, inv_ready, half_ready = (S(n) for n in ("aggr_done", "var_ready", "inv_ready", "half_ready"))
        block = ctx.enter_context(nc.Block())

        @block.sync
        def _(sp):
            if sparse:
                load_qk(v, sp, wq_in)
                for n, dst in (("bq", bqbc), ("bk", bkbc)):
                    sp.dma_start(dst, v[n].rearrange("(a d) -> a d", a=1).to_broadcast([P, D])).then_inc(bias_in, 16)
                sp.wait_ge(wqk_used, len(v["qk_jobs"]))
            load_dense_weights(v, sp, w_in)
            for t in range(NT):
                w = width(t)
                sp.wait_ge(normed, t + 1)
                sp.dma_start(x1_dram[t * P:t * P + w, :], x1[0:w, t, :]).then_inc(x1_out, 16)
                sp.wait_ge(wh_used, t + 1)
                sp.dma_start(rec_dram[t * P:t * P + w, 0:D], nodes[0:w, t, :]).then_inc(rec_out, 16)
            sp.dma_start(rec_dram[0:NFULL * P, D:].rearrange("(t p) c -> p t c", p=P), esd[:, 0:NFULL, :]
                         ).then_inc(rec_out, 16)
            sp.dma_start(rec_dram[NFULL * P:N, D:], esd[0:LAST, NFULL, :]).then_inc(rec_out, 16)
            sp.wait_ge(w_in, 64)
            sp.wait_ge(x1_out, 16 * NT)
            sp.wait_ge(rec_out, 16 * (NT + 2))

        @block.gpsimd
        def _(pool):
            def count(dst, pattern, base=0, channel=0):
                nc.gpsimd.iota(dst, pattern=pattern, base=base, channel_multiplier=channel,
                               allow_small_or_imprecise_dtypes=True).then_inc(iota_ready, 1)

            def power(tiles, n):
                pool.wait_ge(var_ready, n)
                var, inv = ((stat[:, k, tiles[0]:tiles[0] + tiles[1]] for k in (1, 3)) if tiles else
                            (mv[:, 1:2], mv[:, 3:4]))
                nc.gpsimd.tensor_tensor(inv, var, half[:, 0:var.shape[-1]], ALU.pow).then_inc(inv_ready, 1)

            count(slotnum.rearrange("p (t c) -> p t c", t=NT), [[0, NT], [P, CT]], 0, 1)
            count(rankno, [[1, KMAX]])
            if sparse:
                count(iota, [[1, N]])
            nc.gpsimd.memset(half, -0.5).then_inc(half_ready, 1)
            pool.wait_ge(half_ready, 1)
            power(TG[0], 1)
            nc.gpsimd.memset(qk[:, 0:GW], 0.0)
            if not sparse:
                power(TG[1], 2)
                power(TG[2], 3)
                return
            power(TG[1], 2)
            pool.wait_ge(idx_ready, 1)
            for k, src, dst in ((0, v["x"], xs), (1, v["x"], xo), (0, v["y_dram"], ys)):
                nc.gpsimd.indirect_dma_start(
                    out=dst, out_offset=None, in_=src, in_offset=bass.IndirectOffsetOnAxis(
                        ap=slotidx[:, k:k + 1].bitcast(U32), axis=0),
                    bounds_check=N - 1, oob_is_err=False).then_inc(rows_in, 16)
            nc.gpsimd.indirect_dma_start(
                out=adjrow, out_offset=None, in_=v["adj"], in_offset=bass.IndirectOffsetOnAxis(
                    ap=slotidx[:, 0:1].bitcast(U32), axis=0),
                bounds_check=N - 1, oob_is_err=False).then_inc(adj_in, 16)
            power(TG[2], 3)
            power(None, 4)
            pool.wait_ge(x1s_ready, 1)
            pool.wait_ge(x1_out, 16 * NT)
            nc.gpsimd.indirect_dma_start(
                out=x1_dram, out_offset=bass.IndirectOffsetOnAxis(ap=slotidx[:, 2:3].bitcast(U32), axis=0),
                in_=bqbc, in_offset=None, bounds_check=N - 1, oob_is_err=False).then_inc(scattered, 16)
            pool.wait_ge(srec_ready, 2)
            pool.wait_ge(rec_out, 16 * (NT + 2))
            nc.gpsimd.indirect_dma_start(
                out=rec_dram, out_offset=bass.IndirectOffsetOnAxis(ap=slotidx[:, 2:3].bitcast(U32), axis=0),
                in_=recs, in_offset=None, bounds_check=N - 1, oob_is_err=False).then_inc(scattered, 16)
            pool.wait_ge(scattered, 32)

        @block.scalar
        def _(act):
            def scale(t):
                nc.scalar.activation(x1[:, t, :], x1[:, t, :], ACT.Copy, scale=fd[:, 0, t:t + 1]).then_inc(scaled, 1)

            def keep_flip(t):
                act.wait_ge(tp_full, t + 1)
                nc.scalar.copy(xT[t % 2].rearrange("p f n -> p (f n)"), TP[:, :]).then_inc(tp_used, 1)

            def keep_record(low, high, dst, t):
                nc.scalar.copy(dst[:, 0:HR], low[:, 0:HR])
                nc.scalar.copy(dst[:, HR:D], high[:, 0:D - HR])
                return nc.scalar.copy(esd[:, t, :], high[:, D - HR:HR])

            def wh(t):
                if t + 1 < NT:
                    keep_flip(t + 1)
                act.wait_ge(wh_full, t + 1)
                keep_record(WP[:, t % 2, 0, :], WP[:, t % 2, 1, :], nodes[:, t, :], t).then_inc(wh_used, 1)

            def keep_table(n):
                s0, k = SG[n]
                act.wait_ge(tab_full, n + 1)
                nc.scalar.copy(table[:, s0:s0 + k, :], PC[:, 0:k * W].rearrange("p (s w) -> p s w", w=W)
                               ).then_inc(tab_used, 1)

            if sparse:
                act.wait_ge(fd_ready, 1)
                for t in range(TG[0][1]):
                    scale(t)
                keep_blocks(nc, act, v["qk_jobs"], (PB, PC), wqk_full, wqk_used)
            keep_flip(0)
            wh(0)
            if sparse:
                for t in range(TG[1][0], TG[2][0]):
                    scale(t)
            wh(1)
            if sparse:
                for t in range(TG[2][0], NT):
                    scale(t)
            wh(2)
            wh(3)
            if sparse:
                for k, (dst, bank) in enumerate(((xsT, PA), (xoT, PC))):
                    act.wait_ge(xt_full, k + 1)
                    nc.scalar.copy(dst, bank[:, :]).then_inc(xt_ready, 1)
            for t in (4, 5, 6, 7):
                wh(t)
            keep_table(0)
            if sparse:
                act.wait_ge(args_ready, 1)
                nc.scalar.activation(t8, t8, ACT.Exp)
                nc.scalar.activation(ex3, ex3, ACT.Exp).then_inc(exp_ready, 1)
            wh(8)
            keep_table(1)
            wh(9)
            keep_table(2)
            if sparse:
                act.wait_ge(st_full, 1)
                nc.scalar.copy(xsT, PA[:, :]).then_inc(st_ready, 1)
                act.wait_ge(swh_full, 1)
                keep_record(PB[:, :], PC[:, :], recs, NT).then_inc(srec_ready, 1)
                act.wait_ge(srec_ready, 1)
                nc.scalar.copy(recs[:, D:], esd[:, NT, :]).then_inc(srec_ready, 1)
            wh(10)

        @block.tensor
        def _(pe):
            def flip(t):
                pe.wait_ge(normed, t + 1)
                if t >= 1:
                    pe.wait_ge(tp_used, t)
                for f in range(FT):
                    last = nc.tensor.transpose(TP[:, f * P:(f + 1) * P], x1[:, t, f * P:(f + 1) * P], ident[:, :])
                last.then_inc(tp_full, 1)

            def project(rows, bank, half):
                for f in range(FT):
                    last = nc.tensor.matmul(bank[:, 0:HR], rows[:, f, :], wcat[:, f, half * HR:(half + 1) * HR],
                                            start=(f == 0), stop=(f == FT - 1))
                return last

            def wh(t):
                pe.wait_ge(tp_used, t + 1)
                if t >= 2:
                    pe.wait_ge(wh_used, t - 1)
                project(xT[t % 2], WP[:, t % 2, 0, :], 0)
                if t + 1 < NT:
                    flip(t + 1)
                project(xT[t % 2], WP[:, t % 2, 1, :], 1).then_inc(wh_full, 1)

            def make_table(n):
                s0, k = SG[n]
                if n >= 1:
                    pe.wait_ge(tab_used, n)
                for i in range(k):
                    t, b = (s0 + i) // CT, (s0 + i) % CT
                    for a in range(2):
                        last = nc.tensor.matmul(PC[:, i * W:(i + 1) * W], slotT[:, t, b * P:(b + 1) * P],
                                                ellb[:, t, a, :], start=(a == 0), stop=(a == 1))
                last.then_inc(tab_full, 1)

            if sparse:
                pe.wait_ge(colb_ready, 1)
                nc.tensor.matmul(PA[0:EROWS, 0:ECOLS], before[0:EROWS, 0:EROWS], met[:, :], start=True, stop=False)
                nc.tensor.matmul(PA[0:EROWS, 0:ECOLS], colb, before[0:ECOLS, 0:ECOLS], start=False, stop=True
                                 ).then_inc(place_full, 1)
                pe.wait_ge(wq_in, 32)
                flip_blocks(nc, pe, v["qk_jobs"], (PB, PC), ident, wqk_full, wqk_used)
            flip(0)
            wh(0)
            if sparse:
                pe.wait_ge(wqk_used, len(v["qk_jobs"]))
                pe.wait_ge(halves_ready, 1)
                for n in range(ECOLS // CC):
                    if n == 4:
                        wh(1)
                    pe.wait_ge(hot_ready, n + 1)
                    for k in range(CC):
                        e = n * CC + k
                        last = nc.tensor.matmul(PB[:, 0:6], onehot[n % 4][:, k, :], halves[:, e, :], start=(e == 0),
                                                stop=(e == ECOLS - 1))
                    last.then_inc(hot_used, 1)
            else:
                wh(1)
            wh(2)
            if sparse:
                pe.wait_ge(diag_ready, 1)
                nc.tensor.matmul(PA[:, 0:2 * P], ones[:, :], d8[:, 0:2, :].rearrange("p h s -> p (h s)"), start=True,
                                 stop=True).then_inc(bc_full, 1)
            wh(3)
            if sparse:
                pe.wait_ge(uniq_ready, 1)
                nc.tensor.matmul(PB[:, 0:P], ones[:, :], d8[:, 2, :], start=True, stop=True).then_inc(ub_full, 1)
                pe.wait_ge(rows_in, 48)
                for k, (src, bank) in enumerate(((xs, PA), (xo, PC))):
                    if k == 0:
                        pe.wait_ge(eqm_ready, 1)
                    for f in range(FT):
                        last = nc.tensor.transpose(bank[:, f * P:(f + 1) * P], src[:, f * P:(f + 1) * P], ident[:, :])
                    last.then_inc(xt_full, 1)
            wh(4)
            if sparse:
                pe.wait_ge(xt_ready, 2)
                pe.wait_ge(ub_used, 1)
                for l, w, bank in ((xsT, qTw, PA), (xoT, kTw, PB)):
                    for f in range(FT):
                        last = nc.tensor.matmul(bank[:, :], parts(l)[:, f, :], w[:, f, :], start=(f == 0),
                                                stop=(f == FT - 1))
                    last.then_inc(proj_full, 1)
            wh(5)
            if sparse:
                pe.wait_ge(d8_ready, 1)
                d8f = d8.rearrange("p h s -> p (h s)")
                for k, bank in enumerate((PA, PB)):
                    last = nc.tensor.matmul(bank[:, :], ones[:, :], d8f[:, k * 512:(k + 1) * 512], start=True,
                                            stop=True)
                last.then_inc(att_full, 1)
            wh(6)
            wh(7)
            pe.wait_ge(ell_ready, 1)
            make_table(0)
            wh(8)
            make_table(1)
            if sparse:
                pe.wait_ge(gain_ready, 1)
                nc.tensor.matmul(PA[:, :], eqm, gains, start=True, stop=True).then_inc(own_full, 1)
            wh(9)
            make_table(2)
            if sparse:
                pe.wait_ge(x1s_ready, 1)
                for f in range(FT):
                    last = nc.tensor.transpose(PA[:, f * P:(f + 1) * P], bqbc[:, f * P:(f + 1) * P], ident[:, :])
                last.then_inc(st_full, 1)
                pe.wait_ge(st_ready, 1)
                pe.wait_ge(tab_used, len(SG))
                project(parts(xsT), PB, 0)
                project(parts(xsT), PC, 1).then_inc(swh_full, 1)
            wh(10)
            pe.wait_ge(ext_ready, 1)
            for k in range(2):
                last = nc.tensor.transpose(PB[0:HEADS, k * P:(k + 1) * P], ext8[:, k * HEADS:(k + 1) * HEADS],
                                           ident[:, :])
            last.then_inc(ext_full, 1)
            pe.wait_ge(lone_ready, 1)
            nc.tensor.matmul(PB[:, 256:264], ones[0:HEADS, :], mid8, start=True, stop=True)
            nc.tensor.matmul(PB[0:1, 264:265], ext[:, 2:3], ones[0:HEADS, 0:1], start=True, stop=True)
            nc.tensor.matmul(PB[0:1, 265:266], lones, ones[:, 0:1], start=True, stop=True).then_inc(lone_full, 1)

        @block.vector
        def _(dve):
            links = [0]

            def link(ins):
                links[0] += 1
                ins.then_inc(chain, 1)
                dve.wait_ge(chain, links[0])

            TT, TS, STT = nc.vector.tensor_tensor, nc.vector.tensor_scalar, nc.vector.scalar_tensor_tensor
            RED = nc.vector.tensor_reduce

            powers = [0]

            def invert(inv, var, tmp):
                n = powers[0] = powers[0] + 1
                TS(var, var, EPS, None, ALU.add).then_inc(var_ready, 1)
                dve.wait_ge(inv_ready, n)
                link(TT(tmp, inv, inv, ALU.mult))
                link(TT(tmp, tmp, var, ALU.mult))
                link(TS(tmp, tmp, -0.5, 1.5, ALU.mult, ALU.add))
                link(TT(inv, inv, tmp, ALU.mult))

            def norm(g):
                t0, k = TG[g]
                for t in range(t0, t0 + k):
                    if sparse:
                        dve.wait_ge(scaled, t + 1)
                        link(STT(x1[:, t, :], nodes[:, t, :], fd[:, 1, t:t + 1], x1[:, t, :], ALU.mult, ALU.add))
                    link(nc.vector.bn_stats(stats[:, t, :], x1[:, t, :]))
                    nc.vector.bn_aggr(stat[:, 0:2, t], stats[:, t, :]).then_inc(aggr_done, 1)
                dve.wait_ge(aggr_done, t0 + k)
                var = stat[:, 1, t0:t0 + k]
                invert(stat[:, 3, t0:t0 + k], var, small[:, 0:k])
                for t in range(t0, t0 + k):
                    TS(x1[:, t, :], x1[:, t, :], stat[:, 0, t:t + 1], stat[:, 3, t:t + 1], ALU.subtract, ALU.mult
                       ).then_inc(normed, 1)

            if sparse:
                W0 = 1.0 - 2.0 ** -23
                link(TS(fd[:, 1, :], deg0[:, :], W0, 1.0, ALU.mult, ALU.add))
                link(nc.vector.reciprocal(fd[:, 1, :], fd[:, 1, :]))
                link(TS(fd[:, 0, :], fd[:, 1, :], W0, None, ALU.mult))
                TS(fd[:, 1, :], fd[:, 1, :], 1.0, None, ALU.add).then_inc(fd_ready, 1)
                dve.wait_ge(fd_ready, 1)
                TS(colb, ones[0:ECOLS, 0:EROWS], colsum[:, 0:1], None, ALU.mult).then_inc(colb_ready, 1)
            link(nc.vector.tensor_copy(ellb[:, :, 0, :], ell[:, :, :]))
            TT(ellb[:, :, 1, :], ell[:, :, :], ellb[:, :, 0, :], ALU.subtract).then_inc(ell_ready, 1)
            norm(0)
            if sparse:
                ends4 = halves[:, :, :].rearrange("p e (k a) -> p e k a", a=2)
                link(nc.vector.tensor_copy(ends4[:, :, :, 0], edges[:, :, :]))
                TT(ends4[:, :, :, 1], edges[:, :, :], ends4[:, :, :, 0], ALU.subtract).then_inc(halves_ready, 1)
                dve.wait_ge(place_full, 1)
                link(STT(place[:, :], PA[0:EROWS, 0:ECOLS], 1.0, met[:, :], ALU.add, ALU.mult))
                link(TS(place[:, :], place[:, :], -1.0, None, ALU.add))
                dve.wait_ge(iota_ready, 3)
                nums = iota[0:EROWS, 0:P].rearrange("p (c s) -> p c s", c=1).to_broadcast([EROWS, CC, P])
                for n in range(ECOLS // CC):
                    if n >= 4:
                        dve.wait_ge(hot_used, n - 3)
                    at = place[:, n * CC:(n + 1) * CC].rearrange("p (c s) -> p c s", s=1).to_broadcast([EROWS, CC, P])
                    TT(onehot[n % 4], nums, at, ALU.is_equal).then_inc(hot_ready, 1)
            norm(1)
            if sparse:
                dve.wait_ge(hot_used, ECOLS // CC)
                link(RED(c[:, 0:3], PB[:, 0:6].rearrange("p (k a) -> p k a", a=2), AX_X, ALU.add))
                nc.vector.tensor_copy(slotidx[:, 0:2], c[:, 0:2]).then_inc(idx_ready, 1)
                link(STT(key, sub, float(N), obj, ALU.mult, ALU.add))
                link(TS(d8[:, 0, :], ident[:, :], key, None, ALU.mult))
                TS(d8[:, 1, :], ident[:, :], sub, None, ALU.mult).then_inc(diag_ready, 1)
                dve.wait_ge(bc_full, 1)
                link(TT(ub, before[:, :], ident[:, :], ALU.add))
                link(TS(ub, ub, -1.0, 1.0, ALU.mult, ALU.add))
                link(STT(keq, PA[:, 0:P], key, ub, ALU.is_equal, ALU.mult))
                link(RED(dup, keq, AX_X, ALU.max))
                link(TS(uniq, dup, 0.5, used, ALU.is_lt, ALU.mult))
                TS(d8[:, 2, :], ident[:, :], uniq, None, ALU.mult).then_inc(uniq_ready, 1)
                TS(eqm, PA[:, P:2 * P], sub, None, ALU.is_equal).then_inc(eqm_ready, 1)
                dve.wait_ge(ub_full, 1)
                dve.wait_ge(eqm_ready, 1)
                TT(same, eqm, PB[:, 0:P], ALU.mult).then_inc(ub_used, 1)
                dve.wait_ge(ub_used, 1)
                link(TT(keq, same, ub, ALU.mult))
                link(RED(dup, keq, AX_X, ALU.max))
                link(TS(rep, dup, 0.5, uniq, ALU.is_lt, ALU.mult))
                link(STT(far, sub, -float(GONE), rep, ALU.add, ALU.mult))
                link(TS(slotidx[:, 2:3], far, float(GONE), None, ALU.add))
                link(RED(cnt, same, AX_X, ALU.add))
                link(TS(penal, same, -1.0, BIG, ALU.add, ALU.mult))
                dve.wait_ge(adj_in, 16)
                link(TS(adjrow, adjrow, 1.0, None, ALU.is_equal))
                link(STT(adjrow, iota, sub, adjrow, ALU.not_equal, ALU.mult, accum_out=deg))
            norm(2)
            if sparse:
                dve.wait_ge(bias_in, 32)
                dve.wait_ge(proj_full, 2)
                link(TT(bqbc, PA[:, :], bqbc, ALU.add))
                link(TT(bkbc, PB[:, :], bkbc, ALU.add))
                link(TT(prod, bqbc, bkbc, ALU.mult))
                link(RED(att, prod.rearrange("p (h d) -> p h d", h=HEADS), AX_X, ALU.add))
                link(TS(att, att, DK ** -0.5, uniq, ALU.mult, ALU.mult))
                wide = lambda a: a.rearrange("p (h s) -> p h s", h=1).to_broadcast([P, HEADS, P])
                deep = lambda a: a.rearrange("p (h s) -> p h s", s=1).to_broadcast([P, HEADS, P])
                TT(d8, wide(ident[:, :]), deep(att), ALU.mult).then_inc(d8_ready, 1)
                dve.wait_ge(att_full, 1)
                for k, bank in enumerate((PA, PB)):
                    half = slice(k * HEADS // 2, (k + 1) * HEADS // 2)
                    link(TT(t8[:, half, :], bank[:, :].rearrange("p (h s) -> p h s", s=P),
                            same.rearrange("p (h s) -> p h s", h=1).to_broadcast([P, HEADS // 2, P]), ALU.mult))
                link(TT(t8, t8, wide(penal), ALU.add))
                link(RED(top, t8, AX_X, ALU.max))
                link(TS(top, top, 1.0e-7, None, ALU.max))
                link(TT(t8, t8, deep(top), ALU.subtract))
                link(TT(ex3[:, 0, :], att, top, ALU.subtract))
                link(TS(ex3[:, 1, :], top, -1.0, None, ALU.mult))
                TS(ex3[:, 2, :], top, -1.0, 1.0e-7, ALU.mult, ALU.add).then_inc(args_ready, 1)
                dve.wait_ge(exp_ready, 1)
                link(RED(zsum, t8, AX_X, ALU.add))
                link(TT(deg, deg, cnt, ALU.subtract))
                link(TT(zsum, zsum, ex3[:, 2, :], ALU.add))
                link(STT(den, ex3[:, 1, :], deg, zsum, ALU.mult, ALU.add))
                link(nc.vector.reciprocal(den, den))
                link(TS(den, den, 1.0 / HEADS, None, ALU.mult))
                link(TT(fsum, ex3, den.rearrange("p (k h) -> p k h", k=1).to_broadcast([P, 3, HEADS]), ALU.mult))
                link(RED(f3, fsum, AX_X, ALU.add))
                link(TT(gain, f3[:, 0:1], f3[:, 1:2], ALU.subtract))
                link(TT(gain, gain, uniq, ALU.mult))
                TS(gains, xo, gain, None, ALU.mult).then_inc(gain_ready, 1)
                link(STT(prod, xs, f3[:, 2:3], xs, ALU.mult, ALU.add))
                link(STT(prod, ys, f3[:, 1:2], prod, ALU.mult, ALU.add))
                dve.wait_ge(own_full, 1)
                link(TT(prod, PA[:, :], prod, ALU.add))
                link(nc.vector.bn_stats(sstats, prod))
                link(nc.vector.bn_aggr(mv[:, 0:2], sstats))
                invert(mv[:, 3:4], mv[:, 1:2], newton)
                TS(bqbc, prod, mv[:, 0:1], mv[:, 3:4], ALU.subtract, ALU.mult).then_inc(x1s_ready, 1)
            dve.wait_ge(iota_ready, 2)
            dve.wait_ge(tab_used, len(SG))
            SHAPE = [P, NT * CT, KMAX]
            link(TT(rank, slotnum, table[:, :, KMAX], ALU.subtract))
            link(TT(column, rankno.rearrange("p (s k) -> p s k", s=1).to_broadcast(SHAPE),
                    rank.rearrange("p (s k) -> p s k", k=1).to_broadcast(SHAPE), ALU.is_equal))
            link(TT(column, column, table[:, :, 0:KMAX], ALU.mult))
            link(RED(rank, column, AX_X, ALU.add))
            TS(nbr[:, :, :].rearrange("p t c -> p (t c)"), rank, -1.0, float(GONE), ALU.mult, ALU.add)
            nc.vector.tensor_copy(owner[:, :, :].rearrange("p t c -> p (t c)"), table[:, :, KMAX + 1])
            link(RED(summed, ell[:, :, 0:KMAX], AX_X, ALU.add))
            link(TT(summed, summed, allsum[:, :], ALU.not_equal))
            link(TS(lone, allsum[:, :], 0.0, None, ALU.is_le))
            link(TT(lone, lone, summed, ALU.add))
            link(TS(summed[:, 0:NFULL], ends[:, 0:NFULL], float(CT * P), None, ALU.is_gt))
            link(TS(summed[:, NFULL:], ends[:, NFULL:], float(CLAST * P), None, ALU.is_gt))
            link(TT(lone, lone, summed, ALU.add))
            link(RED(lones, lone, AX_X, ALU.add))
            dve.wait_ge(wh_used, NT)
            if sparse:
                dve.wait_ge(srec_ready, 1)
            byhead = esd[:, 0:NT + sparse, HEADS:].rearrange("p t h -> p h t")
            RED(ext8[:, 0:HEADS], byhead, AX_X, ALU.max)
            RED(ext8[:, HEADS:], byhead, AX_X, ALU.min).then_inc(ext_ready, 1)
            dve.wait_ge(ext_full, 1)
            link(RED(ext[:, 0:1], PB[0:HEADS, 0:P], AX_X, ALU.max))
            link(RED(ext[:, 1:2], PB[0:HEADS, P:2 * P], AX_X, ALU.min))
            link(TT(ext[:, 2:3], ext[:, 0:1], ext[:, 1:2], ALU.subtract))
            link(TS(ext[:, 2:3], ext[:, 2:3], SPREAD, None, ALU.is_le))
            TS(mid8, ident[0:HEADS, 0:HEADS], ext[:, 0:1], None, ALU.mult).then_inc(lone_ready, 1)
            dve.wait_ge(lone_full, 1)
            nc.vector.tensor_copy(small[:, 24:32], PB[:, 256:264])
            link(nc.vector.tensor_copy(cnt2[:, 0:2], PB[0:1, 264:266]))
            link(TS(cnt2[:, 0:1], cnt2[:, 0:1], float(HEADS), None, ALU.is_ge))
            link(TS(cnt2[:, 1:2], cnt2[:, 1:2], 0.0, None, ALU.is_le))
            TT(flags[0:1, 1:2], cnt2[:, 0:1], cnt2[:, 1:2], ALU.mult)


def layer0_dense(nc, sem, v):
    nodes, x1, qk, ident, work, small, featT = (v[k] for k in (
        "nodes", "x1", "qk4", "ident", "work", "small", "featT"))
    spare = featT[:, :, :].rearrange("p f n -> p (f n)")
    edge_dram = v["edge_dram"]
    o = 0
    def cut(w):
        nonlocal o
        o += w
        return work[:, o - w:o]
    T = [cut(N), cut(N)]
    mask, acc, adjt = spare[:, 0:NP], spare[:, NP:2 * NP], spare[:, 2 * NP:2 * NP + N]
    edge = cut(N)
    qs = cut(FT * P).rearrange("p (f n) -> p f n", f=FT)
    factT = cut(NP)
    with ExitStack() as ctx:
        def S(name):
            return sem(ctx, "l0_" + name)
        SP_ = [ctx.enter_context(nc.psum_tensor(f"S{k}", [P, 3, 512], F32)) for k in range(2)]
        Y = ctx.enter_context(nc.psum_tensor("Y", [P, D], F32))
        Sf = [s[:, :, :].rearrange("p b n -> p (b n)") for s in SP_]
        edge_in, q_staged, scores, masked, top, prob, accd, transposed, copied, summed, done, mask_ready, chain = (
            S(n) for n in ("edge_in", "q_staged", "scores", "masked", "top", "prob", "accd", "transposed", "copied",
                           "summed", "done", "mask_ready", "chain"))
        nmax, den, rden = small[:, 0:8], small[:, 8:16], small[:, 16:24]
        block = ctx.enter_context(nc.Block())

        @block.sync
        def _(sp):
            with sp.Fori(0, NT) as t:
                sp.wait_ge(done, t + 1)
                sp.dma_start(edge, edge_dram[bass.ts(t, P), :]).then_inc(edge_in, 16)
                sp.dma_start(adjt, v["adj_dram"][bass.ts(t, P), :]).then_inc(edge_in, 16)

        @block.scalar
        def _(act):
            act.sem_inc(copied, 1)
            with act.Fori(0, NT) as t:
                act.wait_ge(summed, t + 1)
                nc.scalar.activation(qs, qk[:, 0, :, bass.ts(t, P)], ACT.Copy, scale=DK ** -0.5).then_inc(q_staged, 1)
                for h in range(HEADS):
                    act.wait_ge(top, t * HEADS + (h + 1))
                    nc.scalar.activation(T[h % 2], T[h % 2], ACT.Exp, bias=nmax[:, h:h + 1],
                                         accum_out=den[:, h:h + 1]).then_inc(prob, 1)
                act.wait_ge(transposed, t + 1)
                nc.scalar.copy(factT, Sf[0][:, 0:NP]).then_inc(copied, 1)

        @block.tensor
        def _(pe):
            pe.sem_inc(summed, 1)
            with pe.Fori(0, NT) as t:
                pe.wait_ge(q_staged, t + 1)
                pe.wait_ge(copied, t + 1)
                for h in range(HEADS):
                    if h >= 2:
                        pe.wait_ge(masked, t * HEADS + (h - 1))
                    r = DK * (h % 2)
                    for c, w in CH:
                        last = nc.tensor.matmul(Sf[h % 2][:, c:c + w], qs[r:r + DK, h // 2, :],
                                                qk[r:r + DK, 1, h // 2, c:c + w], start=True, stop=True)
                    last.then_inc(scores, 1)
                pe.wait_ge(accd, t + 1)
                for k in range(NT):
                    last = nc.tensor.transpose(Sf[0][:, k * P:(k + 1) * P], acc[:, k * P:(k + 1) * P], ident[:, :])
                last.then_inc(transposed, 1)
                pe.wait_ge(copied, t + 2)
                pe.wait_ge(done, t + 1)
                for k in range(NT):
                    last = nc.tensor.matmul(Y[:, :], factT[:, k * P:(k + 1) * P], nodes[:, k, :],
                                            start=(k == 0), stop=(k == NT - 1))
                last.then_inc(summed, 1)

        @block.vector
        def _(dve):
            LINKS = 3 + 3 * HEADS - 1
            nc.vector.memset(acc[:, N:NP], 0.0)
            nc.vector.memset(mask[:, N:NP], 0.0)
            dve.sem_inc(done, 1)
            with dve.Fori(0, NT) as t:
                links = [0]

                def link(ins):
                    links[0] += 1
                    ins.then_inc(chain, 1)
                    dve.wait_ge(chain, t * LINKS + links[0])

                dve.wait_ge(edge_in, (t + 1) * 32)
                link(nc.vector.tensor_scalar(mask[:, 0:N], adjt, 1.0, -BIG, ALU.not_equal, ALU.mult))
                dg = mask[:, bass.ts(t, P)]
                link(nc.vector.scalar_tensor_tensor(dg, ident[:, :], 1.0, dg, ALU.not_equal, ALU.mult))
                link(nc.vector.scalar_tensor_tensor(dg, ident[:, :], 1.0e-7, dg, ALU.mult, ALU.add))
                for h in range(HEADS + 1):
                    if h < HEADS:
                        dve.wait_ge(scores, t * HEADS + (h + 1))
                        nc.vector.tensor_tensor(T[h % 2], Sf[h % 2][:, 0:N], edge, ALU.mult).then_inc(masked, 1)
                        dve.wait_ge(masked, t * HEADS + (h + 1))
                        link(nc.vector.tensor_tensor(T[h % 2], T[h % 2], mask[:, 0:N], ALU.add))
                        nc.vector.tensor_reduce(nmax[:, h:h + 1], T[h % 2], AX_X, ALU.max, negate=True).then_inc(top, 1)
                    if h >= 1:
                        g = h - 1
                        dve.wait_ge(prob, t * HEADS + h)
                        link(nc.vector.reciprocal(rden[:, g:g + 1], den[:, g:g + 1]))
                        if g == 0:
                            link(nc.vector.tensor_scalar(acc[:, 0:N], T[0], rden[:, 0:1], None, ALU.mult))
                        elif g < HEADS - 1:
                            link(nc.vector.scalar_tensor_tensor(acc[:, 0:N], T[g % 2], rden[:, g:g + 1], acc[:, 0:N],
                                                                ALU.mult, ALU.add))
                        else:
                            nc.vector.scalar_tensor_tensor(acc[:, 0:N], T[g % 2], rden[:, g:g + 1], acc[:, 0:N],
                                                           ALU.mult, ALU.add).then_inc(accd, 1)
                dve.wait_ge(summed, t + 2)
                nc.vector.scalar_tensor_tensor(x1[:, t, :], Y[:, :], 1.0 / HEADS, nodes[:, t, :],
                                               ALU.mult, ALU.add).then_inc(done, 1)
                assert links[0] == LINKS


def layer_norm_scale(nc, dve, link, stat, var_ready, dev_ready, tmp):
    nc.vector.tensor_scalar(stat[:, 1, :], stat[:, 1, :], EPS, None, ALU.add).then_inc(var_ready, 1)
    dve.wait_ge(dev_ready, 1)
    link(nc.vector.reciprocal(stat[:, 3, :], stat[:, 2, :]))
    link(nc.vector.tensor_tensor(tmp, stat[:, 3, :], stat[:, 3, :], ALU.mult))
    link(nc.vector.tensor_tensor(tmp, tmp, stat[:, 1, :], ALU.mult))
    link(nc.vector.tensor_scalar(tmp, tmp, -0.5, 1.5, ALU.mult, ALU.add))
    link(nc.vector.tensor_tensor(stat[:, 3, :], stat[:, 3, :], tmp, ALU.mult))


def layer1_dense(nc, sem, v):
    work, small, esd, ident = (v[k] for k in ("work", "small", "esd", "ident"))
    dbc, wh, hT1 = v["sbc"], v["wh"], v["hT1"]
    o = 0
    def cut(w):
        nonlocal o
        o += w
        return work[:, o - w:o]
    T = [cut(NP), cut(NP)]
    mask = cut(N)
    scaled = cut(N)
    PT = cut(NP)
    adjt = cut(N)
    with ExitStack() as ctx:
        def S(name):
            return sem(ctx, "l1_" + name)
        SP_ = [ctx.enter_context(nc.psum_tensor(f"PT{k}", [P, 3, 512], F32)) for k in range(2)]
        O = ctx.enter_context(nc.psum_tensor("O", [P, D], F32))
        Sf = [s[:, :, :].rearrange("p b n -> p (b n)") for s in SP_]
        adj_in, dst_in, top, prob, transposed, copied, mixed, done, chain = (
            S(n) for n in ("adj_in", "dst_in", "top", "prob", "transposed", "copied", "mixed", "done", "chain"))
        nmax, den, rden = small[:, 0:8], small[:, 8:16], small[:, 16:24]
        block = ctx.enter_context(nc.Block())

        @block.sync
        def _(sp):
            for h in range(HEADS):
                sp.dma_start(dbc[:, h, :], v["sd_dram"][HEADS + h:HEADS + h + 1, :].to_broadcast([P, N])
                             ).then_inc(dst_in, 16)
            with sp.Fori(0, NT) as t:
                sp.wait_ge(done, t + 1)
                sp.dma_start(adjt, v["adj_dram"][bass.ts(t, P), :]).then_inc(adj_in, 16)

        @block.scalar
        def _(act):
            with act.Fori(0, NT) as t:
                for h in range(HEADS + 1):
                    if h < HEADS:
                        act.wait_ge(top, t * HEADS + (h + 1))
                        nc.scalar.activation(T[h % 2][:, 0:N], T[h % 2][:, 0:N], ACT.Exp, bias=nmax[:, h:h + 1],
                                             accum_out=den[:, h:h + 1]).then_inc(prob, 1)
                    if h >= 1:
                        act.wait_ge(transposed, t * HEADS + (h + 1))
                        act.wait_ge(mixed, t * HEADS + h)
                        nc.scalar.copy(PT, Sf[(h - 1) % 2][:, 0:NP]).then_inc(copied, 1)

        @block.tensor
        def _(pe):
            pe.sem_inc(transposed, 1)
            pe.sem_inc(mixed, 1)
            with pe.Fori(0, NT) as t:
                for h in range(HEADS):
                    pe.wait_ge(prob, t * HEADS + (h + 1))
                    for k in range(NT):
                        last = nc.tensor.transpose(Sf[h % 2][:, k * P:(k + 1) * P], T[h % 2][:, k * P:(k + 1) * P],
                                                   ident[:, :])
                    last.then_inc(transposed, 1)
                    pe.wait_ge(copied, t * HEADS + (h + 1))
                    if h == 0:
                        pe.wait_ge(done, t + 1)
                    for k in range(NT):
                        last = nc.tensor.matmul(O[:, h * DK:(h + 1) * DK], PT[:, k * P:(k + 1) * P],
                                                wh[:, k, h * DK:(h + 1) * DK], start=(k == 0), stop=(k == NT - 1))
                    last.then_inc(mixed, 1)

        @block.vector
        def _(dve):
            LINKS = 2 + 3 * HEADS + 1
            dve.wait_ge(dst_in, 16 * HEADS)
            nc.vector.memset(T[0][:, N:NP], 0.0)
            nc.vector.memset(T[1][:, N:NP], 0.0)
            dve.sem_inc(done, 1)
            with dve.Fori(0, NT) as t:
                links = [0]

                def link(ins):
                    links[0] += 1
                    ins.then_inc(chain, 1)
                    dve.wait_ge(chain, t * LINKS + links[0])

                dve.wait_ge(adj_in, (t + 1) * 16)
                link(nc.vector.tensor_scalar(mask, adjt, 0.0, 1.0e38, ALU.is_gt, ALU.mult))
                link(nc.vector.tensor_scalar(mask, mask, -NEG, None, ALU.add))
                for h in range(HEADS):
                    link(nc.vector.tensor_scalar(scaled, dbc[:, h, :], esd[:, t, h:h + 1], 0.2, ALU.add, ALU.mult))
                    if h >= 2:
                        dve.wait_ge(transposed, t * HEADS + h)
                    else:
                        dve.wait_ge(done, t + 1)
                        dve.wait_ge(transposed, t * HEADS + 1)
                    Th = T[h % 2][:, 0:N]
                    link(nc.vector.scalar_tensor_tensor(Th, dbc[:, h, :], esd[:, t, h:h + 1], scaled, ALU.add, ALU.max))
                    link(nc.vector.tensor_tensor(Th, Th, mask, ALU.min))
                    nc.vector.tensor_reduce(nmax[:, h:h + 1], Th, AX_X, ALU.max, negate=True).then_inc(top, 1)
                dve.wait_ge(mixed, t * HEADS + (HEADS + 1))
                link(nc.vector.reciprocal(rden, den))
                nc.vector.tensor_tensor(hT1[:, t, :].rearrange("p (h d) -> p h d", h=HEADS),
                                        O[:, :].rearrange("p (h d) -> p h d", h=HEADS),
                                        rden.rearrange("p (h d) -> p h d", d=1).to_broadcast([P, HEADS, DK]),
                                        ALU.mult).then_inc(done, 1)
                assert links[0] == LINKS


def layer1_sparse(nc, sem, v):
    slotT, qk, work, featT, esd, nbr, owner, ident, small, x1, stat, bias, b4bc = (v[k] for k in (
        "slotT", "qk", "work", "featT", "esd", "nbr", "owner", "ident", "small", "x1", "stat", "bias", "b4bc"))
    w1T, w2T, w3T, w4T, out = (v[k] for k in ("w1T", "w2T", "w3T", "w4T", "out"))
    G = [b.rearrange("p (c r) -> p c r", c=CT) for b in (
        qk[:, 0:CT * REC], qk[:, CT * REC:2 * CT * REC], work[:, 0:CT * REC])]
    enc = featT[:, :, :].rearrange("p f n -> p (f n)")[:, 0:NT * D].rearrange("p (t d) -> p t d", t=NT)
    nodesf = v["nodes"][:, :, :].rearrange("p t d -> p (t d)")
    room = [(nodesf, 0, NT * D), (qk, 2 * CT * REC, 2 * FT * NP), (work, NAT + 5 * D, 3 * CT * REC),
            (work, CT * REC, NAT)]
    chunks = lambda t: CLAST if t == NT - 1 else CT

    def cut(w):
        for n, (buf, start, end) in enumerate(room):
            if start + w <= end:
                room[n] = (buf, start + w, end)
                return buf[:, start:start + w]
        assert False

    slots = [cut(CT * P).rearrange("p (c i) -> p c i", c=CT) for _ in range(2)]
    rows = cut(P)
    slotsb = [cut(CT * P // 2).bitcast(BF16).rearrange("p (c i) -> p c i", c=CT) for _ in range(2)]
    srcm = cut(NT * 2 * HEADS).rearrange("p (t a) -> p t a", t=NT)
    srcmb = cut(NT * 3 * HEADS).bitcast(BF16).rearrange("p (t n a) -> p t n a", t=NT, n=3)
    wgtb = [cut(CT * HEADS * 3 // 2).bitcast(BF16).rearrange("p (n c h) -> p n c h", n=3, c=CT) for _ in range(2)]
    wrest = cut(CT * HEADS).rearrange("p (c h) -> p c h", c=CT)
    here = cut(CT * 2 * HEADS).rearrange("p (c a) -> p c a", c=CT)
    wgt = [cut(CT * HEADS).rearrange("p (c h) -> p c h", c=CT) for _ in range(2)]
    rden = [cut(HEADS) for _ in range(2)]
    neg = cut(D)
    hs = [cut(D) for _ in range(2)]
    pos = [cut(D) for _ in range(2)]
    ex = [cut(D) for _ in range(2)]
    encT = [cut(FT * 3 * P).rearrange("p (f n) -> p f n", f=FT) for _ in range(2)]
    o1 = cut(6 * P).rearrange("p (f n) -> p f n", f=2)
    o2 = cut(3 * P)
    o3 = cut(6 * P).rearrange("p (f n) -> p f n", f=2)
    half = cut(NT)
    stats = cut(NT * 6).rearrange("p (t k) -> p t k", t=NT)
    PAIRS = NT // 2
    LASTSTEP = 2 * (PAIRS - 1) + 5
    FIRSTNORM = 8
    with ExitStack() as ctx:
        def S(name):
            return sem(ctx, "g_" + name)

        Z = ctx.enter_context(nc.psum_tensor("Zg", [P, 2, 512], F32))
        SB = ctx.enter_context(nc.psum_tensor("SBg", [P, 512], F32))
        TR = ctx.enter_context(nc.psum_tensor("TRg", [P, 512], F32))
        MP = ctx.enter_context(nc.psum_tensor("MPg", [P, 2, 512], F32))
        OP = ctx.enter_context(nc.psum_tensor("OPg", [P, 2, 512], F32))
        rec_in = [S(f"rec_in{k}") for k in range(3)]
        (rows_ready, srcm_ready, here_full, here_used, slots_ready, args_ready, exp_ready, prod_ready, sum_full, h_ready,
         elu_parts, enc_ready, tr_full, tr_used, mm_full, mm_used, out_full, out_used, var_ready, inv_ready, normed,
         stored, cleared, chain) = (S(n) for n in (
            "rows_ready", "srcm_ready", "here_full", "here_used", "slots_ready", "args_ready", "exp_ready",
            "prod_ready", "sum_full", "h_ready", "elu_parts", "enc_ready", "tr_full", "tr_used", "mm_full", "mm_used",
            "out_full", "out_used", "var_ready", "inv_ready", "normed", "stored", "cleared", "chain"))
        x1_in = [S(f"x1_in{t}") for t in range(NT)]
        (esd_in, mlp_full, mlp_used, flat_ready, wparts_ready) = (S(n) for n in (
            "esd_in", "mlp_full", "mlp_used", "flat_ready", "wparts_ready"))
        norms = ((0, FIRSTNORM), (FIRSTNORM, NT))
        pair = lambda g: range(2 * g, NT if g == PAIRS - 1 else 2 * g + 2)
        block = ctx.enter_context(nc.Block())

        @block.gpsimd
        def _(pool):
            nc.gpsimd.iota(rows, pattern=[[1, P]], base=1, channel_multiplier=0,
                           allow_small_or_imprecise_dtypes=True).then_inc(rows_ready, 1)
            for t in range(NT):
                if t == 2:
                    nc.gpsimd.memset(G[2], 0.0).then_inc(cleared, 1)
                    pool.wait_ge(cleared, 1)
                if t >= 3:
                    pool.wait_ge(sum_full, t - 2)
                for c in range(chunks(t)):
                    nc.gpsimd.indirect_dma_start(
                        out=G[t % 3][:, c, :], out_offset=None, in_=v["rec_dram"],
                        in_offset=bass.IndirectOffsetOnAxis(ap=nbr[:, t, c:c + 1].bitcast(U32), axis=0),
                        bounds_check=N - 1, oob_is_err=False).then_inc(rec_in[t % 3], 16)
            nc.gpsimd.memset(half, -0.5).then_inc(cleared, 1)
            pool.wait_ge(cleared, 2)
            for n, (a, b) in enumerate(norms):
                pool.wait_ge(var_ready, n + 1)
                nc.gpsimd.tensor_tensor(stat[:, 3, a:b], stat[:, 1, a:b], half[:, 0:b - a], ALU.pow
                                        ).then_inc(inv_ready, 1)

        @block.sync
        def _(sp):
            sp.dma_start(esd[:, 0:NFULL, 0:HEADS], v["rec_dram"][0:NFULL * P, D:D + HEADS]
                         .rearrange("(t p) c -> p t c", p=P)).then_inc(esd_in, 16)
            sp.dma_start(esd[0:LAST, NFULL, 0:HEADS], v["rec_dram"][NFULL * P:N, D:D + HEADS]).then_inc(esd_in, 16)
            load_x1(v, sp, x1_in, sum_full)
            for a, b in norms:
                sp.wait_ge(normed, b)
                full = min(b, NFULL) - a
                sp.dma_start(out[a * P:(a + full) * P, :].rearrange("(t p) f -> p t f", p=P),
                             x1[:, a:a + full, :]).then_inc(stored, 16)
            sp.dma_start(out[NFULL * P:N, :], x1[0:LAST, NFULL, :]).then_inc(stored, 16)
            sp.wait_ge(stored, 16 * 3)

        @block.scalar
        def _(act):
            m = [0]

            def relu_out(dst, w, b):
                act.wait_ge(mm_full, m[0] + 1)
                nc.scalar.activation(dst, MP[:, m[0] % 2, 0:w], ACT.Relu, bias=bias[:, b:b + 1]).then_inc(mm_used, 1)
                m[0] += 1

            def flip(t):
                act.wait_ge(tr_full, t + 1)
                g = min(t // 2, PAIRS - 1)
                at = (t - 2 * g) * P
                nc.scalar.copy(encT[g % 2][:, :, at:at + P], TR[:, :].rearrange("p (f n) -> p f n", f=FT)
                               ).then_inc(tr_used, 1)

            def flatten(t):
                act.wait_ge(slots_ready, t + 1)
                nc.scalar.copy(slotsb[t % 2], slots[t % 2]).then_inc(flat_ready, 1)

            keep_blocks(nc, act, v["mlp_jobs"], (MP[:, 0, :], MP[:, 1, :]), mlp_full, mlp_used)
            flatten(0)
            for s in range(LASTSTEP + 1):
                if s < NT:
                    act.wait_ge(args_ready, s + 1)
                    nc.scalar.activation(wgt[s % 2], wgt[s % 2], ACT.Exp).then_inc(exp_ready, 1)
                g = (s - 4) // 2
                w = len(pair(g)) * P if 0 <= g < PAIRS else 0
                if s % 2 and w:
                    relu_out(o2[:, 0:w], w, 10)
                if 2 <= s < NT + 2:
                    flip(s - 2)
                if w:
                    dst, b = (o3, 11) if s % 2 else (o1, 8)
                    for k in range(2):
                        relu_out(dst[:, k, 0:w], w, b + k)
                if 1 <= s <= NT:
                    t = s - 1
                    act.wait_ge(h_ready, t + 1)
                    nc.scalar.activation(neg, hs[t % 2], ACT.Relu, scale=-1.0).then_inc(elu_parts, 1)
                    nc.scalar.activation(pos[t % 2], hs[t % 2], ACT.Relu).then_inc(elu_parts, 1)
                    act.wait_ge(elu_parts, 3 * t + 2)
                    nc.scalar.activation(ex[t % 2], neg, ACT.Exp, scale=-1.0).then_inc(elu_parts, 1)
                if s + 1 < NT:
                    flatten(s + 1)

        @block.vector
        def _(dve):
            links = [0]

            def link(ins):
                links[0] += 1
                ins.then_inc(chain, 1)
                dve.wait_ge(chain, links[0])

            TT, TS, STT = nc.vector.tensor_tensor, nc.vector.tensor_scalar, nc.vector.scalar_tensor_tensor
            byhead = lambda a: a.rearrange("p (t h) -> p t h", t=1).to_broadcast([P, NT, HEADS])

            def make_slots(t):
                if t >= 2:
                    dve.wait_ge(sum_full, t - 1)
                TT(slots[t % 2], rows.rearrange("p (c i) -> p c i", c=1).to_broadcast([P, CT, P]),
                   owner[:, t, :].rearrange("p (c i) -> p c i", i=1).to_broadcast([P, CT, P]), ALU.is_equal
                   ).then_inc(slots_ready, 1)

            def take_here(t):
                dve.wait_ge(here_full, t + 1)
                if t >= 1:
                    nc.vector.reciprocal(rden[(t - 1) % 2], SB[:, 96:104])
                if t < NT:
                    nc.vector.tensor_copy(here, SB[:, 0:96].rearrange("p (c a) -> p c a", c=CT)).then_inc(here_used, 1)
                else:
                    dve.sem_inc(here_used, 1)

            def scores(t):
                s, g = wgt[t % 2], G[t % 3]
                dve.wait_ge(here_used, t + 1)
                dve.wait_ge(rec_in[t % 3], 16 * (CT * (t // 3) + chunks(t)))
                link(TT(s, g[:, :, D + HEADS:], here[:, :, 0:HEADS], ALU.add))
                link(STT(s, s, 0.2, s, ALU.mult, ALU.max))
                link(TT(s, s, here[:, :, HEADS:], ALU.subtract))
                TS(s, s, 0.0, None, ALU.min).then_inc(args_ready, 1)

            def weigh(t):
                dve.wait_ge(exp_ready, t + 1)
                w, b = wgt[t % 2], wgtb[t % 2]
                link(nc.vector.tensor_copy(b[:, 0], w))
                link(TT(wrest, w, b[:, 0], ALU.subtract))
                link(nc.vector.tensor_copy(b[:, 1], wrest))
                TT(b[:, 2], wrest, b[:, 1], ALU.subtract).then_inc(wparts_ready, 1)
                g = G[t % 3][:, :, 0:D].rearrange("p c (h d) -> p c h d", h=HEADS)
                n = chunks(t)
                TT(g[:, 0:n], g[:, 0:n], wgt[t % 2][:, 0:n].rearrange("p c (h d) -> p c h d", d=1)
                   .to_broadcast([P, n, HEADS, DK]),
                   ALU.mult).then_inc(prod_ready, 1)

            def divide(t):
                dve.wait_ge(sum_full, t + 1)
                if t >= 2:
                    dve.wait_ge(elu_parts, 3 * (t - 1))
                TT(hs[t % 2].rearrange("p (h d) -> p h d", h=HEADS), Z[:, t % 2, :].rearrange("p (h d) -> p h d", h=HEADS),
                   rden[t % 2].rearrange("p (h d) -> p h d", d=1).to_broadcast([P, HEADS, DK]), ALU.mult
                   ).then_inc(h_ready, 1)

            def join(t):
                dve.wait_ge(elu_parts, 3 * t + 3)
                STT(enc[:, t, :], ex[t % 2], -1.0, pos[t % 2], ALU.add, ALU.add).then_inc(enc_ready, 1)

            def residual(t):
                dve.wait_ge(out_full, t + 1)
                TT(x1[:, t, :], OP[:, t % 2, :], x1[:, t, :], ALU.add).then_inc(out_used, 1)
                dve.wait_ge(out_used, t + 1)
                link(nc.vector.bn_stats(stats[:, t, :], x1[:, t, :]))
                link(nc.vector.bn_aggr(stat[:, 0:2, t], stats[:, t, :]))

            def normalise(n):
                a, b = norms[n]
                var, inv, tmp = stat[:, 1, a:b], stat[:, 3, a:b], small[:, a:b]
                TS(var, var, EPS, None, ALU.add).then_inc(var_ready, 1)
                dve.wait_ge(inv_ready, n + 1)
                link(TT(tmp, inv, inv, ALU.mult))
                link(TT(tmp, tmp, var, ALU.mult))
                link(TS(tmp, tmp, -0.5, 1.5, ALU.mult, ALU.add))
                link(TT(inv, inv, tmp, ALU.mult))
                for t in range(a, b):
                    TS(x1[:, t, :], x1[:, t, :], stat[:, 0, t:t + 1], stat[:, 3, t:t + 1], ALU.subtract, ALU.mult
                       ).then_inc(normed, 1)

            dve.wait_ge(esd_in, 32)
            nc.vector.tensor_copy(srcm[:, :, 0:HEADS], esd[:, 0:NT, 0:HEADS])
            link(TT(srcm[:, :, HEADS:], esd[:, 0:NT, 0:HEADS], byhead(small[:, 24:32]), ALU.add))
            link(STT(srcm[:, :, HEADS:], srcm[:, :, HEADS:], 0.2, srcm[:, :, HEADS:], ALU.mult, ALU.max))
            for n in range(2):
                link(nc.vector.tensor_copy(srcmb[:, :, n, :], srcm))
                link(TT(srcm, srcm, srcmb[:, :, n, :], ALU.subtract))
            nc.vector.tensor_copy(srcmb[:, :, 2, :], srcm).then_inc(srcm_ready, 1)
            dve.wait_ge(rows_ready, 1)
            make_slots(0)
            take_here(0)
            scores(0)
            for s in range(LASTSTEP + 2):
                if 2 <= s < NT + 2:
                    join(s - 2)
                if s < NT:
                    weigh(s)
                    if s + 1 < NT:
                        make_slots(s + 1)
                    take_here(s + 1)
                    if s + 1 < NT:
                        scores(s + 1)
                if 1 <= s <= NT:
                    divide(s - 1)
                if 0 <= s - 3 < NT:
                    t = s - 3
                    dve.wait_ge(x1_in[t], 16)
                    link(TT(x1[:, t, :], x1[:, t, :], b4bc[:, :], ALU.add))
                if s % 2 == 0 and 0 <= (s - 6) // 2 < PAIRS:
                    for t in pair((s - 6) // 2):
                        residual(t)
                if s == FIRSTNORM + 4:
                    normalise(0)
            normalise(1)

        @block.tensor
        def _(pe):
            m = [0]

            def dense(terms, w):
                if m[0] >= 2:
                    pe.wait_ge(mm_used, m[0] - 1)
                for n, (l, r) in enumerate(terms):
                    last = nc.tensor.matmul(MP[:, m[0] % 2, 0:w], l, r, start=(n == 0), stop=(n == len(terms) - 1))
                last.then_inc(mm_full, 1)
                m[0] += 1

            def to_slots(t):
                if t >= 1:
                    pe.wait_ge(wparts_ready, t)
                    pe.wait_ge(flat_ready, t)
                    pe.wait_ge(here_used, t)
                    for c in range(chunks(t - 1)):
                        for n in range(3):
                            last = nc.tensor.matmul(SB[:, 96:104], slotsb[(t - 1) % 2][:, c, :],
                                                    wgtb[(t - 1) % 2][:, n, c, :], start=(c == 0 and n == 0),
                                                    stop=(c == chunks(t - 1) - 1 and n == 2))
                for c in range(CT):
                    for n in range(3 if t < NT else 0):
                        last = nc.tensor.matmul(SB[:, c * 16:(c + 1) * 16], slotT[:, t, c * P:(c + 1) * P],
                                                srcmb[:, t, n, :], start=(n == 0), stop=(n == 2))
                last.then_inc(here_full, 1)

            def flip(t):
                pe.wait_ge(enc_ready, t + 1)
                if t >= 1:
                    pe.wait_ge(tr_used, t)
                for f in range(FT):
                    last = nc.tensor.transpose(TR[:, f * P:(f + 1) * P], enc[:, t, f * P:(f + 1) * P], ident[:, :])
                last.then_inc(tr_full, 1)

            def gather_up(t):
                pe.wait_ge(prod_ready, t + 1)
                if t >= 2:
                    pe.wait_ge(h_ready, t - 1)
                for c in range(chunks(t)):
                    last = nc.tensor.matmul(Z[:, t % 2, :], slots[t % 2][:, c, :], G[t % 3][:, c, 0:D],
                                            start=(c == 0), stop=(c == chunks(t) - 1))
                last.then_inc(sum_full, 1)

            flip_blocks(nc, pe, v["mlp_jobs"], (MP[:, 0, :], MP[:, 1, :]), ident, mlp_full, mlp_used)
            pe.wait_ge(srcm_ready, 1)
            to_slots(0)
            pe.wait_ge(mlp_used, len(v["mlp_jobs"]))
            for s in range(LASTSTEP + 1):
                if s < NT:
                    to_slots(s + 1)
                g = (s - 4) // 2
                w = len(pair(g)) * P if 0 <= g < PAIRS else 0
                if s % 2 and w:
                    pe.wait_ge(mm_used, 5 * g + 2)
                    dense([(w2T[:, f, :], o1[:, f, 0:w]) for f in range(2)], w)
                if 2 <= s < NT + 2:
                    flip(s - 2)
                if s % 2 and w:
                    pe.wait_ge(mm_used, 5 * g + 3)
                    for k in range(2):
                        dense([(w3T[:, k * P:(k + 1) * P], o2[:, 0:w])], w)
                if s % 2 == 0 and w:
                    pe.wait_ge(tr_used, pair(g)[-1] + 1)
                    e = encT[g % 2]
                    for k in range(2):
                        dense([(w1T[:, f, k * P:(k + 1) * P], e[:, f, 0:w]) for f in range(FT)], w)
                if s < NT:
                    gather_up(s)
                if s % 2 and w:
                    pe.wait_ge(mm_used, 5 * g + 5)
                    for j, t in enumerate(pair(g)):
                        if t >= 2:
                            pe.wait_ge(out_used, t - 1)
                        for f in range(2):
                            last = nc.tensor.matmul(OP[:, t % 2, :], o3[:, f, j * P:(j + 1) * P], w4T[:, f, :],
                                                    start=(f == 0), stop=(f == 1))
                        last.then_inc(out_full, 1)


def tail(nc, sem, v):
    x1, hT1, stat, ident, work, small, bias, b4bc = (v[k] for k in (
        "x1", "hT1", "stat", "ident", "work", "small", "bias", "b4bc"))
    w1T, w2T, w3T, w4T, out = (v[k] for k in ("w1T", "w2T", "w3T", "w4T", "out"))
    nodes = v["nodes"]
    qkf = v["qk"][:, :]
    encT = [qkf[:, k * 2048:(k + 1) * 2048].rearrange("p (f n) -> p f n", f=FT) for k in range(2)]
    o1 = [work[:, k * 1024:(k + 1) * 1024].rearrange("p (f n) -> p f n", f=2) for k in range(2)]
    o2 = [work[:, 2048 + k * 512:2560 + k * 512] for k in range(2)]
    o3 = [work[:, 3072 + k * 1024:4096 + k * 1024].rearrange("p (f n) -> p f n", f=2) for k in range(2)]
    ex = [work[:, 5120 + k * 512:5632 + k * 512] for k in range(2)]
    with ExitStack() as ctx:
        def S(name):
            return sem(ctx, "t_" + name)
        TP = ctx.enter_context(nc.psum_tensor("TPt", [P, 2, 512], F32))
        MP = ctx.enter_context(nc.psum_tensor("MP", [P, 2, 512], F32))
        OP = ctx.enter_context(nc.psum_tensor("OP", [P, 2, 512], F32))
        stats = ctx.enter_context(nc.sbuf_tensor("stats1", [P, NT, 6], F32))
        (neg_ready, exp_ready, elu_done, tp_full, tp_used, mm_full, mm_used, out_full, out_used, var_ready, dev_ready,
         normed, stored, chain) = (S(n) for n in (
            "neg_ready", "exp_ready", "elu_done", "tp_full", "tp_used", "mm_full", "mm_used", "out_full", "out_used",
            "var_ready", "dev_ready", "normed", "stored", "chain"))
        NG = len(TG)
        block = ctx.enter_context(nc.Block())

        @block.sync
        def _(sp):
            for g, (t0, k) in enumerate(TG):
                sp.wait_ge(normed, t0 + k)
                full = min(k, NFULL - t0)
                sp.dma_start(out[t0 * P:(t0 + full) * P, :].rearrange("(t p) f -> p t f", p=P),
                             x1[:, t0:t0 + full, :]).then_inc(stored, 16)
            sp.dma_start(out[NFULL * P:N, :], x1[0:LAST, NFULL, :]).then_inc(stored, 16)
            sp.wait_ge(stored, 16 * (NG + 1))

        @block.scalar
        def _(act):
            for t in range(NT):
                act.wait_ge(neg_ready, t + 1)
                nc.scalar.activation(ex[t % 2], ex[t % 2], ACT.Exp).then_inc(exp_ready, 1)
            m = 0
            for g, (t0, k) in enumerate(TG):
                w = k * P
                for f in range(FT):
                    act.wait_ge(tp_full, g * FT + f + 1)
                    nc.scalar.copy(encT[g % 2][:, f, 0:w], TP[:, f % 2, 0:w]).then_inc(tp_used, 1)
                for dst, b in ((o1[g % 2][:, 0, 0:w], 8), (o1[g % 2][:, 1, 0:w], 9), (o2[g % 2][:, 0:w], 10),
                               (o3[g % 2][:, 0, 0:w], 11), (o3[g % 2][:, 1, 0:w], 12)):
                    act.wait_ge(mm_full, m + 1)
                    nc.scalar.activation(dst, MP[:, m % 2, 0:w], ACT.Relu, bias=bias[:, b:b + 1]).then_inc(mm_used, 1)
                    m += 1
            act.wait_ge(var_ready, 1)
            nc.scalar.activation(stat[:, 2, :], stat[:, 1, :], ACT.Sqrt).then_inc(dev_ready, 1)

        @block.tensor
        def _(pe):
            m = 0
            for g, (t0, k) in enumerate(TG):
                w = k * P
                pe.wait_ge(elu_done, t0 + k)
                for f in range(FT):
                    if g * FT + f >= 2:
                        pe.wait_ge(tp_used, g * FT + f - 1)
                    for j in range(k):
                        last = nc.tensor.transpose(TP[:, f % 2, j * P:(j + 1) * P], hT1[:, t0 + j, f * P:(f + 1) * P],
                                                   ident[:, :])
                    last.then_inc(tp_full, 1)
                pe.wait_ge(tp_used, (g + 1) * FT)
                e, a, b, c = encT[g % 2], o1[g % 2], o2[g % 2], o3[g % 2]
                layers = ([[(w1T[:, f, o * P:(o + 1) * P], e[:, f, 0:w]) for f in range(FT)] for o in range(2)],
                          [[(w2T[:, f, :], a[:, f, 0:w]) for f in range(2)]],
                          [[(w3T[:, o * P:(o + 1) * P], b[:, 0:w])] for o in range(2)])
                for layer in layers:
                    pe.wait_ge(mm_used, m)
                    for terms in layer:
                        for n, (l, r) in enumerate(terms):
                            last = nc.tensor.matmul(MP[:, m % 2, 0:w], l, r, start=(n == 0), stop=(n == len(terms) - 1))
                        last.then_inc(mm_full, 1)
                        m += 1
                pe.wait_ge(mm_used, m)
                for j in range(k):
                    t = t0 + j
                    if t >= 2:
                        pe.wait_ge(out_used, t - 1)
                    for f in range(2):
                        last = nc.tensor.matmul(OP[:, t % 2, :], c[:, f, j * P:(j + 1) * P], w4T[:, f, :],
                                                start=(f == 0), stop=(f == 1))
                    last.then_inc(out_full, 1)

        @block.vector
        def _(dve):
            links = [0]

            def link(ins):
                links[0] += 1
                ins.then_inc(chain, 1)
                dve.wait_ge(chain, links[0])

            for t in range(NT):
                link(nc.vector.tensor_tensor(x1[:, t, :], x1[:, t, :], b4bc[:, :], ALU.add))
            for t in range(NT + 1):
                if t < NT:
                    nc.vector.tensor_scalar(ex[t % 2], hT1[:, t, :], 0.0, None, ALU.min).then_inc(neg_ready, 1)
                if t >= 1:
                    z = hT1[:, t - 1, :]
                    dve.wait_ge(exp_ready, t)
                    link(nc.vector.tensor_scalar(ex[(t - 1) % 2], ex[(t - 1) % 2], -1.0, None, ALU.add))
                    nc.vector.scalar_tensor_tensor(z, z, 0.0, ex[(t - 1) % 2], ALU.max, ALU.add).then_inc(elu_done, 1)
                    dve.wait_ge(elu_done, t)
            for t in range(NT):
                dve.wait_ge(out_full, t + 1)
                nc.vector.tensor_tensor(x1[:, t, :], OP[:, t % 2, :], x1[:, t, :], ALU.add).then_inc(out_used, 1)
                dve.wait_ge(out_used, t + 1)
                link(nc.vector.bn_stats(stats[:, t, :], x1[:, t, :]))
                link(nc.vector.bn_aggr(stat[:, 0:2, t], stats[:, t, :]))
            layer_norm_scale(nc, dve, link, stat, var_ready, dev_ready, small[:, 0:NT])
            for t in range(NT):
                nc.vector.tensor_scalar(x1[:, t, :], x1[:, t, :], stat[:, 0, t:t + 1], stat[:, 3, t:t + 1],
                                        ALU.subtract, ALU.mult).then_inc(normed, 1)


_INS = ['x', 'adj', 'L0_gnn_rel_pair_index', 'L0_gnn_Wq', 'L0_gnn_bq', 'L0_gnn_Wk', 'L0_gnn_bk', 'L1_gnn_W',
        'L1_gnn_a1', 'L1_gnn_a2', 'L1_gnn_W1', 'L1_gnn_b1', 'L1_gnn_W2', 'L1_gnn_b2', 'L1_gnn_W3', 'L1_gnn_b3',
        'L1_gnn_W4', 'L1_gnn_b4']


def kernel(**inputs):
    import numpy as np
    import concourse.bacc as bacc
    from concourse.bass_utils import run_bass_kernel_spmd

    nc = bacc.Bacc("TRN2", target_bir_lowering=False, num_devices=1)
    arrays, args = {}, []
    for name in _INS:
        a = np.ascontiguousarray(inputs[name])
        arrays[f"in_{name}"] = a
        args.append(nc.dram_tensor(f"in_{name}", a.shape, mybir.dt.from_np(a.dtype), kind="ExternalInput").ap())
    args.append(nc.dram_tensor("out_0", (N, D), F32, kind="ExternalOutput").ap())
    args.append(nc.dram_tensor("edge_matrix", (NP, N), F32, kind="Internal").ap())
    args.append(nc.dram_tensor("adj_padded", (NP, N), F32, kind="Internal").ap())
    args.append(nc.dram_tensor("scores_src_dst", (2 * HEADS, N), F32, kind="Internal").ap())
    args.append(nc.dram_tensor("node_records", (N, REC), F32, kind="Internal").ap())
    args.append(nc.dram_tensor("x1_rows", (N, D), F32, kind="Internal").ap())
    args.append(nc.dram_tensor("adj_x_rows", (N, D), F32, kind="Internal").ap())
    program(nc, *args)
    r = run_bass_kernel_spmd(nc, [arrays], core_ids=[0])
    return r.results[0]["out_0"]
```
